# Optimizing a Trainium2 kernel written in Bass

```python
import numpy as np
import jax
import jax.numpy as jnp

def _softmax(x, axis=-1):
    return jax.nn.softmax(x, axis=axis)

def _gelu(x):
    return jax.nn.gelu(x, approximate=True)

def _silu(x):
    return jax.nn.silu(x)

def _sigmoid(x):
    return jax.nn.sigmoid(x)

def _layernorm(x, axis=-1, eps=1e-05):
    m = jnp.mean(x, axis=axis, keepdims=True)
    v = jnp.var(x, axis=axis, keepdims=True)
    return (x - m) / jnp.sqrt(v + eps)

def _scatter_add(tgt, idx, src, axis=0):
    return tgt.at[idx].add(src)

def _segment_sum(src, seg, n):
    return jax.ops.segment_sum(src, seg, n)
kernel_name = 'mk_xattn_seq_d4_seqx_r4_3291c4'

def setup_inputs(seed: int=0):
    np.random.seed(seed)
    _w = jnp.asarray

    def _rec_inputs():
        import jax
        import jax.numpy as jnp
        _rk = jax.random.key(seed)
        x = -0.0002928 + 1 * jax.random.normal(jax.random.fold_in(_rk, 1), (16, 128, 256), jnp.float32)
        _lenS = 128 - jax.random.randint(jax.random.fold_in(_rk, 7), (16,), 0, max(1, 128 // 4) + 1, jnp.int32)
        _lenS2 = 128 - jax.random.randint(jax.random.fold_in(_rk, 8), (16,), 0, max(1, 128 // 4) + 1, jnp.int32)
        _ctx_768P = jax.random.normal(jax.random.fold_in(_rk, 11), (16, 16, 192), jnp.float32)
        _ctx_768c = jax.random.dirichlet(jax.random.fold_in(_rk, 511), 0.3 * jnp.ones((16,), jnp.float32), (16, 128))
        _ctx_768t = jnp.einsum('bsk,bkd->bsd', _ctx_768c, _ctx_768P)
        _ctx_768t = _ctx_768t * jax.lax.rsqrt(jnp.mean(jnp.square(_ctx_768t)) + 1e-12) * 0.953939
        ctx_768 = -0.00423632 + 0.9977 * (_ctx_768t + 0.3 * jax.random.normal(jax.random.fold_in(_rk, 611), (16, 128, 192), jnp.float32))
        _validS = jnp.arange(128)[None, :] < _lenS[:, None]
        _validS2 = jnp.arange(128)[None, :] < _lenS2[:, None]
        _causal = jnp.tril(jnp.ones((128, 128), dtype=bool))
        mask_BxS2_if1 = jnp.where(jnp.ones((16, 128), dtype=bool), 1, 0).astype(jnp.int32)
        return (x, ctx_768, mask_BxS2_if1)
    x, ctx_768, mask_BxS2_if1 = _rec_inputs()

    def _L0_xattn_setup():
        import jax, jax.numpy as jnp
        import numpy as np
        EPS = 1e-05
        HEADS = 16
        D_HEAD = 64
        SCALE = D_HEAD ** (-0.5)

        def layernorm(x, g, b):
            m = jnp.mean(x, axis=-1, keepdims=True)
            v = jnp.var(x, axis=-1, keepdims=True)
            return (x - m) * jax.lax.rsqrt(v + EPS) * g + b

        def attention(x, ctx, Wq, Wk, Wv, Wo, bo):
            b, n, _ = x.shape
            m = ctx.shape[1]
            q = (x @ Wq).reshape(b, n, HEADS, D_HEAD)
            k = (ctx @ Wk).reshape(b, m, HEADS, D_HEAD)
            v = (ctx @ Wv).reshape(b, m, HEADS, D_HEAD)
            sim = jnp.einsum('bihd,bjhd->bhij', q, k) * SCALE
            attn = jax.nn.softmax(sim, axis=-1)
            out = jnp.einsum('bhij,bjhd->bihd', attn, v).reshape(b, n, HEADS * D_HEAD)
            return out @ Wo + bo
        key = jax.random.key(seed)
        ks = jax.random.split(key, 16)
        dim, ctx_dim, inner = (256, 192, HEADS * D_HEAD)
        ff_inner = 4 * dim
        s = lambda k, *sh: jax.random.normal(k, sh, jnp.float32) * 0.02
        return {'x': jax.random.normal(ks[0], (2, 512, dim), jnp.float32), 'context': jax.random.normal(ks[1], (2, 77, ctx_dim), jnp.float32), 'ln1_g': jnp.ones((dim,), jnp.float32), 'ln1_b': jnp.zeros((dim,), jnp.float32), 'a1_Wq': s(ks[2], dim, inner), 'a1_Wk': s(ks[3], dim, inner), 'a1_Wv': s(ks[4], dim, inner), 'a1_Wo': s(ks[5], inner, dim), 'a1_bo': jnp.zeros((dim,), jnp.float32), 'ln2_g': jnp.ones((dim,), jnp.float32), 'ln2_b': jnp.zeros((dim,), jnp.float32), 'a2_Wq': s(ks[6], dim, inner), 'a2_Wk': s(ks[7], ctx_dim, inner), 'a2_Wv': s(ks[8], ctx_dim, inner), 'a2_Wo': s(ks[9], inner, dim), 'a2_bo': jnp.zeros((dim,), jnp.float32), 'ln3_g': jnp.ones((dim,), jnp.float32), 'ln3_b': jnp.zeros((dim,), jnp.float32), 'ff_Wp': s(ks[10], dim, 2 * ff_inner), 'ff_bp': jnp.zeros((2 * ff_inner,), jnp.float32), 'ff_Wo': s(ks[11], ff_inner, dim), 'ff_bo': jnp.zeros((dim,), jnp.float32)}
    _L0_xattn_all = _L0_xattn_setup()
    _L0_xattn_in = {k: v for k, v in _L0_xattn_all.items() if k in ('ln1_g', 'ln1_b', 'a1_Wq', 'a1_Wk', 'a1_Wv', 'a1_Wo', 'a1_bo', 'ln2_g', 'ln2_b', 'a2_Wq', 'a2_Wk', 'a2_Wv', 'a2_Wo', 'a2_bo', 'ln3_g', 'ln3_b', 'ff_Wp', 'ff_bp', 'ff_Wo', 'ff_bo')}
    del _L0_xattn_all

    def _L1_xattn_setup():
        import jax, jax.numpy as jnp
        import numpy as np
        import math
        H = 8
        D = 256
        D_I = 256
        D_L = 192
        EPS = 1e-05
        key = jax.random.key(seed)
        ks = jax.random.split(key, 8)
        B, NQ, NK = (8, 196, 128)
        img_embed = jax.random.normal(ks[0], (B, NQ, D_I), dtype=jnp.float32)
        sent_embed = jax.random.normal(ks[1], (B, NK, D_L), dtype=jnp.float32)
        atten_mask = jnp.ones((B, NK), dtype=jnp.int32)
        Wq = jax.random.normal(ks[2], (D_I, H * D), dtype=jnp.float32) * (1.0 / math.sqrt(D_I))
        Wk = jax.random.normal(ks[3], (D_L, H * D), dtype=jnp.float32) * (1.0 / math.sqrt(D_L))
        Wv = jax.random.normal(ks[4], (D_L, H * D), dtype=jnp.float32) * (1.0 / math.sqrt(D_L))
        Wo = jax.random.normal(ks[5], (H * D, D_I), dtype=jnp.float32) * (1.0 / math.sqrt(H * D))
        gamma = jnp.ones((D_I,), dtype=jnp.float32)
        beta = jnp.zeros((D_I,), dtype=jnp.float32)
        return {'img_embed': img_embed, 'sent_embed': sent_embed, 'atten_mask': atten_mask, 'Wq': Wq, 'Wk': Wk, 'Wv': Wv, 'Wo': Wo, 'gamma': gamma, 'beta': beta}
    _L1_xattn_all = _L1_xattn_setup()
    _L1_xattn_in = {k: v for k, v in _L1_xattn_all.items() if k in ('Wq', 'Wk', 'Wv', 'Wo', 'gamma', 'beta')}
    del _L1_xattn_all

    def _L2_xattn_setup():
        import jax, jax.numpy as jnp
        import numpy as np
        D_Q, D_CTX, N_HEADS, HEAD_DIM = (256, 192, 16, 64)
        INNER = N_HEADS * HEAD_DIM
        EPS = 1e-05

        def _layernorm(x, gamma, beta):
            mu = jnp.mean(x, axis=-1, keepdims=True)
            var = jnp.var(x, axis=-1, keepdims=True)
            return (x - mu) * jax.lax.rsqrt(var + EPS) * gamma + beta
        key = jax.random.key(seed)
        ks = jax.random.split(key, 8)
        B, NQ, NC = (4, 256, 256)
        s_q = 1.0 / np.sqrt(D_Q)
        s_c = 1.0 / np.sqrt(D_CTX)
        s_i = 1.0 / np.sqrt(INNER)
        return {'x': jax.random.normal(ks[0], (B, NQ, D_Q), jnp.float32), 'context': jax.random.normal(ks[1], (B, NC, D_CTX), jnp.float32), 'Wq': jax.random.normal(ks[2], (D_Q, INNER), jnp.float32) * s_q, 'Wk': jax.random.normal(ks[3], (D_CTX, INNER), jnp.float32) * s_c, 'Wv': jax.random.normal(ks[4], (D_CTX, INNER), jnp.float32) * s_c, 'Wo': jax.random.normal(ks[5], (INNER, D_Q), jnp.float32) * s_i, 'bo': jnp.zeros((D_Q,), jnp.float32), 'gamma': jnp.ones((D_Q,), jnp.float32), 'beta': jnp.zeros((D_Q,), jnp.float32)}
    _L2_xattn_all = _L2_xattn_setup()
    _L2_xattn_in = {k: v for k, v in _L2_xattn_all.items() if k in ('Wq', 'Wk', 'Wv', 'Wo', 'bo', 'gamma', 'beta')}
    del _L2_xattn_all

    def _L3_xattn_setup():
        import jax, jax.numpy as jnp
        import numpy as np
        DIM, HEADS, DHEAD, CTX_DIM = (256, 16, 64, 192)
        INNER = HEADS * DHEAD
        FF_HID = 4 * DIM
        EPS = 1e-05

        def _ln(x, g, b):
            mu = jnp.mean(x, axis=-1, keepdims=True)
            var = jnp.mean(jnp.square(x - mu), axis=-1, keepdims=True)
            return (x - mu) * jax.lax.rsqrt(var + EPS) * g + b

        def _attn(x, ctx, Wq, Wk, Wv, Wo, bo):
            b, n, _ = x.shape
            m = ctx.shape[1]
            q = (x @ Wq).reshape(b, n, HEADS, DHEAD)
            k = (ctx @ Wk).reshape(b, m, HEADS, DHEAD)
            v = (ctx @ Wv).reshape(b, m, HEADS, DHEAD)
            scale = DHEAD ** (-0.5)
            sim = jnp.einsum('bihd,bjhd->bhij', q, k) * scale
            attn = jax.nn.softmax(sim, axis=-1)
            out = jnp.einsum('bhij,bjhd->bihd', attn, v).reshape(b, n, INNER)
            return out @ Wo + bo
        key = jax.random.key(seed)
        ks = jax.random.split(key, 24)

        def w(k, shape, fan_in):
            return jax.random.normal(k, shape, jnp.float32) * fan_in ** (-0.5)
        inp = {'x': jax.random.normal(ks[0], (2, 512, DIM), jnp.float32), 'context': jax.random.normal(ks[1], (2, 77, CTX_DIM), jnp.float32), 'Wq1': w(ks[2], (DIM, INNER), DIM), 'Wk1': w(ks[3], (DIM, INNER), DIM), 'Wv1': w(ks[4], (DIM, INNER), DIM), 'Wo1': w(ks[5], (INNER, DIM), INNER), 'bo1': jnp.zeros((DIM,), jnp.float32), 'Wq2': w(ks[6], (DIM, INNER), DIM), 'Wk2': w(ks[7], (CTX_DIM, INNER), CTX_DIM), 'Wv2': w(ks[8], (CTX_DIM, INNER), CTX_DIM), 'Wo2': w(ks[9], (INNER, DIM), INNER), 'bo2': jnp.zeros((DIM,), jnp.float32), 'Wp': w(ks[10], (DIM, 2 * FF_HID), DIM), 'bp': jnp.zeros((2 * FF_HID,), jnp.float32), 'W2': w(ks[11], (FF_HID, DIM), FF_HID), 'b2': jnp.zeros((DIM,), jnp.float32), 'g1': jnp.ones((DIM,), jnp.float32), 'be1': jnp.zeros((DIM,), jnp.float32), 'g2': jnp.ones((DIM,), jnp.float32), 'be2': jnp.zeros((DIM,), jnp.float32), 'g3': jnp.ones((DIM,), jnp.float32), 'be3': jnp.zeros((DIM,), jnp.float32)}
        return inp
    _L3_xattn_all = _L3_xattn_setup()
    _L3_xattn_in = {k: v for k, v in _L3_xattn_all.items() if k in ('Wq1', 'Wk1', 'Wv1', 'Wo1', 'bo1', 'Wq2', 'Wk2', 'Wv2', 'Wo2', 'bo2', 'Wp', 'bp', 'W2', 'b2', 'g1', 'be1', 'g2', 'be2', 'g3', 'be3')}
    del _L3_xattn_all
    return {'x': x, 'ctx_768': ctx_768, 'mask_BxS2_if1': mask_BxS2_if1, 'L0_xattn_ln1_g': _L0_xattn_in['ln1_g'], 'L0_xattn_ln1_b': _L0_xattn_in['ln1_b'], 'L0_xattn_a1_Wq': _L0_xattn_in['a1_Wq'], 'L0_xattn_a1_Wk': _L0_xattn_in['a1_Wk'], 'L0_xattn_a1_Wv': _L0_xattn_in['a1_Wv'], 'L0_xattn_a1_Wo': _L0_xattn_in['a1_Wo'], 'L0_xattn_a1_bo': _L0_xattn_in['a1_bo'], 'L0_xattn_ln2_g': _L0_xattn_in['ln2_g'], 'L0_xattn_ln2_b': _L0_xattn_in['ln2_b'], 'L0_xattn_a2_Wq': _L0_xattn_in['a2_Wq'], 'L0_xattn_a2_Wk': _L0_xattn_in['a2_Wk'], 'L0_xattn_a2_Wv': _L0_xattn_in['a2_Wv'], 'L0_xattn_a2_Wo': _L0_xattn_in['a2_Wo'], 'L0_xattn_a2_bo': _L0_xattn_in['a2_bo'], 'L0_xattn_ln3_g': _L0_xattn_in['ln3_g'], 'L0_xattn_ln3_b': _L0_xattn_in['ln3_b'], 'L0_xattn_ff_Wp': _L0_xattn_in['ff_Wp'], 'L0_xattn_ff_bp': _L0_xattn_in['ff_bp'], 'L0_xattn_ff_Wo': _L0_xattn_in['ff_Wo'], 'L0_xattn_ff_bo': _L0_xattn_in['ff_bo'], 'L1_xattn_Wq': _L1_xattn_in['Wq'], 'L1_xattn_Wk': _L1_xattn_in['Wk'], 'L1_xattn_Wv': _L1_xattn_in['Wv'], 'L1_xattn_Wo': _L1_xattn_in['Wo'], 'L1_xattn_gamma': _L1_xattn_in['gamma'], 'L1_xattn_beta': _L1_xattn_in['beta'], 'L2_xattn_Wq': _L2_xattn_in['Wq'], 'L2_xattn_Wk': _L2_xattn_in['Wk'], 'L2_xattn_Wv': _L2_xattn_in['Wv'], 'L2_xattn_Wo': _L2_xattn_in['Wo'], 'L2_xattn_bo': _L2_xattn_in['bo'], 'L2_xattn_gamma': _L2_xattn_in['gamma'], 'L2_xattn_beta': _L2_xattn_in['beta'], 'L3_xattn_Wq1': _L3_xattn_in['Wq1'], 'L3_xattn_Wk1': _L3_xattn_in['Wk1'], 'L3_xattn_Wv1': _L3_xattn_in['Wv1'], 'L3_xattn_Wo1': _L3_xattn_in['Wo1'], 'L3_xattn_bo1': _L3_xattn_in['bo1'], 'L3_xattn_Wq2': _L3_xattn_in['Wq2'], 'L3_xattn_Wk2': _L3_xattn_in['Wk2'], 'L3_xattn_Wv2': _L3_xattn_in['Wv2'], 'L3_xattn_Wo2': _L3_xattn_in['Wo2'], 'L3_xattn_bo2': _L3_xattn_in['bo2'], 'L3_xattn_Wp': _L3_xattn_in['Wp'], 'L3_xattn_bp': _L3_xattn_in['bp'], 'L3_xattn_W2': _L3_xattn_in['W2'], 'L3_xattn_b2': _L3_xattn_in['b2'], 'L3_xattn_g1': _L3_xattn_in['g1'], 'L3_xattn_be1': _L3_xattn_in['be1'], 'L3_xattn_g2': _L3_xattn_in['g2'], 'L3_xattn_be2': _L3_xattn_in['be2'], 'L3_xattn_g3': _L3_xattn_in['g3'], 'L3_xattn_be3': _L3_xattn_in['be3']}

def reference(x, ctx_768, mask_BxS2_if1, L0_xattn_ln1_g, L0_xattn_ln1_b, L0_xattn_a1_Wq, L0_xattn_a1_Wk, L0_xattn_a1_Wv, L0_xattn_a1_Wo, L0_xattn_a1_bo, L0_xattn_ln2_g, L0_xattn_ln2_b, L0_xattn_a2_Wq, L0_xattn_a2_Wk, L0_xattn_a2_Wv, L0_xattn_a2_Wo, L0_xattn_a2_bo, L0_xattn_ln3_g, L0_xattn_ln3_b, L0_xattn_ff_Wp, L0_xattn_ff_bp, L0_xattn_ff_Wo, L0_xattn_ff_bo, L1_xattn_Wq, L1_xattn_Wk, L1_xattn_Wv, L1_xattn_Wo, L1_xattn_gamma, L1_xattn_beta, L2_xattn_Wq, L2_xattn_Wk, L2_xattn_Wv, L2_xattn_Wo, L2_xattn_bo, L2_xattn_gamma, L2_xattn_beta, L3_xattn_Wq1, L3_xattn_Wk1, L3_xattn_Wv1, L3_xattn_Wo1, L3_xattn_bo1, L3_xattn_Wq2, L3_xattn_Wk2, L3_xattn_Wv2, L3_xattn_Wo2, L3_xattn_bo2, L3_xattn_Wp, L3_xattn_bp, L3_xattn_W2, L3_xattn_b2, L3_xattn_g1, L3_xattn_be1, L3_xattn_g2, L3_xattn_be2, L3_xattn_g3, L3_xattn_be3):
    import jax
    import jax.numpy as jnp

    def _L0_xattn_ref(x, context, ln1_g, ln1_b, a1_Wq, a1_Wk, a1_Wv, a1_Wo, a1_bo, ln2_g, ln2_b, a2_Wq, a2_Wk, a2_Wv, a2_Wo, a2_bo, ln3_g, ln3_b, ff_Wp, ff_bp, ff_Wo, ff_bo):
        import jax, jax.numpy as jnp
        import numpy as np
        EPS = 1e-05
        HEADS = 16
        D_HEAD = 64
        SCALE = D_HEAD ** (-0.5)

        def layernorm(x, g, b):
            m = jnp.mean(x, axis=-1, keepdims=True)
            v = jnp.var(x, axis=-1, keepdims=True)
            return (x - m) * jax.lax.rsqrt(v + EPS) * g + b

        def attention(x, ctx, Wq, Wk, Wv, Wo, bo):
            b, n, _ = x.shape
            m = ctx.shape[1]
            q = (x @ Wq).reshape(b, n, HEADS, D_HEAD)
            k = (ctx @ Wk).reshape(b, m, HEADS, D_HEAD)
            v = (ctx @ Wv).reshape(b, m, HEADS, D_HEAD)
            sim = jnp.einsum('bihd,bjhd->bhij', q, k) * SCALE
            attn = jax.nn.softmax(sim, axis=-1)
            out = jnp.einsum('bhij,bjhd->bihd', attn, v).reshape(b, n, HEADS * D_HEAD)
            return out @ Wo + bo
        h = layernorm(x, ln1_g, ln1_b)
        x = attention(h, h, a1_Wq, a1_Wk, a1_Wv, a1_Wo, a1_bo) + x
        h = layernorm(x, ln2_g, ln2_b)
        x = attention(h, context, a2_Wq, a2_Wk, a2_Wv, a2_Wo, a2_bo) + x
        h = layernorm(x, ln3_g, ln3_b)
        p = h @ ff_Wp + ff_bp
        u, gate = jnp.split(p, 2, axis=-1)
        ff = u * jax.nn.gelu(gate, approximate=False) @ ff_Wo + ff_bo
        return ff + x

    def _L1_xattn_ref(img_embed, sent_embed, atten_mask, Wq, Wk, Wv, Wo, gamma, beta):
        import jax, jax.numpy as jnp
        import numpy as np
        import math
        H = 8
        D = 256
        D_I = 256
        D_L = 192
        EPS = 1e-05
        B = img_embed.shape[0]
        Q = (img_embed @ Wq).reshape(B, -1, H, D).transpose(0, 2, 1, 3)
        K = (sent_embed @ Wk).reshape(B, -1, H, D).transpose(0, 2, 1, 3)
        V = (sent_embed @ Wv).reshape(B, -1, H, D).transpose(0, 2, 1, 3)
        score = jnp.einsum('bhqd,bhkd->bhqk', Q, K) / math.sqrt(D)
        mask = (atten_mask != 0)[:, None, None, :]
        score = jnp.where(mask, score, -jnp.inf)
        attn = jax.nn.softmax(score, axis=-1)
        ctx = jnp.einsum('bhqk,bhkd->bqhd', attn, V).reshape(B, -1, H * D)
        out = ctx @ Wo + img_embed
        mu = jnp.mean(out, axis=-1, keepdims=True)
        var = jnp.var(out, axis=-1, keepdims=True)
        return (out - mu) * jax.lax.rsqrt(var + EPS) * gamma + beta

    def _L2_xattn_ref(x, context, Wq, Wk, Wv, Wo, bo, gamma, beta):
        import jax, jax.numpy as jnp
        import numpy as np
        D_Q, D_CTX, N_HEADS, HEAD_DIM = (256, 192, 16, 64)
        INNER = N_HEADS * HEAD_DIM
        EPS = 1e-05

        def _layernorm(x, gamma, beta):
            mu = jnp.mean(x, axis=-1, keepdims=True)
            var = jnp.var(x, axis=-1, keepdims=True)
            return (x - mu) * jax.lax.rsqrt(var + EPS) * gamma + beta
        scale = HEAD_DIM ** (-0.5)
        h = _layernorm(x, gamma, beta)
        B, NQ, _ = x.shape
        NC = context.shape[1]
        Q = (h @ Wq).reshape(B, NQ, N_HEADS, HEAD_DIM)
        K = (context @ Wk).reshape(B, NC, N_HEADS, HEAD_DIM)
        V = (context @ Wv).reshape(B, NC, N_HEADS, HEAD_DIM)
        attn = jnp.einsum('bihd,bjhd->bhij', Q, K)
        attn = jax.nn.softmax(attn, axis=-1) * scale
        vals = jnp.einsum('bhij,bjhd->bihd', attn, V).reshape(B, NQ, INNER)
        out = vals @ Wo + bo
        return x + out

    def _L3_xattn_ref(x, context, Wq1, Wk1, Wv1, Wo1, bo1, Wq2, Wk2, Wv2, Wo2, bo2, Wp, bp, W2, b2, g1, be1, g2, be2, g3, be3):
        import jax, jax.numpy as jnp
        import numpy as np
        DIM, HEADS, DHEAD, CTX_DIM = (256, 16, 64, 192)
        INNER = HEADS * DHEAD
        FF_HID = 4 * DIM
        EPS = 1e-05

        def _ln(x, g, b):
            mu = jnp.mean(x, axis=-1, keepdims=True)
            var = jnp.mean(jnp.square(x - mu), axis=-1, keepdims=True)
            return (x - mu) * jax.lax.rsqrt(var + EPS) * g + b

        def _attn(x, ctx, Wq, Wk, Wv, Wo, bo):
            b, n, _ = x.shape
            m = ctx.shape[1]
            q = (x @ Wq).reshape(b, n, HEADS, DHEAD)
            k = (ctx @ Wk).reshape(b, m, HEADS, DHEAD)
            v = (ctx @ Wv).reshape(b, m, HEADS, DHEAD)
            scale = DHEAD ** (-0.5)
            sim = jnp.einsum('bihd,bjhd->bhij', q, k) * scale
            attn = jax.nn.softmax(sim, axis=-1)
            out = jnp.einsum('bhij,bjhd->bihd', attn, v).reshape(b, n, INNER)
            return out @ Wo + bo
        h = _ln(x, g1, be1)
        x = _attn(h, h, Wq1, Wk1, Wv1, Wo1, bo1) + x
        h = _ln(x, g2, be2)
        x = _attn(h, context, Wq2, Wk2, Wv2, Wo2, bo2) + x
        h = _ln(x, g3, be3)
        y = h @ Wp + bp
        a, gate = (y[..., :FF_HID], y[..., FF_HID:])
        x = a * jax.nn.gelu(gate, approximate=False) @ W2 + b2 + x
        return x
    x = _L0_xattn_ref(x, ctx_768, L0_xattn_ln1_g, L0_xattn_ln1_b, L0_xattn_a1_Wq, L0_xattn_a1_Wk, L0_xattn_a1_Wv, L0_xattn_a1_Wo, L0_xattn_a1_bo, L0_xattn_ln2_g, L0_xattn_ln2_b, L0_xattn_a2_Wq, L0_xattn_a2_Wk, L0_xattn_a2_Wv, L0_xattn_a2_Wo, L0_xattn_a2_bo, L0_xattn_ln3_g, L0_xattn_ln3_b, L0_xattn_ff_Wp, L0_xattn_ff_bp, L0_xattn_ff_Wo, L0_xattn_ff_bo)
    x = _L1_xattn_ref(x, ctx_768, mask_BxS2_if1, L1_xattn_Wq, L1_xattn_Wk, L1_xattn_Wv, L1_xattn_Wo, L1_xattn_gamma, L1_xattn_beta)
    x = _L2_xattn_ref(x, ctx_768, L2_xattn_Wq, L2_xattn_Wk, L2_xattn_Wv, L2_xattn_Wo, L2_xattn_bo, L2_xattn_gamma, L2_xattn_beta)
    x = _L3_xattn_ref(x, ctx_768, L3_xattn_Wq1, L3_xattn_Wk1, L3_xattn_Wv1, L3_xattn_Wo1, L3_xattn_bo1, L3_xattn_Wq2, L3_xattn_Wk2, L3_xattn_Wv2, L3_xattn_Wo2, L3_xattn_bo2, L3_xattn_Wp, L3_xattn_bp, L3_xattn_W2, L3_xattn_b2, L3_xattn_g1, L3_xattn_be1, L3_xattn_g2, L3_xattn_be2, L3_xattn_g3, L3_xattn_be3)
    return x

_drawn_inputs = setup_inputs


def setup_inputs(seed=0):
    import zlib

    import numpy as np

    out = dict(_drawn_inputs(seed))
    spreads = {'L0_xattn_ln1_g': (1.0, 0.6),
     'L0_xattn_ln1_b': (0.0, 0.36),
     'L0_xattn_a1_bo': (0.0, 0.1),
     'L0_xattn_ln2_g': (1.0, 0.6),
     'L0_xattn_ln2_b': (0.0, 0.8),
     'L0_xattn_a2_bo': (0.0, 0.1),
     'L0_xattn_ln3_g': (1.0, 0.6),
     'L0_xattn_ln3_b': (0.0, 0.8),
     'L0_xattn_ff_bp': (0.0, 0.567),
     'L0_xattn_ff_bo': (0.0, 0.1),
     'L1_xattn_gamma': (1.0, 0.2),
     'L1_xattn_beta': (0.0, 0.1),
     'L2_xattn_bo': (0.0, 0.1),
     'L2_xattn_gamma': (1.0, 0.2),
     'L2_xattn_beta': (0.0, 0.383),
     'L3_xattn_bo1': (0.0, 0.1),
     'L3_xattn_bo2': (0.0, 0.1),
     'L3_xattn_bp': (0.0, 0.1),
     'L3_xattn_b2': (0.0, 0.1),
     'L3_xattn_g1': (1.0, 0.2),
     'L3_xattn_be1': (0.0, 0.1),
     'L3_xattn_g2': (1.0, 0.2),
     'L3_xattn_be2': (0.0, 0.465),
     'L3_xattn_g3': (1.0, 0.2),
     'L3_xattn_be3': (0.0, 0.1)}
    factors = {'L0_xattn_a1_Wq': 8.0, 'L0_xattn_a1_Wk': 8.0, 'L0_xattn_a2_Wq': 8.0, 'L0_xattn_a2_Wk': 8.0}
    for name, (base, spread) in spreads.items():
        noise = np.random.default_rng([zlib.crc32(name.encode()), seed]).standard_normal(out[name].shape)
        drawn = base * np.exp(spread * noise) if base else spread * noise
        out[name] = jnp.asarray(drawn.astype(out[name].dtype))
    for name, factor in factors.items():
        out[name] = (out[name] * factor).astype(out[name].dtype)
    return out
```

```python
from contextlib import ExitStack

import concourse.bass as bass
from concourse import mybir

ALU = mybir.AluOpType
ACT = mybir.ActivationFunctionType
F32 = mybir.dt.float32
F32R = mybir.dt.float32r
I32 = mybir.dt.int32
AX_X = mybir.AxisListType.X

P = 128
B = 16
D = 256
DC = 192
DB = DC - P
INNER = 1024
HD = 64
PAIRS = INNER // P
HID = 1024
H1 = 8
D1 = 256
GROUPS = B // 2
GT = 2 * P
EPS = 1e-5
MAGIC = float(0x5F3759DF)
NEG = -1e30
CH = 1024

SELF, CROSS, FF, L1 = "self", "cross", "ff", "l1"
KIND = [SELF, CROSS, FF, L1, CROSS, SELF, CROSS, FF]
LAST = len(KIND) - 1
L1PH = KIND.index(L1)
WEIGHTS = [
    ("L0_xattn_a1_Wq", "L0_xattn_a1_Wk", "L0_xattn_a1_Wv", "L0_xattn_a1_Wo"),
    ("L0_xattn_a2_Wq", "L0_xattn_a2_Wk", "L0_xattn_a2_Wv", "L0_xattn_a2_Wo"),
    ("L0_xattn_ff_Wp", "L0_xattn_ff_Wo"),
    ("L1_xattn_Wq", "L1_xattn_Wk", "L1_xattn_Wv", "L1_xattn_Wo"),
    ("L2_xattn_Wq", "L2_xattn_Wk", "L2_xattn_Wv", "L2_xattn_Wo"),
    ("L3_xattn_Wq1", "L3_xattn_Wk1", "L3_xattn_Wv1", "L3_xattn_Wo1"),
    ("L3_xattn_Wq2", "L3_xattn_Wk2", "L3_xattn_Wv2", "L3_xattn_Wo2"),
    ("L3_xattn_Wp", "L3_xattn_W2"),
]
NORMS = [("L0_xattn_ln1_g", "L0_xattn_ln1_b"), ("L0_xattn_ln2_g", "L0_xattn_ln2_b"),
         ("L0_xattn_ln3_g", "L0_xattn_ln3_b"), None, ("L2_xattn_gamma", "L2_xattn_beta"),
         ("L3_xattn_g1", "L3_xattn_be1"), ("L3_xattn_g2", "L3_xattn_be2"),
         ("L3_xattn_g3", "L3_xattn_be3")]
BIASES = ["L0_xattn_a1_bo", "L0_xattn_a2_bo", "L0_xattn_ff_bo", None, "L2_xattn_bo",
          "L3_xattn_bo1", "L3_xattn_bo2", "L3_xattn_b2"]
HIDDEN_BIAS = {2: "L0_xattn_ff_bp", 7: "L3_xattn_bp"}
Q_SCALE = [HD ** -0.5, HD ** -0.5, None, None, 1.0, HD ** -0.5, HD ** -0.5, None]
V_SCALE = [1.0, 1.0, None, None, HD ** -0.5, 1.0, 1.0, None]

QUADS = [{SELF: 8, CROSS: 8, FF: 0, L1: 4}[k] for k in KIND]
O_USES = [{SELF: 4, CROSS: 4, FF: 0, L1: 4}[k] for k in KIND]
MAIN_USES = [{SELF: 14, CROSS: 14, FF: 10, L1: 8}[k] for k in KIND]
PREP_USES = [{SELF: 2, CROSS: 4, FF: 2, L1: 4}[k] for k in KIND] + [0]
A_CHUNKS = [{SELF: 6, CROSS: 6, FF: 4, L1: 0}[k] for k in KIND]
B_CHUNKS = [{SELF: 2, CROSS: 2, FF: 2, L1: 0}[k] for k in KIND]


def before(counts, ph):
    return sum(counts[:ph])


G_BASE = [PREP_USES[0]]
for _p in range(len(KIND)):
    G_BASE.append(G_BASE[-1] + GROUPS * MAIN_USES[_p] + (GROUPS - 1) * PREP_USES[_p] + PREP_USES[_p + 1])


def halves_before(ph, g):
    return G_BASE[ph] // 2 + g * ((MAIN_USES[ph] + PREP_USES[ph]) // 2)


def uses_before(ph, g):
    return G_BASE[ph] + g * (MAIN_USES[ph] + PREP_USES[ph])


def quads_before(ph, g):
    return GROUPS * before(QUADS, ph) + g * QUADS[ph]


def o_before(ph, g):
    return GROUPS * before(O_USES, ph) + g * O_USES[ph]


def context_preps_before(ph, g):
    return GROUPS * sum(k in (CROSS, L1) for k in KIND[:ph]) + g


def norms_before(ph, g):
    return GROUPS * sum(k != L1 for k in KIND[:ph]) + g


def following(ph, g, last):
    if not last:
        return ph, g + 1
    return None if ph + 1 in (L1PH, LAST + 1) else (ph + 1, 0)


def build(nc, t, out):
    with ExitStack() as ctx:
        def sb(name, shape, dt=F32):
            return ctx.enter_context(nc.sbuf_tensor(name, shape, dt))

        def sem(name):
            return ctx.enter_context(nc.semaphore(name))

        X = sb("X", [P, B, D])
        XB = sb("XB", [P, 2, D])
        WAh, WAl = sb("WAh", [P, 6 * CH], F32R), sb("WAl", [P, 6 * CH], F32R)
        WBh, WBl = sb("WBh", [P, 2 * CH], F32R), sb("WBl", [P, 2 * CH], F32R)
        raw = sb("raw", [P, 8 * CH])
        big = sb("big", [P, 8 * CH])
        Oh, Ol = sb("Oh", [P, 2 * CH], F32R), sb("Ol", [P, 2 * CH], F32R)
        hTh, hTl = sb("hTh", [P, 2, GT], F32R), sb("hTl", [P, 2, GT], F32R)
        hTf = sb("hTf", [P, 2, GT])
        cRaw = sb("cRaw", [P, 2, 2 * P])
        cTh, cTl = sb("cTh", [P, 2, GT], F32R), sb("cTl", [P, 2, GT], F32R)
        Z = sb("Z", [P, 2, D])
        Pr = sb("Pr", [P, 4, 4 * P])
        PT = sb("PT", [P, 2, 4 * P])
        GE = sb("GE", [P, 2, GT])
        Uf = sb("Uf", [P, 2, GT])
        ident = sb("ident", [P, P])
        bo_rows = sb("bo_rows", [P, 9, D])
        norm_cols = sb("norm_cols", [P, len(NORMS), 2, 2])
        hid_cols = sb("hid_cols", [P, 2, 16])
        negmax = sb("negmax", [P, 4, 4])
        esum = sb("esum", [P, 4, 4])
        rsum = sb("rsum", [P, 4, 4])
        stats, means, ve = sb("stats", [P, 2, 6]), sb("means", [P, 2]), sb("ve", [P, 2])
        sa, sc, rstd = sb("sa", [P, 3, 2]), sb("sc", [P, 2, 2]), sb("rstd", [P, 4, 2])
        pstats, pmeans, pve = sb("pstats", [P, 1, 6]), sb("pmeans", [P, 1]), sb("pve", [P, 1])
        psa, psc, prstd = sb("psa", [P, 3, 1]), sb("psc", [P, 2, 1]), sb("prstd", [P, 4, 1])

        Q = big[:, 0:2 * CH].rearrange("p (f n) -> p f n", f=PAIRS)
        K = big[:, 2 * CH:6 * CH].rearrange("p (f b e n) -> p f b e n", f=PAIRS, b=2, e=2)
        V = big[:, 6 * CH:8 * CH].rearrange("p (b n) -> p b n", b=2)
        TT = big[:, 0:12 * GT].rearrange("p (m n) -> p m n", m=12)
        Sm = big[:, 12 * GT:16 * GT].rearrange("p (s h n) -> p s h n", s=2, h=4)
        cA = big[:, 16 * GT:17 * GT]
        cB = big[:, 17 * GT:19 * GT].rearrange("p (b e n) -> p b e n", b=2, e=2)
        cU = big[:, 19 * GT:21 * GT].rearrange("p (b n) -> p b n", b=2)
        maskb = big[:, 21 * GT:22 * GT].rearrange("p (b n) -> p b n", b=2)
        maski = big[:, 22 * GT:23 * GT].bitcast(I32)
        R1 = big[:, 23 * GT:24 * GT]
        R2 = big[:, 24 * GT:25 * GT]
        R3 = big[:, 25 * GT:26 * GT]
        raw_q1 = raw[:, 0:4 * CH].rearrange("p (c n) -> p c n", c=2)
        raw_k1 = raw[:, 4 * CH:8 * CH].rearrange("p (c n) -> p c n", c=2)
        raw_v1 = big[:, 0:4 * CH].rearrange("p (c n) -> p c n", c=2)
        raw_o1 = big[:, 4 * CH:8 * CH].rearrange("p (c n) -> p c n", c=16)
        NA = 12 * P

        psS = [ctx.enter_context(nc.psum_tensor(f"psS{i}", [P, 512], F32)) for i in range(3)]
        psT = ctx.enter_context(nc.psum_tensor("psT", [P, 512], F32))
        psO = [ctx.enter_context(nc.psum_tensor(f"psO{i}", [P, 512], F32)) for i in range(2)]
        psG = [ctx.enter_context(nc.psum_tensor(f"psG{i}", [P, 512], F32)) for i in range(2)]

        x_loaded = sem("x_loaded")
        params_loaded = sem("params_loaded")
        raw_loaded = sem("raw_loaded")
        big_loaded = sem("big_loaded")
        context_loaded = sem("context_loaded")
        mask_loaded = sem("mask_loaded")
        stored = sem("stored")
        ident_ready = sem("ident_ready")
        k_zeroed = sem("k_zeroed")
        wa_rounded, wa_split = sem("wa_rounded"), sem("wa_split")
        wb_rounded, wb_split = sem("wb_rounded"), sem("wb_split")
        g_full = sem("g_full")
        g_drained = [sem("g_drained0"), sem("g_drained1")]
        ln_step = sem("ln_step")
        z_ready = sem("z_ready")
        x_turned = sem("x_turned")
        c_turned = sem("c_turned")
        cu_copied = sem("cu_copied")
        turn_step = sem("turn_step")
        s_full = sem("s_full")
        max_ready = sem("max_ready")
        mask_added = sem("mask_added")
        mask_ready = sem("mask_ready")
        exp_done = sem("exp_done")
        rsum_ready = sem("rsum_ready")
        p_ready = sem("p_ready")
        t_full = sem("t_full")
        pt_ready = sem("pt_ready")
        pv_done = sem("pv_done")
        o_rounded, o_drained = sem("o_rounded"), sem("o_drained")
        xb_ready = sem("xb_ready")
        gelu_done = sem("gelu_done")
        gh_done, gl_done = sem("gh_done"), sem("gl_done")
        post_step = sem("post_step")
        post_done = sem("post_done")
        pre_turned, pre_q, pre_k = sem("pre_turned"), sem("pre_q"), sem("pre_k")
        pre_full, pre_hi, pre_lo = sem("pre_full"), sem("pre_hi"), sem("pre_lo")

        MOMENT_STEPS = 9 + 9
        LN_STEPS = 2 + MOMENT_STEPS
        POST_STEPS = 1 + MOMENT_STEPS + 2

        def rows_of(ph):
            w = [t[n] for n in WEIGHTS[ph]]
            if KIND[ph] == FF:
                yield raw[:, 0:4 * CH].rearrange("p (c n) -> p c n", c=2), w[0].rearrange("(c p) n -> p c n", p=P)
                yield raw[:, 6 * CH:8 * CH].rearrange("p (c n) -> p c n", c=8), w[1].rearrange("(c p) n -> p c n", p=P)
                return
            if KIND[ph] == L1:
                yield raw_q1, w[0].rearrange("(c p) n -> p c n", p=P)
                yield raw_k1[:, 0, :], w[1][0:P, :]
                yield raw_k1[0:DB, 1, :], w[1][P:DC, :]
                return
            yield raw[:, 0:2 * CH].rearrange("p (c n) -> p c n", c=2), w[0].rearrange("(c p) n -> p c n", p=P)
            for n in (1, 2):
                to = raw[:, 2 * n * CH:(2 * n + 2) * CH].rearrange("p (c n) -> p c n", c=2)
                if KIND[ph] == SELF:
                    yield to, w[n].rearrange("(c p) n -> p c n", p=P)
                else:
                    yield to[:, 0, :], w[n][0:P, :]
                    yield to[0:DB, 1, :], w[n][P:DC, :]
                    yield to[DB:P, 1, :], w[n][P:DC, :]
            yield raw[:, 6 * CH:8 * CH].rearrange("p (c n) -> p c n", c=8), w[3].rearrange("(c p) n -> p c n", p=P)

        RAW_DMAS = [{SELF: 4, CROSS: 8, FF: 2, L1: 3}[k] for k in KIND]

        def raw_due(ph):
            return 16 * before(RAW_DMAS, ph + 1)

        def wa_due(ph, chunks):
            return before(A_CHUNKS, ph) + chunks

        def wb_due(ph, chunks):
            return before(B_CHUNKS, ph) + chunks

        def stacked(ph, c):
            return KIND[ph] == CROSS and c in (3, 5)

        x_rest_loaded = sem("x_rest_loaded")

        PARAMS = 3

        def gh_due(ph, g, tiles):
            return GROUPS * 8 * sum(k == FF for k in KIND[:ph]) + 8 * g + tiles

        def prep_uses(nxt):
            return PREP_USES[nxt[0]] if nxt else 0

        def product_parts(W, n):
            h, e = n % H1, n % 2
            ps = psG[n % 2]
            if n < H1:
                to = W[:, 0:2 * NA].rearrange("p (c n) -> p c n", c=2)
                of = ps[:, 0:2 * DC].rearrange("p (c n) -> p c n", c=2)
                return [(to[:, :, h * P:(h + 1) * P], of[:, :, 0:P]),
                        (to[:, :, CH + h * DB:CH + (h + 1) * DB], of[:, :, P:DC])]
            rows, at = slice(e * DB, (e + 1) * DB), 2 * NA + H1 * D + (h // 2) * D
            return [(W[:, 2 * NA + h * D:2 * NA + (h + 1) * D], ps[:, 0:D]),
                    (W[rows, at:at + D], ps[rows, D:2 * D])]

        block = ctx.enter_context(nc.Block())

        def chunk(c):
            return slice(c * CH, (c + 1) * CH)

        def groups(eng, body, ph):
            with eng.Fori(0, GROUPS - 1) as g:
                body(ph, g, False)
            body(ph, GROUPS - 1, True)


        @block.sync
        def _(sp):
            def load_weights(ph):
                for to, src in rows_of(ph):
                    sp.dma_start(to, src).then_inc(raw_loaded, 16)

            def load_context(ph, g):
                n = context_preps_before(ph, g)
                if ph > 1 or not isinstance(g, int):
                    sp.wait_ge(c_turned, 2 * n)
                if ph == L1PH and not (isinstance(g, int) and g == 0):
                    sp.wait_ge(cu_copied, g)
                if ph == L1PH + 1 and isinstance(g, int) and g == 0:
                    sp.wait_ge(cu_copied, GROUPS)
                src = t["ctx_768"][bass.ds(2 * g, 2), :, :].rearrange("b p n -> p b n")
                sp.dma_start(cRaw[:, :, 0:DC], src).then_inc(context_loaded, 16)
                sp.dma_start(cRaw[:, :, DC:2 * P], src[:, :, P:DC]).then_inc(context_loaded, 16)

            def load_mask(g):
                rows = t["mask_BxS2_if1"][bass.ds(2 * g, 2), :].rearrange("b n -> (b n)")
                sp.dma_start(maski, rows.partition_broadcast(P)).then_inc(mask_loaded, 16)

            def body(ph, g, last):
                if KIND[ph] == L1 and not last:
                    sp.wait_ge(mask_ready, g + 1)
                    load_mask(g + 1)
                nxt = following(ph, g, last)
                if nxt and KIND[nxt[0]] in (CROSS, L1):
                    load_context(*nxt)
                if ph == LAST:
                    for k in (0, 1):
                        sp.wait_ge(g_drained[k], G_BASE[LAST + 1] // 2 if last else halves_before(ph, g + 1))
                    sp.dma_start(out[bass.ds(2 * g, 2), :, :].rearrange("b p n -> p b n"),
                                 X[:, bass.ds(2 * g, 2), :]).then_inc(stored, 16)

            xs = t["x"].rearrange("b p n -> p b n")
            sp.dma_start(X[:, 0:2, :], xs[:, 0:2, :]).then_inc(x_loaded, 16)
            load_weights(0)
            sp.dma_start(X[:, 2:B, :], xs[:, 2:B, :]).then_inc(x_rest_loaded, 16)
            for ph in range(len(KIND)):
                if ph < LAST and ph + 1 != L1PH + 1:
                    if KIND[ph] != L1:
                        sp.wait_ge(wa_split, wa_due(ph, A_CHUNKS[ph]))
                        sp.wait_ge(wb_split, wb_due(ph, B_CHUNKS[ph]))
                    load_weights(ph + 1)
                if ph + 1 == L1PH:
                    sp.wait_ge(g_full, uses_before(ph, 0))
                    sp.dma_start(raw_v1[:, 0, :], t["L1_xattn_Wv"][0:P, :]).then_inc(big_loaded, 16)
                    sp.dma_start(raw_v1[0:DB, 1, :], t["L1_xattn_Wv"][P:DC, :]).then_inc(big_loaded, 16)
                    sp.dma_start(raw_o1, t["L1_xattn_Wo"].rearrange("(c p) n -> p c n", p=P)).then_inc(big_loaded, 16)
                if ph == L1PH:
                    load_context(ph, 0)
                    sp.wait_ge(pre_turned, H1)
                    load_weights(ph + 1)
                    sp.wait_ge(pre_full, 2 * H1)
                    load_mask(0)
                groups(sp, body, ph)
            sp.wait_ge(stored, 16 * GROUPS)

        @block.gpsimd
        def _(pool):
            pool.memset(ident[:, :], 0.0).then_inc(ident_ready, 1)
            pool.wait_ge(ident_ready, 1)
            pool.affine_select(out=ident[:, :], in_=ident[:, :], compare_op=ALU.not_equal, fill=1.0, base=0,
                               pattern=[[-1, P]], channel_multiplier=1).then_inc(ident_ready, 1)
            def low_part(ph, c):
                pool.wait_ge(wa_rounded, wa_due(ph, c + 1))
                to, off = (WAh, WAl) if stacked(ph, c) else (WAl, WAh)
                pool.tensor_tensor(to[:, chunk(c)], raw[:, chunk(c)], off[:, chunk(c)].bitcast(F32),
                                   ALU.subtract).then_inc(wa_split, 1)

            def normalise(ph, g, i):
                qb = quads_before(ph, g)
                pool.wait_ge(rsum_ready, qb + i + 1)
                p4 = Pr[:, i % 4, :].rearrange("p (h n) -> p h n", h=4)
                pool.tensor_tensor(p4, p4, rsum[:, i % 4, :].unsqueeze(2).to_broadcast([P, 4, P]),
                                   ALU.mult).then_inc(p_ready, 1)

            def body(ph, g, last):
                if KIND[ph] != L1:
                    for k in (0, 1):
                        pool.wait_ge(g_drained[k], halves_before(ph, g))
                    if ph == L1PH + 1:
                        pool.wait_ge(post_done, B)
                    pool.tensor_tensor(XB[:, :, :], X[:, bass.ds(2 * g, 2), :],
                                       bo_rows[:, ph:ph + 1, :].to_broadcast([P, 2, D]), ALU.add).then_inc(xb_ready, 1)
                if KIND[ph] == FF:
                    for m in range(8):
                        pool.wait_ge(gh_done, gh_due(ph, g, m + 1))
                        pool.tensor_tensor(Ol[:, m * GT:(m + 1) * GT], Uf[:, m % 2, :],
                                           Oh[:, m * GT:(m + 1) * GT].bitcast(F32), ALU.subtract).then_inc(gl_done, 1)
                for i in range(QUADS[ph]):
                    normalise(ph, g, i)
                    if last and KIND[ph] in (SELF, CROSS) and i < A_CHUNKS[ph + 1]:
                        low_part(ph + 1, i)

            pool.wait_ge(params_loaded, 16 * PARAMS)
            pool.wait_ge(x_loaded, 16)
            pool.wait_ge(x_rest_loaded, 16)
            for ph in range(len(KIND)):
                for c in range(B_CHUNKS[ph]):
                    pool.wait_ge(wb_rounded, wb_due(ph, c + 1))
                    pool.tensor_tensor(WBl[:, chunk(c)], raw[:, chunk(6 + c)], WBh[:, chunk(c)].bitcast(F32),
                                       ALU.subtract).then_inc(wb_split, 1)
                groups(pool, body, ph)

        @block.scalar
        def _(act):
            act.dma_start(norm_cols[:, :, :, :], t["norm_columns"]).then_inc(params_loaded, 16)
            act.dma_start(hid_cols[:, :, :], t["hidden_bias_columns"]).then_inc(params_loaded, 16)
            act.dma_start(bo_rows[:, :, :], t["bias_rows"].partition_broadcast(P)).then_inc(params_loaded, 16)

            def round_chunk(ph, c):
                if stacked(ph, c):
                    act.activation(WAl[0:DB, chunk(c)], raw[0:DB, chunk(c)], ACT.Copy, scale=0.0)
                    act.activation(WAl[DB:P, chunk(c)], raw[DB:P, chunk(c)], ACT.Copy).then_inc(wa_rounded, 1)
                else:
                    act.activation(WAh[:, chunk(c)], raw[:, chunk(c)], ACT.Copy).then_inc(wa_rounded, 1)

            def turn_x(ph, g, first):
                use, parity = first
                for b in range(2):
                    ps = psG[(parity + b) % 2]
                    act.wait_ge(g_full, use + b + 1)
                    if KIND[ph] == L1:
                        act.activation(hTh[:, :, b * P:(b + 1) * P], ps[:, 0:GT].rearrange("p (c n) -> p c n", c=2),
                                       ACT.Copy).then_inc(x_turned, 1)
                        continue
                    for c in range(2):
                        ins = act.activation(hTh[:, c, b * P:(b + 1) * P], ps[:, c * P:(c + 1) * P], ACT.Identity,
                                             scale=norm_cols[:, ph, 0, c:c + 1], bias=norm_cols[:, ph, 1, c:c + 1])
                    ins.then_inc(x_turned, 1)

            def turn_c(ph, first):
                use, parity = first
                for b in range(2):
                    ps = psG[(parity + b) % 2]
                    act.wait_ge(g_full, use + b + 1)
                    if KIND[ph] == L1:
                        act.activation(cA[:, b * P:(b + 1) * P], ps[:, 0:P], ACT.Copy).then_inc(c_turned, 1)
                    else:
                        act.activation(cTh[:, :, b * P:(b + 1) * P], ps[:, 0:GT].rearrange("p (c n) -> p c n", c=2),
                                       ACT.Copy).then_inc(c_turned, 1)

            def exps(ph, g, i, scores):
                qb = quads_before(ph, g)
                act.wait_ge(max_ready, qb + i + 1)
                for h in range(4):
                    ins = act.activation(Pr[:, i % 4, h * P:(h + 1) * P], scores[:, h * P:(h + 1) * P], ACT.Exp,
                                         bias=negmax[:, i % 4, h:h + 1], accum_out=esum[:, i % 4, h:h + 1])
                ins.then_inc(exp_done, 1)

            def round_o(ph, g, o):
                act.wait_ge(pv_done, quads_before(ph, g) + 2 * o + 2)
                act.activation(Oh[:, o * 512:(o + 1) * 512], psO[o % 2][:, :], ACT.Copy).then_inc(o_rounded, 1)

            def attention(ph, g, last):
                nxt, ub = following(ph, g, last), uses_before(ph, g)
                for u in range(4):
                    act.wait_ge(g_full, ub + u + 1)
                    act.activation(Q[:, 2 * u:2 * u + 2, :], psG[u % 2][:, :].rearrange("p (f n) -> p f n", f=2),
                                   ACT.Copy, scale=Q_SCALE[ph]).then_inc(g_drained[u % 2], 1)
                for u in (1, 3):
                    act.wait_ge(g_full, ub + 4 + u + 1)
                    for e in range(2):
                        rows = slice(e * HD, (e + 1) * HD)
                        ins = act.activation(K[rows, 2 * u:2 * u + 2, :, e, :],
                                             psG[u % 2][rows, :].rearrange("p (f b n) -> p f b n", f=2, b=2), ACT.Copy)
                    ins.then_inc(g_drained[u % 2], 1)
                exps(ph, g, 0, psS[0])
                exps(ph, g, 1, psS[1])
                for k in (9, 11):
                    act.wait_ge(g_full, ub + k + 1)
                    act.activation(V[:, (k - 8) // 2, 512:1024], psG[k % 2][:, :], ACT.Copy,
                                   scale=V_SCALE[ph]).then_inc(g_drained[k % 2], 1)
                exps(ph, g, 2, psS[2])
                for i in range(8):
                    if i + 3 < 8:
                        exps(ph, g, i + 3, psS[(i + 3) % 3])
                    if i in (2, 4, 6):
                        round_o(ph, g, i // 2 - 1)
                    if last and nxt and i < A_CHUNKS[nxt[0]]:
                        if i == 0:
                            act.wait_ge(g_full, ub + 12)
                            act.wait_ge(raw_loaded, raw_due(nxt[0]))
                        round_chunk(nxt[0], i)
                round_o(ph, g, 3)
                if nxt:
                    turn_x(*nxt, (ub + 13, 1))
                    if KIND[nxt[0]] == CROSS:
                        turn_c(nxt[0], (ub + 15, 1))

            def mlp(ph, g, last):
                nxt, ub = following(ph, g, last), uses_before(ph, g)
                bias = hid_cols[:, list(HIDDEN_BIAS).index(ph), :]

                def gate(m):
                    act.wait_ge(g_full, ub + m + 1)
                    if m >= 2:
                        act.wait_ge(g_drained[m % 2], halves_before(ph, g) + m // 2)
                    act.activation(GE[:, m % 2, :], psG[m % 2][:, GT:2 * GT], ACT.Gelu,
                                   bias=bias[:, 8 + m:9 + m]).then_inc(gelu_done, 1)

                def round_hidden(m):
                    act.wait_ge(g_drained[m % 2], halves_before(ph, g) + m // 2 + 1)
                    act.activation(Oh[:, m * GT:(m + 1) * GT], Uf[:, m % 2, :], ACT.Copy).then_inc(gh_done, 1)

                gate(0)
                for m in range(1, 8):
                    gate(m)
                    round_hidden(m - 1)
                round_hidden(7)
                if nxt:
                    turn_x(*nxt, (ub + 8, 0))
                    if KIND[nxt[0]] == CROSS:
                        turn_c(nxt[0], (ub + 10, 0))

            def reassociated(ph, g, last):
                nxt, ub, qb = following(ph, g, last), uses_before(ph, g), quads_before(ph, g)

                def round_u(i):
                    act.wait_ge(pv_done, qb + i + 1)
                    if i == 2:
                        act.wait_ge(g_full, ub + 7)
                    j = i % 2
                    act.activation(Oh[:, j * 512:(j + 1) * 512], psO[0][:, :], ACT.Copy)
                    act.activation(Oh[:, CH + j * GT:CH + (j + 1) * GT], psO[1][:, 0:GT], ACT.Copy).then_inc(o_rounded, 1)

                for u in (1, 3, 5):
                    act.wait_ge(g_full, ub + u + 1)
                    act.activation(TT[:, 2 * u:2 * u + 2, :], psG[1][:, :].rearrange("p (m n) -> p m n", m=2),
                                   ACT.Copy, scale=D1 ** -0.5).then_inc(g_drained[1], 1)
                for i in range(4):
                    exps(ph, g, i, Sm[:, i % 2, :, :].rearrange("p h n -> p (h n)"))
                for i in range(3):
                    round_u(i)
                if nxt:
                    turn_x(*nxt, (ub + 7, 1))
                round_u(3)
                if nxt:
                    turn_c(nxt[0], (ub + 9, 1))
                if last:
                    act.wait_ge(g_full, uses_before(ph + 1, 0))
                    act.wait_ge(raw_loaded, raw_due(ph + 1))
                    for c in range(A_CHUNKS[ph + 1]):
                        round_chunk(ph + 1, c)

            def round_product(n):
                h, e = n % H1, n % 2
                act.wait_ge(pre_full, n + 1)
                for to, of in product_parts(WAh, n):
                    ins = act.activation(to, of, ACT.Copy)
                ins.then_inc(pre_hi, 1)

            bodies = {SELF: attention, CROSS: attention, FF: mlp, L1: reassociated}
            act.wait_ge(raw_loaded, raw_due(0))
            for c in range(A_CHUNKS[0]):
                round_chunk(0, c)
                if c == 1:
                    act.wait_ge(params_loaded, 16 * PARAMS)
                    turn_x(0, 0, (0, 0))
            for ph in range(len(KIND)):
                if KIND[ph] == L1:
                    act.wait_ge(g_full, uses_before(ph, 0) - PREP_USES[ph])
                    for n in range(2 * H1):
                        h, s = n % H1, n % 2
                        if n < H1:
                            act.wait_ge(pre_turned, n + 1)
                            if n >= 2:
                                act.wait_ge(pre_full, n - 1)
                            act.activation(Pr[:, 2 * s, :], psS[s][:, :], ACT.Copy).then_inc(pre_q, 1)
                        if n >= 1:
                            round_product(n - 1)
                    round_product(2 * H1 - 1)
                    turn_x(ph, 0, (uses_before(ph, 0) - 4, 0))
                    turn_c(ph, (uses_before(ph, 0) - 2, 0))
                for c in range(B_CHUNKS[ph]):
                    if c == 0:
                        act.wait_ge(raw_loaded, raw_due(ph))
                        if ph > 0:
                            act.wait_ge(g_full, uses_before(ph, 0))
                    act.activation(WBh[:, chunk(c)], raw[:, chunk(6 + c)], ACT.Copy).then_inc(wb_rounded, 1)
                groups(act, bodies[KIND[ph]], ph)

        @block.vector
        def _(dve):
            def moments(step, done, st, m, y, a, c, e):
                dve.wait_ge(step, done)
                dve.tensor_tensor(a[:, 0, :], st[:, :, 1], st[:, :, 4], ALU.add).then_inc(step, 1)
                dve.tensor_tensor(a[:, 1, :], st[:, :, 1], st[:, :, 4], ALU.subtract).then_inc(step, 1)
                dve.tensor_tensor(a[:, 2, :], st[:, :, 2], st[:, :, 5], ALU.add).then_inc(step, 1)
                dve.wait_ge(step, done + 3)
                dve.tensor_scalar(m, a[:, 0, :], 0.5, None, ALU.mult).then_inc(step, 1)
                dve.scalar_tensor_tensor(c[:, 0, :], a[:, 1, :], 0.25, a[:, 1, :], ALU.mult, ALU.mult).then_inc(step, 1)
                dve.tensor_scalar(c[:, 1, :], a[:, 2, :], 1.0 / D, EPS, ALU.mult, ALU.add).then_inc(step, 1)
                dve.wait_ge(step, done + 6)
                dve.tensor_tensor(e, c[:, 0, :], c[:, 1, :], ALU.add).then_inc(step, 1)
                a, c = a[:, 0, :], c[:, 0, :]
                dve.wait_ge(step, done + 7)
                dve.tensor_scalar(a.bitcast(I32), e.bitcast(I32), 1, None, ALU.logical_shift_right).then_inc(step, 1)
                dve.wait_ge(step, done + 8)
                dve.tensor_scalar(y[:, 0, :].bitcast(I32), a.bitcast(I32), -1.0, MAGIC, ALU.mult, ALU.add).then_inc(step, 1)
                for k in range(3):
                    now = done + 9 + 3 * k
                    dve.wait_ge(step, now)
                    dve.tensor_tensor(a, y[:, k, :], y[:, k, :], ALU.mult).then_inc(step, 1)
                    dve.wait_ge(step, now + 1)
                    dve.scalar_tensor_tensor(c, a, -0.5, e, ALU.mult, ALU.mult).then_inc(step, 1)
                    dve.wait_ge(step, now + 2)
                    dve.scalar_tensor_tensor(y[:, k + 1, :], c, 1.5, y[:, k, :], ALU.add, ALU.mult).then_inc(step, 1)

            def normalise_tokens(ph, g):
                if KIND[ph] == L1:
                    for b in range(2):
                        dve.tensor_copy(Z[:, b:b + 1, :], X[:, bass.ds(2 * g + b, 1), :]).then_inc(z_ready, 1)
                    return
                done = LN_STEPS * norms_before(ph, g)
                for b in range(2):
                    dve.bn_stats(stats[:, b, :], X[:, bass.ds(2 * g + b, 1), :].rearrange("p b n -> p (b n)")).then_inc(ln_step, 1)
                moments(ln_step, done + 2, stats, means[:, :], rstd, sa, sc, ve[:, :])
                dve.wait_ge(ln_step, done + LN_STEPS)
                for b in range(2):
                    dve.tensor_scalar(Z[:, b:b + 1, :], X[:, bass.ds(2 * g + b, 1), :], means[:, b:b + 1], rstd[:, 3, b:b + 1],
                                      ALU.subtract, ALU.mult).then_inc(z_ready, 1)

            def turn_x(ph, g, first):
                use, parity = first
                r, done = 2 * (GROUPS * ph + g), 4 * norms_before(ph, g)
                for b in range(2):
                    k = (parity + b) % 2
                    ps, cols = psG[k], slice(b * P, (b + 1) * P)
                    dve.wait_ge(g_full, use + b + 1)
                    dve.wait_ge(x_turned, r + b + 1)
                    if KIND[ph] == L1:
                        dve.tensor_tensor(hTl[:, :, cols], ps[:, 0:GT].rearrange("p (c n) -> p c n", c=2),
                                          hTh[:, :, cols].bitcast(F32), ALU.subtract).then_inc(g_drained[k], 1)
                        continue
                    for c in range(2):
                        dve.tensor_scalar(hTf[:, c, cols], ps[:, c * P:(c + 1) * P], norm_cols[:, ph, 0, c:c + 1],
                                          norm_cols[:, ph, 1, c:c + 1], ALU.mult, ALU.add).then_inc(turn_step, 1)
                    dve.wait_ge(turn_step, done + 2 * b + 2)
                    dve.tensor_tensor(hTl[:, :, cols], hTf[:, :, cols], hTh[:, :, cols].bitcast(F32),
                                      ALU.subtract).then_inc(g_drained[k], 1)

            def turn_c(ph, g, first):
                use, parity = first
                n = 2 * context_preps_before(ph, g)
                for b in range(2):
                    k = (parity + b) % 2
                    ps, cols = psG[k], slice(b * P, (b + 1) * P)
                    dve.wait_ge(g_full, use + b + 1)
                    dve.wait_ge(c_turned, n + b + 1)
                    if KIND[ph] == L1:
                        dve.tensor_copy(cB[0:DB, b, 0, :], ps[0:DB, P:2 * P])
                        dve.tensor_copy(cB[DB:P, b, 1, :], ps[DB:P, P:2 * P]).then_inc(g_drained[k], 1)
                    else:
                        dve.tensor_tensor(cTl[:, :, cols], ps[:, 0:GT].rearrange("p (c n) -> p c n", c=2),
                                          cTh[:, :, cols].bitcast(F32), ALU.subtract).then_inc(g_drained[k], 1)
                if KIND[ph] == L1:
                    dve.tensor_copy(cU[:, :, 0:DC], cRaw[:, :, 0:DC]).then_inc(cu_copied, 1)

            def maxima(ph, g, i, scores):
                dve.reduce_max(negmax[:, i % 4, :], scores, AX_X, negate=True).then_inc(max_ready, 1)

            def score_maxima(ph, g, i):
                dve.wait_ge(s_full, quads_before(ph, g) + i + 1)
                maxima(ph, g, i, psS[i % 3][:, :].rearrange("p (h n) -> p h n", h=4))

            def reciprocals(ph, g, i):
                dve.wait_ge(exp_done, quads_before(ph, g) + i + 1)
                dve.reciprocal(rsum[:, i % 4, :], esum[:, i % 4, :]).then_inc(rsum_ready, 1)

            def drain_turned(ph, g, i):
                dve.wait_ge(t_full, quads_before(ph, g) + i + 1)
                dve.tensor_copy(PT[:, i % 2, :], psT[:, :]).then_inc(pt_ready, 1)

            def low_o(ph, g, o):
                dve.wait_ge(o_rounded, o_before(ph, g) + o + 1)
                cols = slice(o * 512, (o + 1) * 512)
                dve.tensor_tensor(Ol[:, cols], psO[o % 2][:, :], Oh[:, cols].bitcast(F32),
                                  ALU.subtract).then_inc(o_drained, 1)

            def residual(ph, g, b, use, k):
                dve.wait_ge(g_full, use + 1)
                dve.wait_ge(xb_ready, norms_before(ph, g) + 1)
                dve.tensor_tensor(X[:, bass.ds(2 * g + b, 1), :], psG[k][:, 0:D].unsqueeze(1), XB[:, b:b + 1, :],
                                  ALU.add).then_inc(g_drained[k], 1)

            def own_writes(ph, g):
                for k in (0, 1):
                    dve.wait_ge(g_drained[k], halves_before(ph, g))
                if ph == L1PH + 1:
                    dve.wait_ge(post_done, B)

            def attention(ph, g, last):
                nxt, ub = following(ph, g, last), uses_before(ph, g)
                own_writes(ph, g)
                if nxt:
                    normalise_tokens(*nxt)
                for u in (0, 2):
                    dve.wait_ge(g_full, ub + 4 + u + 1)
                    for e in range(2):
                        rows = slice(e * HD, (e + 1) * HD)
                        ins = dve.tensor_copy(K[rows, 2 * u:2 * u + 2, :, e, :],
                                              psG[0][rows, :].rearrange("p (f b n) -> p f b n", f=2, b=2))
                    ins.then_inc(g_drained[0], 1)
                score_maxima(ph, g, 0)
                score_maxima(ph, g, 1)
                for k in (8, 10):
                    dve.wait_ge(g_full, ub + k + 1)
                    dve.tensor_scalar(V[:, (k - 8) // 2, 0:512], psG[0][:, :], V_SCALE[ph], None,
                                      ALU.mult).then_inc(g_drained[0], 1)
                reciprocals(ph, g, 0)
                reciprocals(ph, g, 1)
                score_maxima(ph, g, 2)
                for i in range(8):
                    if i in (3, 5, 7):
                        low_o(ph, g, (i - 3) // 2)
                    drain_turned(ph, g, i)
                    if i + 3 < 8:
                        score_maxima(ph, g, i + 3)
                    if i + 2 < 8:
                        reciprocals(ph, g, i + 2)
                residual(ph, g, 0, ub + 12, 0)
                low_o(ph, g, 3)
                if nxt:
                    turn_x(*nxt, (ub + 13, 1))
                    if KIND[nxt[0]] == CROSS:
                        turn_c(*nxt, (ub + 15, 1))
                residual(ph, g, 1, ub + 13 + prep_uses(nxt), 1)

            def mlp(ph, g, last):
                nxt, ub = following(ph, g, last), uses_before(ph, g)
                bias = hid_cols[:, list(HIDDEN_BIAS).index(ph), :]
                own_writes(ph, g)
                for m in range(8):
                    dve.wait_ge(gelu_done, gh_due(ph, g, m + 1))
                    if m >= 2:
                        dve.wait_ge(gl_done, gh_due(ph, g, m - 1))
                    dve.scalar_tensor_tensor(Uf[:, m % 2, :], psG[m % 2][:, 0:GT], bias[:, m:m + 1], GE[:, m % 2, :],
                                             ALU.add, ALU.mult).then_inc(g_drained[m % 2], 1)
                    if m == 3 and nxt:
                        normalise_tokens(*nxt)
                if nxt:
                    turn_x(*nxt, (ub + 8, 0))
                    if KIND[nxt[0]] == CROSS:
                        turn_c(*nxt, (ub + 10, 0))
                for b in range(2):
                    residual(ph, g, b, ub + 8 + b + prep_uses(nxt), b)

            def reassociated(ph, g, last):
                nxt, ub, qb = following(ph, g, last), uses_before(ph, g), quads_before(ph, g)
                own_writes(ph, g)
                if nxt:
                    normalise_tokens(*nxt)
                dve.wait_ge(mask_loaded, 16 * g + 16)
                dve.tensor_scalar(maskb.rearrange("p b n -> p (b n)"), maski, 0, NEG, ALU.is_equal,
                                  ALU.mult).then_inc(mask_ready, 1)
                for u in (0, 2, 4):
                    dve.wait_ge(g_full, ub + u + 1)
                    dve.tensor_scalar(TT[:, 2 * u:2 * u + 2, :], psG[0][:, :].rearrange("p (m n) -> p m n", m=2),
                                      D1 ** -0.5, None, ALU.mult).then_inc(g_drained[0], 1)
                dve.wait_ge(mask_ready, g + 1)

                def masked(i):
                    dve.wait_ge(s_full, qb + i + 1)
                    if i >= 2:
                        dve.wait_ge(exp_done, qb + i - 1)
                    dve.tensor_tensor(Sm[:, i % 2, :, :], psS[i % 3][:, :].rearrange("p (h n) -> p h n", h=4),
                                      maskb[:, i // 2:i // 2 + 1, :].to_broadcast([P, 4, P]), ALU.add).then_inc(mask_added, 1)
                    dve.wait_ge(mask_added, 4 * g + i + 1)
                    maxima(ph, g, i, Sm[:, i % 2, :, :])

                def low_u(i):
                    dve.wait_ge(o_rounded, o_before(ph, g) + i + 1)
                    j = i % 2
                    for cols, of in ((slice(j * 512, (j + 1) * 512), psO[0][:, :]),
                                     (slice(CH + j * GT, CH + (j + 1) * GT), psO[1][:, 0:GT])):
                        ins = dve.tensor_tensor(Ol[:, cols], of, Oh[:, cols].bitcast(F32), ALU.subtract)
                    ins.then_inc(o_drained, 1)

                def post_norm(b, ub, offset, k):
                    done = POST_STEPS * (2 * g + b)
                    dve.wait_ge(g_full, ub + offset + 1)
                    dve.tensor_tensor(R1.unsqueeze(1), psG[k][:, 0:D].unsqueeze(1), X[:, bass.ds(2 * g + b, 1), :],
                                      ALU.add).then_inc(g_drained[k], 1)
                    dve.wait_ge(g_drained[k], halves_before(ph, g) + offset // 2 + 1)
                    dve.bn_stats(pstats[:, 0, :], R1).then_inc(post_step, 1)
                    moments(post_step, done + 1, pstats, pmeans[:, :], prstd, psa, psc, pve[:, :])
                    dve.wait_ge(post_step, done + 1 + MOMENT_STEPS)
                    dve.tensor_scalar(R2, R1, pmeans[:, :], prstd[:, 3, :], ALU.subtract, ALU.mult).then_inc(post_step, 1)
                    dve.wait_ge(post_step, done + 2 + MOMENT_STEPS)
                    dve.tensor_tensor(R3, R2, bo_rows[:, L1PH, :], ALU.mult).then_inc(post_step, 1)
                    dve.wait_ge(post_step, done + 3 + MOMENT_STEPS)
                    dve.tensor_tensor(X[:, bass.ds(2 * g + b, 1), :], R3.unsqueeze(1), bo_rows[:, 8:9, :],
                                      ALU.add).then_inc(post_done, 1)

                masked(0)
                masked(1)
                reciprocals(ph, g, 0)
                masked(2)
                reciprocals(ph, g, 1)
                drain_turned(ph, g, 0)
                masked(3)
                reciprocals(ph, g, 2)
                drain_turned(ph, g, 1)
                low_u(0)
                reciprocals(ph, g, 3)
                drain_turned(ph, g, 2)
                low_u(1)
                drain_turned(ph, g, 3)
                low_u(2)
                post_norm(0, ub, 6, 0)
                if nxt:
                    turn_x(*nxt, (ub + 7, 1))
                low_u(3)
                if nxt:
                    turn_c(*nxt, (ub + 9, 1))
                post_norm(1, ub, 7 + prep_uses(nxt), 1)

            def low_product(n):
                dve.wait_ge(pre_hi, n + 1)
                for (to, of), (hi, _) in zip(product_parts(WAl, n), product_parts(WAh, n)):
                    ins = dve.tensor_tensor(to, of, hi.bitcast(F32), ALU.subtract)
                ins.then_inc(pre_lo, 1)

            def low_chunk(ph, c):
                dve.wait_ge(wa_rounded, wa_due(ph, c + 1))
                to, off = (WAh, WAl) if stacked(ph, c) else (WAl, WAh)
                dve.tensor_tensor(to[:, chunk(c)], raw[:, chunk(c)], off[:, chunk(c)].bitcast(F32),
                                  ALU.subtract).then_inc(wa_split, 1)

            bodies = {SELF: attention, CROSS: attention, FF: mlp, L1: reassociated}

            def zero_k():
                dve.memset(K[0:HD, :, :, 1, :], 0.0).then_inc(k_zeroed, 1)
                dve.memset(K[HD:P, :, :, 0, :], 0.0).then_inc(k_zeroed, 1)

            zero_k()
            dve.wait_ge(x_loaded, 16)
            normalise_tokens(0, 0)
            for c in range(A_CHUNKS[0]):
                low_chunk(0, c)
                if c == 1:
                    turn_x(0, 0, (0, 0))
            dve.wait_ge(x_rest_loaded, 16)
            for ph in range(len(KIND)):
                if KIND[ph] == L1:
                    own_writes_before_l1 = uses_before(ph, 0) - PREP_USES[ph]
                    for k in (0, 1):
                        dve.wait_ge(g_drained[k], own_writes_before_l1 // 2)
                    normalise_tokens(ph, 0)
                    for n in range(2 * H1):
                        s = n % 2
                        dve.wait_ge(pre_turned, n + 1)
                        if n >= 2:
                            dve.wait_ge(pre_full, n - 1)
                        dve.tensor_copy(Pr[:, 2 * s + 1, 0:2 * DC], psO[s][:, 0:2 * DC]).then_inc(pre_k, 1)
                        if n >= 1:
                            low_product(n - 1)
                    low_product(2 * H1 - 1)
                    dve.memset(cB[0:DB, :, 1, :], 0.0).then_inc(k_zeroed, 1)
                    dve.memset(cB[DB:P, :, 0, :], 0.0).then_inc(k_zeroed, 1)
                    turn_x(ph, 0, (uses_before(ph, 0) - 4, 0))
                    turn_c(ph, 0, (uses_before(ph, 0) - 2, 0))
                if ph == L1PH + 1:
                    for c in range(A_CHUNKS[ph]):
                        low_chunk(ph, c)
                    zero_k()
                groups(dve, bodies[KIND[ph]], ph)

        @block.tensor
        def _(pe):
            def three(ps, lh, ll, rh, rl, start, stop):
                pe.matmul(ps, lh, rh, start=start, stop=False)
                pe.matmul(ps, lh, rl, start=False, stop=False)
                return pe.matmul(ps, ll, rh, start=False, stop=stop)

            def bank_free(ph, g, k):
                pe.wait_ge(g_drained[k % 2], halves_before(ph, g) + k // 2)

            def turn_x(ph, g, first, free):
                r = 2 * (GROUPS * ph + g)
                for b in range(2):
                    k = first + b
                    free(k)
                    pe.wait_ge(z_ready, r + b + 1)
                    for c in range(2):
                        ins = pe.transpose(psG[k % 2][:, c * P:(c + 1) * P], Z[:, b, c * P:(c + 1) * P], ident[:, :])
                    ins.then_inc(g_full, 1)

            def turn_c(ph, g, first, free):
                pe.wait_ge(context_loaded, 32 * (context_preps_before(ph, g) + 1))
                for b in range(2):
                    k = first + b
                    free(k)
                    for c in range(2):
                        ins = pe.transpose(psG[k % 2][:, c * P:(c + 1) * P], cRaw[:, b, c * P:(c + 1) * P], ident[:, :])
                    ins.then_inc(g_full, 1)

            def turn_probabilities(ph, g, i):
                qb = quads_before(ph, g)
                pe.wait_ge(p_ready, qb + i + 1)
                if i >= 1:
                    pe.wait_ge(pt_ready, qb + i)
                for h in range(4):
                    ins = pe.transpose(psT[:, h * P:(h + 1) * P], Pr[:, i % 4, h * P:(h + 1) * P], ident[:, :])
                ins.then_inc(t_full, 1)

            def attention(ph, g, last):
                nxt, ub, hb = following(ph, g, last), uses_before(ph, g), halves_before(ph, g)
                qb, ob = quads_before(ph, g), o_before(ph, g)
                cross = KIND[ph] == CROSS

                def free(k):
                    bank_free(ph, g, k)

                def project(c0, k, tiles):
                    context = cross and c0 > 0
                    free(k)
                    for f in tiles:
                        ps = psG[k % 2][:, (f % 2) * GT:(f % 2 + 1) * GT]
                        for c in range(2):
                            cols = slice((c0 + c) * CH + f * P, (c0 + c) * CH + (f + 1) * P)
                            if context and c == 1:
                                pe.matmul(ps, WAh[:, cols], cTh[:, 1, :], start=False, stop=False)
                                ins = pe.matmul(ps, WAh[:, cols], cTl[:, 1, :], start=False, stop=True)
                            else:
                                h, l = (cTh, cTl) if context else (hTh, hTl)
                                ins = three(ps, WAh[:, cols], WAl[:, cols], h[:, c, :], l[:, c, :], c == 0, c == 1)
                    ins.then_inc(g_full, 1)

                def values(k):
                    b, half = (k - 8) // 2, k % 2
                    ps, tok = psG[k % 2][:, :], slice(b * P, (b + 1) * P)
                    free(k)
                    h, l = (cTh, cTl) if cross else (hTh, hTl)
                    for c in range(2):
                        cols = slice((4 + c) * CH + half * 512, (4 + c) * CH + (half + 1) * 512)
                        if cross and c == 1:
                            pe.matmul(ps, h[:, 1, tok], WAh[:, cols], start=False, stop=False)
                            ins = pe.matmul(ps, l[:, 1, tok], WAh[:, cols], start=False, stop=True)
                        else:
                            ins = three(ps, h[:, c, tok], l[:, c, tok], WAh[:, cols], WAl[:, cols], c == 0, c == 1)
                    ins.then_inc(g_full, 1)

                def scores(i):
                    b, j = i // 4, i % 4
                    if i >= 3:
                        pe.wait_ge(exp_done, qb + i - 2)
                    for p in range(2):
                        f = 2 * j + p
                        ins = pe.matmul(psS[i % 3][:, p * GT:(p + 1) * GT], Q[:, f, b * P:(b + 1) * P],
                                        K[:, f, b, :, :].rearrange("p e n -> p (e n)"), start=True, stop=True)
                    ins.then_inc(s_full, 1)

                def weigh(i):
                    b, j, o = i // 4, i % 4, i // 2
                    pe.wait_ge(pt_ready, qb + i + 1)
                    if i % 2 == 0 and o >= 2:
                        pe.wait_ge(o_drained, ob + o - 1)
                    for h in range(4):
                        e, at = h % 2, (i % 2) * GT + (h // 2) * P
                        ins = pe.matmul(psO[o % 2][e * HD:(e + 1) * HD, at:at + P],
                                        V[:, b, (4 * j + h) * HD:(4 * j + h + 1) * HD], PT[:, i % 2, h * P:(h + 1) * P],
                                        start=True, stop=True)
                    ins.then_inc(pv_done, 1)

                def merge(b, k):
                    free(k)
                    pe.wait_ge(wb_split, wb_due(ph, B_CHUNKS[ph]))
                    pe.wait_ge(o_drained, ob + 2 * b + 2)
                    for f in range(PAIRS):
                        o = slice(b * CH + f * P, b * CH + (f + 1) * P)
                        w = slice(f * D, (f + 1) * D)
                        ins = three(psG[k % 2][:, 0:D], Oh[:, o], Ol[:, o], WBh[:, w], WBl[:, w], f == 0, f == PAIRS - 1)
                    ins.then_inc(g_full, 1)

                pe.wait_ge(g_drained[1], hb if ph == 0 else hb - 1)
                pe.wait_ge(wa_split, wa_due(ph, 2))
                for u in range(4):
                    project(0, u, (2 * u, 2 * u + 1))
                pe.wait_ge(wa_split, wa_due(ph, 4))
                for u in range(4):
                    project(2, 4 + u, (2 * u, 2 * u + 1))
                for k in (0, 1):
                    pe.wait_ge(g_drained[k], hb + 4)
                scores(0)
                scores(1)
                pe.wait_ge(wa_split, wa_due(ph, 6))
                for k in range(8, 12):
                    values(k)
                scores(2)
                for i in range(8):
                    turn_probabilities(ph, g, i)
                    if i + 3 < 8:
                        scores(i + 3)
                    if i == 1:
                        for k in (0, 1):
                            pe.wait_ge(g_drained[k], hb + 6)
                    if i >= 1:
                        weigh(i - 1)
                merge(0, 12)
                weigh(7)
                if nxt:
                    turn_x(*nxt, 13, free)
                    if KIND[nxt[0]] == CROSS:
                        turn_c(*nxt, 15, free)
                merge(1, 13 + prep_uses(nxt))

            def mlp(ph, g, last):
                nxt, hb = following(ph, g, last), halves_before(ph, g)

                def free(k):
                    bank_free(ph, g, k)

                pe.wait_ge(g_drained[1], hb - 1)
                pe.wait_ge(wa_split, wa_due(ph, 4))
                for m in range(8):
                    free(m)
                    for part in range(2):
                        for c in range(2):
                            at = (2 * c + part) * CH + m * P
                            ins = three(psG[m % 2][:, part * GT:(part + 1) * GT], WAh[:, at:at + P], WAl[:, at:at + P],
                                        hTh[:, c, :], hTl[:, c, :], c == 0, c == 1)
                    ins.then_inc(g_full, 1)
                if nxt:
                    turn_x(*nxt, 8, free)
                    if KIND[nxt[0]] == CROSS:
                        turn_c(*nxt, 10, free)
                pe.wait_ge(wb_split, wb_due(ph, B_CHUNKS[ph]))
                for b in range(2):
                    k = 8 + b + prep_uses(nxt)
                    free(k)
                    for m in range(8):
                        if b == 0:
                            pe.wait_ge(gl_done, gh_due(ph, g, m + 1))
                        o, w = slice(m * GT + b * P, m * GT + (b + 1) * P), slice(m * D, (m + 1) * D)
                        ins = three(psG[k % 2][:, 0:D], Oh[:, o], Ol[:, o], WBh[:, w], WBl[:, w], m == 0, m == 7)
                    ins.then_inc(g_full, 1)

            def reassociated(ph, g, last):
                nxt, hb = following(ph, g, last), halves_before(ph, g)
                qb, ob = quads_before(ph, g), o_before(ph, g)

                def free(k):
                    bank_free(ph, g, k)

                def scores(i):
                    b, j = i // 2, i % 2
                    tok = slice(b * P, (b + 1) * P)
                    if i == 3:
                        pe.wait_ge(mask_added, 4 * g + 1)
                    for p in range(2):
                        ps = psS[i % 3]
                        pe.matmul(ps[:, p * GT:(p + 1) * GT], TT[:, H1 + 2 * j + p, tok],
                                  cB[:, b, :, :].rearrange("p e n -> p (e n)"), start=True, stop=False, skip_group_check=True)
                        for e in range(2):
                            h = 2 * p + e
                            ins = pe.matmul(ps[:, h * P:(h + 1) * P], TT[:, 4 * j + h, tok], cA[:, tok],
                                            start=False, stop=True, skip_group_check=True)
                    ins.then_inc(s_full, 1)

                def weigh(i):
                    b = i // 2
                    pe.wait_ge(pt_ready, qb + i + 1)
                    if i >= 1:
                        pe.wait_ge(o_drained, ob + i)
                    pe.matmul(psO[0][:, :], cU[:, b, 0:P], PT[:, i % 2, :], start=True, stop=True)
                    pairs = PT[:, i % 2, :].rearrange("p (f e n) -> p f e n", f=2, e=2)
                    for e in range(2):
                        ins = pe.matmul(psO[1][e * DB:(e + 1) * DB, 0:GT], cU[:, b, P:DC], pairs[:, :, e, :],
                                        start=True, stop=True)
                    ins.then_inc(pv_done, 1)

                def merge(b, k):
                    free(k)
                    pe.wait_ge(o_drained, ob + 2 * b + 2)
                    for n in range(H1 + H1 // 2):
                        o, w = slice(n * P, (n + 1) * P), slice(2 * NA + n * D, 2 * NA + (n + 1) * D)
                        ins = three(psG[k % 2][:, 0:D], Oh[:, o], Ol[:, o], WAh[:, w], WAl[:, w], n == 0, n == 11)
                    ins.then_inc(g_full, 1)

                pe.wait_ge(g_drained[1], hb - 1)
                for u in range(6):
                    free(u)
                    for m in (2 * u, 2 * u + 1):
                        for c in range(2):
                            at = c * NA + m * P
                            ins = three(psG[u % 2][:, (m % 2) * GT:(m % 2 + 1) * GT], WAh[:, at:at + P], WAl[:, at:at + P],
                                        hTh[:, c, :], hTl[:, c, :], c == 0, c == 1)
                    ins.then_inc(g_full, 1)
                for k in (0, 1):
                    pe.wait_ge(g_drained[k], hb + 3)
                scores(0)
                scores(1)
                scores(2)
                turn_probabilities(ph, g, 0)
                scores(3)
                turn_probabilities(ph, g, 1)
                weigh(0)
                turn_probabilities(ph, g, 2)
                weigh(1)
                turn_probabilities(ph, g, 3)
                merge(0, 6)
                weigh(2)
                if nxt:
                    turn_x(*nxt, 7, free)
                weigh(3)
                if nxt:
                    turn_c(*nxt, 9, free)
                merge(1, 7 + prep_uses(nxt))

            def products_of_weights():
                def turn(n):
                    h, s = n % H1, n % 2
                    if 2 <= n < H1:
                        pe.wait_ge(pre_q, n - 1)
                    if n >= 2:
                        pe.wait_ge(pre_k, n - 1)
                    if n == H1:
                        pe.wait_ge(big_loaded, 48)
                    for d in range(2):
                        at = h * D1 + d * P
                        if n < H1:
                            for c in range(2):
                                pe.transpose(psS[s][:, d * D + c * P:d * D + (c + 1) * P], raw_q1[:, c, at:at + P], ident[:, :])
                        w = raw_k1 if n < H1 else raw_v1
                        pe.transpose(psO[s][:, d * DC:d * DC + P], w[:, 0, at:at + P], ident[:, :])
                        ins = pe.transpose(psO[s][:, d * DC + P:(d + 1) * DC], w[0:DB, 1, at:at + P], ident[0:DB, 0:DB])
                    ins.then_inc(pre_turned, 1)

                def product(n):
                    h, s, e = n % H1, n % 2, n % 2
                    q, w = Pr[:, 2 * s, :], Pr[:, 2 * s + 1, :]
                    if n < H1:
                        pe.wait_ge(pre_q, n + 1)
                    pe.wait_ge(pre_k, n + 1)
                    if n >= 2:
                        pe.wait_ge(pre_lo, n - 1)
                    if n < H1:
                        for c in range(2):
                            for d in range(2):
                                ins = pe.matmul(psG[s][:, c * DC:(c + 1) * DC], q[:, d * D + c * P:d * D + (c + 1) * P],
                                                w[:, d * DC:(d + 1) * DC], start=d == 0, stop=d == 1)
                    else:
                        for d in range(2):
                            pe.matmul(psG[s][:, 0:D], w[:, d * DC:d * DC + P], raw_o1[:, 2 * h + d, :],
                                      start=d == 0, stop=d == 1)
                        for d in range(2):
                            ins = pe.matmul(psG[s][e * DB:(e + 1) * DB, D:2 * D], w[:, d * DC + P:(d + 1) * DC],
                                            raw_o1[:, 2 * h + d, :], start=d == 0, stop=d == 1)
                    ins.then_inc(pre_full, 1)

                pe.wait_ge(raw_loaded, raw_due(L1PH))
                turn(0)
                for n in range(2 * H1):
                    if n + 1 < 2 * H1:
                        turn(n + 1)
                    product(n)

            bodies = {SELF: attention, CROSS: attention, FF: mlp, L1: reassociated}
            pe.wait_ge(ident_ready, 2)
            turn_x(0, 0, 0, lambda k: None)
            pe.wait_ge(g_drained[1], 1)
            for ph in range(len(KIND)):
                if KIND[ph] == L1:
                    first = (uses_before(ph, 0) - PREP_USES[ph]) // 2
                    for k in (0, 1):
                        pe.wait_ge(g_drained[k], first)
                    products_of_weights()
                    pe.wait_ge(pre_lo, 2 * H1)
                    turn_x(ph, 0, 0, lambda k: None)
                    turn_c(ph, 0, 2, lambda k: pe.wait_ge(g_drained[k % 2], first + 1))
                    pe.wait_ge(g_drained[1], first + 2)
                    pe.wait_ge(k_zeroed, 4)
                if ph in (0, L1PH + 1):
                    pe.wait_ge(k_zeroed, 2 if ph == 0 else 6)
                groups(pe, bodies[KIND[ph]], ph)


def kernel(**inputs):
    import numpy as np
    import concourse.bacc as bacc
    from concourse.bass_utils import run_bass_kernel_spmd

    laid_out = {name: inputs[name] for name in ["x", "ctx_768", "mask_BxS2_if1"] + [n for ws in WEIGHTS for n in ws]}
    pairs = [pair or ("L1_xattn_gamma", "L1_xattn_beta") for pair in NORMS]
    laid_out["norm_columns"] = np.stack([[inputs[n] for n in pair] for pair in pairs]).reshape(
        len(NORMS), 2, 2, P).transpose(3, 0, 1, 2)
    laid_out["hidden_bias_columns"] = np.stack([inputs[n] for n in HIDDEN_BIAS.values()]).reshape(
        2, 16, P).transpose(2, 0, 1)
    rows = BIASES[:L1PH] + ["L1_xattn_gamma"] + BIASES[L1PH + 1:] + ["L1_xattn_beta"]
    laid_out["bias_rows"] = np.stack([inputs[n] for n in rows])

    nc = bacc.Bacc("TRN2", target_bir_lowering=False, num_devices=1)
    arrays, tensors = {}, {}
    for name, a in laid_out.items():
        arrays[f"in_{name}"] = a = np.ascontiguousarray(a)
        tensors[name] = nc.dram_tensor(f"in_{name}", a.shape, mybir.dt.from_np(a.dtype), kind="ExternalInput").ap()
    out = nc.dram_tensor("out_x", (B, P, D), F32, kind="ExternalOutput").ap()
    build(nc, tensors, out)
    result = run_bass_kernel_spmd(nc, [arrays], core_ids=[0])
    return result.results[0]["out_x"]
```

```python
from contextlib import ExitStack

import concourse.bass as bass
from concourse import mybir

ALU = mybir.AluOpType
ACT = mybir.ActivationFunctionType
F32 = mybir.dt.float32
F32R = mybir.dt.float32r
I32 = mybir.dt.int32
AX_X = mybir.AxisListType.X

P = 128
B = 16
D = 256
DC = 192
DB = DC - P
INNER = 1024
HD = 64
PAIRS = INNER // P
HID = 1024
H1 = 8
D1 = 256
GROUPS = B // 2
GT = 2 * P
EPS = 1e-5
MAGIC = float(0x5F3759DF)
NEG = -1e30
CH = 1024

SELF, CROSS, FF, L1 = "self", "cross", "ff", "l1"
KIND = [SELF, CROSS, FF, L1, CROSS, SELF, CROSS, FF]
LAST = len(KIND) - 1
L1PH = KIND.index(L1)
WEIGHTS = [
    ("L0_xattn_a1_Wq", "L0_xattn_a1_Wk", "L0_xattn_a1_Wv", "L0_xattn_a1_Wo"),
    ("L0_xattn_a2_Wq", "L0_xattn_a2_Wk", "L0_xattn_a2_Wv", "L0_xattn_a2_Wo"),
    ("L0_xattn_ff_Wp", "L0_xattn_ff_Wo"),
    ("L1_xattn_Wq", "L1_xattn_Wk", "L1_xattn_Wv", "L1_xattn_Wo"),
    ("L2_xattn_Wq", "L2_xattn_Wk", "L2_xattn_Wv", "L2_xattn_Wo"),
    ("L3_xattn_Wq1", "L3_xattn_Wk1", "L3_xattn_Wv1", "L3_xattn_Wo1"),
    ("L3_xattn_Wq2", "L3_xattn_Wk2", "L3_xattn_Wv2", "L3_xattn_Wo2"),
    ("L3_xattn_Wp", "L3_xattn_W2"),
]
NORMS = [("L0_xattn_ln1_g", "L0_xattn_ln1_b"), ("L0_xattn_ln2_g", "L0_xattn_ln2_b"),
         ("L0_xattn_ln3_g", "L0_xattn_ln3_b"), None, ("L2_xattn_gamma", "L2_xattn_beta"),
         ("L3_xattn_g1", "L3_xattn_be1"), ("L3_xattn_g2", "L3_xattn_be2"),
         ("L3_xattn_g3", "L3_xattn_be3")]
BIASES = ["L0_xattn_a1_bo", "L0_xattn_a2_bo", "L0_xattn_ff_bo", None, "L2_xattn_bo",
          "L3_xattn_bo1", "L3_xattn_bo2", "L3_xattn_b2"]
HIDDEN_BIAS = {2: "L0_xattn_ff_bp", 7: "L3_xattn_bp"}
Q_SCALE = [HD ** -0.5, HD ** -0.5, None, None, 1.0, HD ** -0.5, HD ** -0.5, None]
V_SCALE = [1.0, 1.0, None, None, HD ** -0.5, 1.0, 1.0, None]

QUADS = [{SELF: 8, CROSS: 8, FF: 0, L1: 4}[k] for k in KIND]
O_USES = [{SELF: 4, CROSS: 4, FF: 0, L1: 4}[k] for k in KIND]
PREP_USES = {SELF: 2, CROSS: 4, FF: 2, L1: 4}
A_CHUNKS = [{SELF: 6, CROSS: 6, FF: 4, L1: 0}[k] for k in KIND]
B_CHUNKS = [{SELF: 2, CROSS: 2, FF: 2, L1: 0}[k] for k in KIND]


def before(counts, ph):
    return sum(counts[:ph])


def attends(ph):
    return ph <= LAST and KIND[ph] in (SELF, CROSS)


LOOP = 2


def later(ph, g, left, n):
    return (ph, g + n) if left >= n else (ph + 1, n - left - 1)


def projected(ph, g, left):
    after = later(ph, g, left, 1)
    return after if attends(ph) and attends(after[0]) else None


def prepared(ph, g, left):
    if attends(ph):
        after = later(ph, g, left, 2)
        return after if attends(after[0]) or left == 1 else None
    after = later(ph, g, left, 1)
    return None if after[0] in (L1PH, LAST + 1) and left == 0 else after


def prep_uses(group):
    return PREP_USES[KIND[group[0]]] if group else 0


def body_uses(ph, left):
    main = {SELF: 2, CROSS: 2, FF: 2, L1: 8}[KIND[ph]]
    return main + 12 * bool(projected(ph, 0, left)) + prep_uses(prepared(ph, 0, left))


def opening_uses(ph):
    if attends(ph) and not (ph and attends(ph - 1)):
        return 12 + PREP_USES[KIND[ph]] + (PREP_USES[KIND[ph]] if ph == 0 else 0)
    return PREP_USES[L1] if KIND[ph] == L1 else 0


G_BASE = []
_n = 0
for _p in range(LAST + 1):
    G_BASE.append(_n + opening_uses(_p))
    _n = G_BASE[-1] + (GROUPS - 2) * body_uses(_p, LOOP) + body_uses(_p, 1) + body_uses(_p, 0)
G_BASE.append(_n)
assert all(n % 2 == 0 for n in G_BASE)


def uses_before(ph, g):
    if isinstance(g, int) and g == GROUPS - 1:
        return G_BASE[ph] + (GROUPS - 2) * body_uses(ph, LOOP) + body_uses(ph, 1)
    return G_BASE[ph] + g * body_uses(ph, LOOP)


def halves_before(ph, g):
    if isinstance(g, int):
        return uses_before(ph, g) // 2
    return G_BASE[ph] // 2 + g * (body_uses(ph, LOOP) // 2)


def halves_behind(ph, g):
    return G_BASE[ph + 1] // 2 if isinstance(g, int) and g == GROUPS - 1 else halves_before(ph, g + 1)


def quads_before(ph, g):
    return GROUPS * before(QUADS, ph) + g * QUADS[ph]


def o_before(ph, g):
    return GROUPS * before(O_USES, ph) + g * O_USES[ph]


def context_preps_before(ph, g):
    return GROUPS * sum(k in (CROSS, L1) for k in KIND[:ph]) + g


def norms_before(ph, g):
    return GROUPS * sum(k != L1 for k in KIND[:ph]) + g


def build(nc, t, out):
    with ExitStack() as ctx:
        def sb(name, shape, dt=F32):
            return ctx.enter_context(nc.sbuf_tensor(name, shape, dt))

        def sem(name):
            return ctx.enter_context(nc.semaphore(name))

        X = sb("X", [P, B, D])
        XB = sb("XB", [P, 2, D])
        WAh, WAl = sb("WAh", [P, 6 * CH], F32R), sb("WAl", [P, 6 * CH], F32R)
        WBh, WBl = sb("WBh", [P, 2 * CH], F32R), sb("WBl", [P, 2 * CH], F32R)
        raw = sb("raw", [P, 8 * CH])
        big = sb("big", [P, 8 * CH])
        Oh, Ol = sb("Oh", [P, 2 * CH], F32R), sb("Ol", [P, 2 * CH], F32R)
        hTh, hTl = sb("hTh", [P, 2, GT], F32R), sb("hTl", [P, 2, GT], F32R)
        hTf = sb("hTf", [P, 2, GT])
        cRaw = sb("cRaw", [P, 2, 2 * P])
        cTh, cTl = sb("cTh", [P, 2, GT], F32R), sb("cTl", [P, 2, GT], F32R)
        Z = sb("Z", [P, 2, D])
        Pr = sb("Pr", [P, 4, 4 * P])
        PT = sb("PT", [P, 2, 4 * P])
        ident = sb("ident", [P, P])
        bo_rows = sb("bo_rows", [P, 9, D])
        norm_cols = sb("norm_cols", [P, len(NORMS), 2, 2])
        hid_cols = sb("hid_cols", [P, 2, 16])
        negmax = sb("negmax", [P, 4, 4])
        esum = sb("esum", [P, 4, 4])
        rsum = sb("rsum", [P, 4, 4])
        stats, means, ve = sb("stats", [P, 2, 6]), sb("means", [P, 2]), sb("ve", [P, 2])
        sa, sc, rstd = sb("sa", [P, 3, 2]), sb("sc", [P, 2, 2]), sb("rstd", [P, 4, 2])
        pstats, pmeans, pve = sb("pstats", [P, 1, 6]), sb("pmeans", [P, 1]), sb("pve", [P, 1])
        psa, psc, prstd = sb("psa", [P, 3, 1]), sb("psc", [P, 2, 1]), sb("prstd", [P, 4, 1])

        Q = big[:, 0:2 * CH].rearrange("p (f n) -> p f n", f=PAIRS)
        K = big[:, 2 * CH:6 * CH].rearrange("p (f b e n) -> p f b e n", f=PAIRS, b=2, e=2)
        V = big[:, 6 * CH:8 * CH].rearrange("p (b n) -> p b n", b=2)
        GE, Uf = Pr[:, :, 0:GT], Pr[:, :, GT:2 * GT]
        TT = big[:, 0:12 * GT].rearrange("p (m n) -> p m n", m=12)
        Sm = big[:, 12 * GT:16 * GT].rearrange("p (s h n) -> p s h n", s=2, h=4)
        cA = big[:, 16 * GT:17 * GT]
        cB = big[:, 17 * GT:19 * GT].rearrange("p (b e n) -> p b e n", b=2, e=2)
        cU = big[:, 19 * GT:21 * GT].rearrange("p (b n) -> p b n", b=2)
        maskb = big[:, 21 * GT:22 * GT].rearrange("p (b n) -> p b n", b=2)
        maski = big[:, 22 * GT:23 * GT].bitcast(I32)
        R1 = big[:, 23 * GT:24 * GT]
        R2 = big[:, 24 * GT:25 * GT]
        R3 = big[:, 25 * GT:26 * GT]
        raw_q1 = raw[:, 0:4 * CH].rearrange("p (c n) -> p c n", c=2)
        raw_k1 = raw[:, 4 * CH:8 * CH].rearrange("p (c n) -> p c n", c=2)
        raw_v1 = big[:, 0:4 * CH].rearrange("p (c n) -> p c n", c=2)
        raw_o1 = big[:, 4 * CH:8 * CH].rearrange("p (c n) -> p c n", c=16)
        NA = 12 * P

        psS = [ctx.enter_context(nc.psum_tensor(f"psS{i}", [P, 512], F32)) for i in range(3)]
        psT = ctx.enter_context(nc.psum_tensor("psT", [P, 512], F32))
        psO = [ctx.enter_context(nc.psum_tensor(f"psO{i}", [P, 512], F32)) for i in range(2)]
        psG = [ctx.enter_context(nc.psum_tensor(f"psG{i}", [P, 512], F32)) for i in range(2)]

        hidden_ps = psS + [psT]

        x_loaded = sem("x_loaded")
        params_loaded = sem("params_loaded")
        raw_loaded = sem("raw_loaded")
        big_loaded = sem("big_loaded")
        context_loaded = sem("context_loaded")
        mask_loaded = sem("mask_loaded")
        stored = sem("stored")
        ident_ready = sem("ident_ready")
        k_zeroed = sem("k_zeroed")
        wa_rounded, wa_split = sem("wa_rounded"), sem("wa_split")
        wb_rounded, wb_split = sem("wb_rounded"), sem("wb_split")
        g_full = sem("g_full")
        g_drained = [sem("g_drained0"), sem("g_drained1")]
        ln_step = sem("ln_step")
        z_ready = sem("z_ready")
        x_turned = sem("x_turned")
        c_turned = sem("c_turned")
        cu_copied = sem("cu_copied")
        turn_step = sem("turn_step")
        s_full = sem("s_full")
        max_ready = sem("max_ready")
        mask_added = sem("mask_added")
        mask_ready = sem("mask_ready")
        exp_done = sem("exp_done")
        rsum_ready = sem("rsum_ready")
        p_ready = sem("p_ready")
        t_full = sem("t_full")
        pt_ready = sem("pt_ready")
        pv_done = sem("pv_done")
        o_rounded, o_drained = sem("o_rounded"), sem("o_drained")
        xb_ready = sem("xb_ready")
        hidden_full = sem("hidden_full")
        gelu_done = sem("gelu_done")
        hidden_done = sem("hidden_done")
        gh_done, gl_done = sem("gh_done"), sem("gl_done")
        post_step = sem("post_step")
        post_done = sem("post_done")
        pre_turned, pre_q, pre_k = sem("pre_turned"), sem("pre_q"), sem("pre_k")
        pre_full, pre_hi, pre_lo = sem("pre_full"), sem("pre_hi"), sem("pre_lo")

        MOMENT_STEPS = 9 + 9
        LN_STEPS = 2 + MOMENT_STEPS
        POST_STEPS = 1 + MOMENT_STEPS + 2

        def rows_of(ph):
            w = [t[n] for n in WEIGHTS[ph]]
            if KIND[ph] == FF:
                yield raw[:, 0:4 * CH].rearrange("p (c n) -> p c n", c=2), w[0].rearrange("(c p) n -> p c n", p=P)
                yield raw[:, 6 * CH:8 * CH].rearrange("p (c n) -> p c n", c=8), w[1].rearrange("(c p) n -> p c n", p=P)
                return
            if KIND[ph] == L1:
                yield raw_q1, w[0].rearrange("(c p) n -> p c n", p=P)
                yield raw_k1[:, 0, :], w[1][0:P, :]
                yield raw_k1[0:DB, 1, :], w[1][P:DC, :]
                return
            yield raw[:, 0:2 * CH].rearrange("p (c n) -> p c n", c=2), w[0].rearrange("(c p) n -> p c n", p=P)
            for n in (1, 2):
                to = raw[:, 2 * n * CH:(2 * n + 2) * CH].rearrange("p (c n) -> p c n", c=2)
                if KIND[ph] == SELF:
                    yield to, w[n].rearrange("(c p) n -> p c n", p=P)
                else:
                    yield to[:, 0, :], w[n][0:P, :]
                    yield to[0:DB, 1, :], w[n][P:DC, :]
                    yield to[DB:P, 1, :], w[n][P:DC, :]
            yield raw[:, 6 * CH:8 * CH].rearrange("p (c n) -> p c n", c=8), w[3].rearrange("(c p) n -> p c n", p=P)

        RAW_DMAS = [{SELF: 4, CROSS: 8, FF: 2, L1: 3}[k] for k in KIND]

        def raw_due(ph):
            return 16 * before(RAW_DMAS, ph + 1)

        def wa_due(ph, chunks):
            return before(A_CHUNKS, ph) + chunks

        def wb_due(ph, chunks):
            return before(B_CHUNKS, ph) + chunks

        def stacked(ph, c):
            return KIND[ph] == CROSS and c in (3, 5)

        x_rest_loaded = sem("x_rest_loaded")

        PARAMS = 3

        def gh_due(ph, g, tiles):
            return GROUPS * 8 * sum(k == FF for k in KIND[:ph]) + 8 * g + tiles

        def o_parts(O, o):
            return O[:, :].rearrange("p (b n) -> p b n", b=2)[:, :, o * GT:(o + 1) * GT]

        def product_parts(W, n):
            h, e = n % H1, n % 2
            ps = psG[n % 2]
            if n < H1:
                to = W[:, 0:2 * NA].rearrange("p (c n) -> p c n", c=2)
                of = ps[:, 0:2 * DC].rearrange("p (c n) -> p c n", c=2)
                return [(to[:, :, h * P:(h + 1) * P], of[:, :, 0:P]),
                        (to[:, :, CH + h * DB:CH + (h + 1) * DB], of[:, :, P:DC])]
            rows, at = slice(e * DB, (e + 1) * DB), 2 * NA + H1 * D + (h // 2) * D
            return [(W[:, 2 * NA + h * D:2 * NA + (h + 1) * D], ps[:, 0:D]),
                    (W[rows, at:at + D], ps[rows, D:2 * D])]

        block = ctx.enter_context(nc.Block())

        def chunk(c):
            return slice(c * CH, (c + 1) * CH)

        def groups(eng, body, ph):
            with eng.Fori(0, GROUPS - 2) as g:
                body(ph, g, LOOP)
            body(ph, GROUPS - 2, 1)
            body(ph, GROUPS - 1, 0)


        @block.sync
        def _(sp):
            def load_weights(ph):
                for to, src in rows_of(ph):
                    sp.dma_start(to, src).then_inc(raw_loaded, 16)

            def load_context(ph, g):
                n = context_preps_before(ph, g)
                if ph > 1 or not isinstance(g, int) or g > 0:
                    sp.wait_ge(c_turned, 2 * n)
                if ph == L1PH and not (isinstance(g, int) and g == 0):
                    sp.wait_ge(cu_copied, g)
                if ph == L1PH + 1 and isinstance(g, int) and g == 0:
                    sp.wait_ge(cu_copied, GROUPS)
                src = t["ctx_768"][bass.ds(2 * g, 2), :, :].rearrange("b p n -> p b n")
                sp.dma_start(cRaw[:, :, 0:DC], src).then_inc(context_loaded, 16)
                sp.dma_start(cRaw[:, :, DC:2 * P], src[:, :, P:DC]).then_inc(context_loaded, 16)

            def load_mask(g):
                rows = t["mask_BxS2_if1"][bass.ds(2 * g, 2), :].rearrange("b n -> (b n)")
                sp.dma_start(maski, rows.partition_broadcast(P)).then_inc(mask_loaded, 16)

            def body(ph, g, left):
                if KIND[ph] == L1 and left:
                    sp.wait_ge(mask_ready, g + 1)
                    load_mask(g + 1)
                nxt = prepared(ph, g, left)
                if nxt and KIND[nxt[0]] in (CROSS, L1):
                    load_context(*nxt)
                if ph == LAST:
                    for k in (0, 1):
                        sp.wait_ge(g_drained[k], halves_behind(ph, g))
                    sp.dma_start(out[bass.ds(2 * g, 2), :, :].rearrange("b p n -> p b n"),
                                 X[:, bass.ds(2 * g, 2), :]).then_inc(stored, 16)

            xs = t["x"].rearrange("b p n -> p b n")
            sp.dma_start(X[:, 0:2, :], xs[:, 0:2, :]).then_inc(x_loaded, 16)
            load_weights(0)
            sp.dma_start(X[:, 2:B, :], xs[:, 2:B, :]).then_inc(x_rest_loaded, 16)
            for ph in range(len(KIND)):
                if ph < LAST and ph + 1 != L1PH + 1:
                    if KIND[ph] != L1:
                        sp.wait_ge(wa_split, wa_due(ph, A_CHUNKS[ph]))
                        sp.wait_ge(wb_split, wb_due(ph, B_CHUNKS[ph]))
                    load_weights(ph + 1)
                if ph + 1 == L1PH:
                    sp.wait_ge(g_full, uses_before(ph, 0))
                    sp.dma_start(raw_v1[:, 0, :], t["L1_xattn_Wv"][0:P, :]).then_inc(big_loaded, 16)
                    sp.dma_start(raw_v1[0:DB, 1, :], t["L1_xattn_Wv"][P:DC, :]).then_inc(big_loaded, 16)
                    sp.dma_start(raw_o1, t["L1_xattn_Wo"].rearrange("(c p) n -> p c n", p=P)).then_inc(big_loaded, 16)
                if attends(ph) and ph and not attends(ph - 1):
                    load_context(ph, 1)
                if ph == L1PH:
                    load_context(ph, 0)
                    sp.wait_ge(pre_turned, H1)
                    load_weights(ph + 1)
                    sp.wait_ge(pre_full, 2 * H1)
                    load_mask(0)
                groups(sp, body, ph)
            sp.wait_ge(stored, 16 * GROUPS)

        @block.gpsimd
        def _(pool):
            pool.memset(ident[:, :], 0.0).then_inc(ident_ready, 1)
            pool.wait_ge(ident_ready, 1)
            pool.affine_select(out=ident[:, :], in_=ident[:, :], compare_op=ALU.not_equal, fill=1.0, base=0,
                               pattern=[[-1, P]], channel_multiplier=1).then_inc(ident_ready, 1)
            def low_part(ph, c):
                pool.wait_ge(wa_rounded, wa_due(ph, c + 1))
                to, off = (WAh, WAl) if stacked(ph, c) else (WAl, WAh)
                pool.tensor_tensor(to[:, chunk(c)], raw[:, chunk(c)], off[:, chunk(c)].bitcast(F32),
                                   ALU.subtract).then_inc(wa_split, 1)

            def normalise(ph, g, i):
                qb = quads_before(ph, g)
                pool.wait_ge(rsum_ready, qb + i + 1)
                p4 = Pr[:, i % 4, :].rearrange("p (h n) -> p h n", h=4)
                pool.tensor_tensor(p4, p4, rsum[:, i % 4, :].unsqueeze(2).to_broadcast([P, 4, P]),
                                   ALU.mult).then_inc(p_ready, 1)

            def body(ph, g, left):
                if KIND[ph] != L1:
                    for k in (0, 1):
                        pool.wait_ge(g_drained[k], halves_before(ph, g))
                    if ph == L1PH + 1:
                        pool.wait_ge(post_done, B)
                    pool.tensor_tensor(XB[:, :, :], X[:, bass.ds(2 * g, 2), :],
                                       bo_rows[:, ph:ph + 1, :].to_broadcast([P, 2, D]), ALU.add).then_inc(xb_ready, 1)
                if KIND[ph] == FF:
                    for m in range(8):
                        pool.wait_ge(gh_done, gh_due(ph, g, m + 1))
                        pool.tensor_tensor(Ol[:, m * GT:(m + 1) * GT], Uf[:, m % 4, :],
                                           Oh[:, m * GT:(m + 1) * GT].bitcast(F32), ALU.subtract).then_inc(gl_done, 1)
                for i in range(QUADS[ph]):
                    normalise(ph, g, i)
                    if left == 0 and attends(ph) and i + 4 < A_CHUNKS[ph + 1]:
                        low_part(ph + 1, i + 4)
                if left == 1 and attends(ph):
                    for c in range(4):
                        low_part(ph + 1, c)

            pool.wait_ge(params_loaded, 16 * PARAMS)
            pool.wait_ge(x_loaded, 16)
            pool.wait_ge(x_rest_loaded, 16)
            for ph in range(len(KIND)):
                for c in range(B_CHUNKS[ph]):
                    pool.wait_ge(wb_rounded, wb_due(ph, c + 1))
                    pool.tensor_tensor(WBl[:, chunk(c)], raw[:, chunk(6 + c)], WBh[:, chunk(c)].bitcast(F32),
                                       ALU.subtract).then_inc(wb_split, 1)
                groups(pool, body, ph)

        @block.scalar
        def _(act):
            act.dma_start(norm_cols[:, :, :, :], t["norm_columns"]).then_inc(params_loaded, 16)
            act.dma_start(hid_cols[:, :, :], t["hidden_bias_columns"]).then_inc(params_loaded, 16)
            act.dma_start(bo_rows[:, :, :], t["bias_rows"].partition_broadcast(P)).then_inc(params_loaded, 16)

            def round_chunk(ph, c):
                if stacked(ph, c):
                    act.activation(WAl[0:DB, chunk(c)], raw[0:DB, chunk(c)], ACT.Copy, scale=0.0)
                    act.activation(WAl[DB:P, chunk(c)], raw[DB:P, chunk(c)], ACT.Copy).then_inc(wa_rounded, 1)
                else:
                    act.activation(WAh[:, chunk(c)], raw[:, chunk(c)], ACT.Copy).then_inc(wa_rounded, 1)

            def turn_x(ph, g, first):
                use, parity = first
                for b in range(2):
                    ps = psG[(parity + b) % 2]
                    act.wait_ge(g_full, use + b + 1)
                    if KIND[ph] == L1:
                        act.activation(hTh[:, :, b * P:(b + 1) * P], ps[:, 0:GT].rearrange("p (c n) -> p c n", c=2),
                                       ACT.Copy).then_inc(x_turned, 1)
                        continue
                    for c in range(2):
                        ins = act.activation(hTh[:, c, b * P:(b + 1) * P], ps[:, c * P:(c + 1) * P], ACT.Identity,
                                             scale=norm_cols[:, ph, 0, c:c + 1], bias=norm_cols[:, ph, 1, c:c + 1])
                    ins.then_inc(x_turned, 1)

            def turn_c(ph, first):
                use, parity = first
                for b in range(2):
                    ps = psG[(parity + b) % 2]
                    act.wait_ge(g_full, use + b + 1)
                    if KIND[ph] == L1:
                        act.activation(cA[:, b * P:(b + 1) * P], ps[:, 0:P], ACT.Copy).then_inc(c_turned, 1)
                    else:
                        act.activation(cTh[:, :, b * P:(b + 1) * P], ps[:, 0:GT].rearrange("p (c n) -> p c n", c=2),
                                       ACT.Copy).then_inc(c_turned, 1)

            def exps(ph, g, i, scores):
                qb = quads_before(ph, g)
                act.wait_ge(max_ready, qb + i + 1)
                for h in range(4):
                    ins = act.activation(Pr[:, i % 4, h * P:(h + 1) * P], scores[:, h * P:(h + 1) * P], ACT.Exp,
                                         bias=negmax[:, i % 4, h:h + 1], accum_out=esum[:, i % 4, h:h + 1])
                ins.then_inc(exp_done, 1)

            def round_o(ph, g, o):
                act.wait_ge(pv_done, quads_before(ph, g) + 2 * o + 2)
                act.activation(o_parts(Oh, o), psO[o % 2][:, :].rearrange("p (b n) -> p b n", b=2),
                               ACT.Copy).then_inc(o_rounded, 1)

            def drain_q(ph, u, use):
                act.wait_ge(g_full, use + 1)
                act.activation(Q[:, 2 * u:2 * u + 2, :], psG[0][:, :].rearrange("p (f n) -> p f n", f=2),
                               ACT.Copy, scale=Q_SCALE[ph]).then_inc(g_drained[0], 1)

            def drain_k(u, use):
                act.wait_ge(g_full, use + 1)
                for e in range(2):
                    rows = slice(e * HD, (e + 1) * HD)
                    ins = act.activation(K[rows, 2 * u:2 * u + 2, :, e, :],
                                         psG[1][rows, :].rearrange("p (f b n) -> p f b n", f=2, b=2), ACT.Copy)
                ins.then_inc(g_drained[1], 1)

            def drain_v(ph, half, use):
                act.wait_ge(g_full, use + 1)
                act.activation(V[:, 1, half * 512:(half + 1) * 512], psG[1][:, :], ACT.Copy,
                               scale=V_SCALE[ph]).then_inc(g_drained[1], 1)

            def project(ph, first):
                for u in range(4):
                    drain_q(ph, u, first + 2 * u)
                    if u % 2:
                        drain_k(u, first + 2 * u + 1)
                drain_v(ph, 0, first + 9)
                drain_v(ph, 1, first + 11)

            def attention(ph, g, left):
                ub, proj, nxt = uses_before(ph, g), projected(ph, g, left), prepared(ph, g, left)
                p0 = 12 if proj else 0
                exps(ph, g, 0, psS[0])
                exps(ph, g, 1, psS[1])
                if proj:
                    drain_q(proj[0], 0, ub)
                for i in range(8):
                    if i + 2 < 8:
                        exps(ph, g, i + 2, psS[(i + 2) % 3])
                    if proj and i in (1, 3, 5):
                        drain_q(proj[0], (i + 1) // 2, ub + i + 1)
                    if proj and i in (2, 6):
                        drain_k(i // 2 if i == 6 else 1, ub + i + 1)
                    if i in (2, 4, 6):
                        round_o(ph, g, i // 2 - 1)
                    if proj and i == 7:
                        drain_v(proj[0], 0, ub + 9)
                    if left == 0 and i + 4 < A_CHUNKS[ph + 1]:
                        if i == 0:
                            act.wait_ge(g_full, uses_before(ph, g))
                        round_chunk(ph + 1, i + 4)
                    if left == 1 and i >= 6:
                        if i == 6:
                            act.wait_ge(raw_loaded, raw_due(ph + 1))
                            act.wait_ge(g_full, ub + 8)
                        round_chunk(ph + 1, i - 6)
                round_o(ph, g, 3)
                if proj:
                    drain_v(proj[0], 1, ub + 11)
                if nxt:
                    turn_x(*nxt, (ub + p0, 0))
                    if KIND[nxt[0]] == CROSS:
                        turn_c(nxt[0], (ub + p0 + 2, 0))
                if left == 1:
                    round_chunk(ph + 1, 2)
                    round_chunk(ph + 1, 3)

            def mlp(ph, g, left):
                nxt, ub = prepared(ph, g, left), uses_before(ph, g)
                bias = hid_cols[:, list(HIDDEN_BIAS).index(ph), :]

                def gate(m):
                    act.wait_ge(hidden_full, gh_due(ph, g, m + 1))
                    if m >= 4:
                        act.wait_ge(hidden_done, gh_due(ph, g, m - 3))
                    act.activation(GE[:, m % 4, :], hidden_ps[m % 4][:, GT:2 * GT], ACT.Gelu,
                                   bias=bias[:, 8 + m:9 + m]).then_inc(gelu_done, 1)

                def round_hidden(m):
                    act.wait_ge(hidden_done, gh_due(ph, g, m + 1))
                    act.activation(Oh[:, m * GT:(m + 1) * GT], Uf[:, m % 4, :], ACT.Copy).then_inc(gh_done, 1)

                gate(0)
                for m in range(1, 8):
                    gate(m)
                    round_hidden(m - 1)
                round_hidden(7)
                if nxt:
                    turn_x(*nxt, (ub, 0))

            def reassociated(ph, g, left):
                nxt, ub, qb = prepared(ph, g, left), uses_before(ph, g), quads_before(ph, g)

                def round_u(i):
                    act.wait_ge(pv_done, qb + i + 1)
                    if i == 2:
                        act.wait_ge(g_full, ub + 7)
                    j = i % 2
                    act.activation(Oh[:, j * 512:(j + 1) * 512], psO[0][:, :], ACT.Copy)
                    act.activation(Oh[:, CH + j * GT:CH + (j + 1) * GT], psO[1][:, 0:GT], ACT.Copy).then_inc(o_rounded, 1)

                for u in (1, 3, 5):
                    act.wait_ge(g_full, ub + u + 1)
                    act.activation(TT[:, 2 * u:2 * u + 2, :], psG[1][:, :].rearrange("p (m n) -> p m n", m=2),
                                   ACT.Copy, scale=D1 ** -0.5).then_inc(g_drained[1], 1)
                for i in range(4):
                    exps(ph, g, i, Sm[:, i % 2, :, :].rearrange("p h n -> p (h n)"))
                for i in range(3):
                    round_u(i)
                if nxt:
                    turn_x(*nxt, (ub + 7, 1))
                round_u(3)
                if nxt:
                    turn_c(nxt[0], (ub + 9, 1))
                if left == 0:
                    act.wait_ge(g_full, G_BASE[ph + 1] - opening_uses(ph + 1))
                    act.wait_ge(raw_loaded, raw_due(ph + 1))
                    for c in range(A_CHUNKS[ph + 1]):
                        round_chunk(ph + 1, c)

            def round_product(n):
                h, e = n % H1, n % 2
                act.wait_ge(pre_full, n + 1)
                for to, of in product_parts(WAh, n):
                    ins = act.activation(to, of, ACT.Copy)
                ins.then_inc(pre_hi, 1)

            bodies = {SELF: attention, CROSS: attention, FF: mlp, L1: reassociated}
            act.wait_ge(raw_loaded, raw_due(0))
            for c in range(A_CHUNKS[0]):
                round_chunk(0, c)
                if c == 1:
                    act.wait_ge(params_loaded, 16 * PARAMS)
                    turn_x(0, 0, (0, 0))
            for ph in range(len(KIND)):
                if KIND[ph] == L1:
                    act.wait_ge(g_full, G_BASE[ph] - opening_uses(ph))
                    for n in range(2 * H1):
                        h, s = n % H1, n % 2
                        if n < H1:
                            act.wait_ge(pre_turned, n + 1)
                            if n >= 2:
                                act.wait_ge(pre_full, n - 1)
                            act.activation(Pr[:, 2 * s, :], psS[s][:, :], ACT.Copy).then_inc(pre_q, 1)
                        if n >= 1:
                            round_product(n - 1)
                    round_product(2 * H1 - 1)
                    turn_x(ph, 0, (G_BASE[ph] - 4, 0))
                    turn_c(ph, (G_BASE[ph] - 2, 0))
                for c in range(B_CHUNKS[ph]):
                    if c == 0:
                        act.wait_ge(raw_loaded, raw_due(ph))
                        if ph > 0:
                            act.wait_ge(g_full, G_BASE[ph] - opening_uses(ph))
                    act.activation(WBh[:, chunk(c)], raw[:, chunk(6 + c)], ACT.Copy).then_inc(wb_rounded, 1)
                if attends(ph) and opening_uses(ph):
                    prep = PREP_USES[KIND[ph]]
                    project(ph, G_BASE[ph] - prep - 12)
                    turn_x(ph, 1, (G_BASE[ph] - prep, 0))
                    if KIND[ph] == CROSS:
                        turn_c(ph, (G_BASE[ph] - 2, 0))
                groups(act, bodies[KIND[ph]], ph)

        @block.vector
        def _(dve):
            def moments_part(step, done, st, m, y, a, c, e, n):
                if n == 0:
                    dve.wait_ge(step, done)
                    dve.tensor_tensor(a[:, 0, :], st[:, :, 1], st[:, :, 4], ALU.add).then_inc(step, 1)
                    dve.tensor_tensor(a[:, 1, :], st[:, :, 1], st[:, :, 4], ALU.subtract).then_inc(step, 1)
                    dve.tensor_tensor(a[:, 2, :], st[:, :, 2], st[:, :, 5], ALU.add).then_inc(step, 1)
                elif n == 1:
                    dve.wait_ge(step, done + 3)
                    dve.tensor_scalar(m, a[:, 0, :], 0.5, None, ALU.mult).then_inc(step, 1)
                    dve.scalar_tensor_tensor(c[:, 0, :], a[:, 1, :], 0.25, a[:, 1, :], ALU.mult, ALU.mult).then_inc(step, 1)
                    dve.tensor_scalar(c[:, 1, :], a[:, 2, :], 1.0 / D, EPS, ALU.mult, ALU.add).then_inc(step, 1)
                elif n == 2:
                    dve.wait_ge(step, done + 6)
                    dve.tensor_tensor(e, c[:, 0, :], c[:, 1, :], ALU.add).then_inc(step, 1)
                elif n == 3:
                    dve.wait_ge(step, done + 7)
                    dve.tensor_scalar(a[:, 0, :].bitcast(I32), e.bitcast(I32), 1, None, ALU.logical_shift_right).then_inc(step, 1)
                elif n == 4:
                    dve.wait_ge(step, done + 8)
                    dve.tensor_scalar(y[:, 0, :].bitcast(I32), a[:, 0, :].bitcast(I32), -1.0, MAGIC, ALU.mult, ALU.add).then_inc(step, 1)
                else:
                    k, at = divmod(n - 5, 3)
                    dve.wait_ge(step, done + 4 + n)
                    if at == 0:
                        dve.tensor_tensor(a[:, 0, :], y[:, k, :], y[:, k, :], ALU.mult).then_inc(step, 1)
                    elif at == 1:
                        dve.scalar_tensor_tensor(c[:, 0, :], a[:, 0, :], -0.5, e, ALU.mult, ALU.mult).then_inc(step, 1)
                    else:
                        dve.scalar_tensor_tensor(y[:, k + 1, :], c[:, 0, :], 1.5, y[:, k, :], ALU.add, ALU.mult).then_inc(step, 1)

            NORM_PARTS = 16

            def norm_part(ph, g, n):
                done = LN_STEPS * norms_before(ph, g)
                if KIND[ph] == L1:
                    if n == 0:
                        for b in range(2):
                            dve.tensor_copy(Z[:, b:b + 1, :], X[:, bass.ds(2 * g + b, 1), :]).then_inc(z_ready, 1)
                elif n == 0:
                    for b in range(2):
                        dve.bn_stats(stats[:, b, :], X[:, bass.ds(2 * g + b, 1), :].rearrange("p b n -> p (b n)")).then_inc(ln_step, 1)
                elif n < NORM_PARTS - 1:
                    moments_part(ln_step, done + 2, stats, means[:, :], rstd, sa, sc, ve[:, :], n - 1)
                else:
                    dve.wait_ge(ln_step, done + LN_STEPS)
                    for b in range(2):
                        dve.tensor_scalar(Z[:, b:b + 1, :], X[:, bass.ds(2 * g + b, 1), :], means[:, b:b + 1], rstd[:, 3, b:b + 1],
                                          ALU.subtract, ALU.mult).then_inc(z_ready, 1)

            def normalise_tokens(ph, g):
                for n in range(NORM_PARTS):
                    norm_part(ph, g, n)

            def turn_x(ph, g, first):
                use, parity = first
                r, done = 2 * (GROUPS * ph + g), 4 * norms_before(ph, g)
                for b in range(2):
                    k = (parity + b) % 2
                    ps, cols = psG[k], slice(b * P, (b + 1) * P)
                    dve.wait_ge(g_full, use + b + 1)
                    dve.wait_ge(x_turned, r + b + 1)
                    if KIND[ph] == L1:
                        dve.tensor_tensor(hTl[:, :, cols], ps[:, 0:GT].rearrange("p (c n) -> p c n", c=2),
                                          hTh[:, :, cols].bitcast(F32), ALU.subtract).then_inc(g_drained[k], 1)
                        continue
                    for c in range(2):
                        dve.tensor_scalar(hTf[:, c, cols], ps[:, c * P:(c + 1) * P], norm_cols[:, ph, 0, c:c + 1],
                                          norm_cols[:, ph, 1, c:c + 1], ALU.mult, ALU.add).then_inc(turn_step, 1)
                    dve.wait_ge(turn_step, done + 2 * b + 2)
                    dve.tensor_tensor(hTl[:, :, cols], hTf[:, :, cols], hTh[:, :, cols].bitcast(F32),
                                      ALU.subtract).then_inc(g_drained[k], 1)

            def turn_c(ph, g, first):
                use, parity = first
                n = 2 * context_preps_before(ph, g)
                for b in range(2):
                    k = (parity + b) % 2
                    ps, cols = psG[k], slice(b * P, (b + 1) * P)
                    dve.wait_ge(g_full, use + b + 1)
                    dve.wait_ge(c_turned, n + b + 1)
                    if KIND[ph] == L1:
                        dve.tensor_copy(cB[0:DB, b, 0, :], ps[0:DB, P:2 * P])
                        dve.tensor_copy(cB[DB:P, b, 1, :], ps[DB:P, P:2 * P]).then_inc(g_drained[k], 1)
                    else:
                        dve.tensor_tensor(cTl[:, :, cols], ps[:, 0:GT].rearrange("p (c n) -> p c n", c=2),
                                          cTh[:, :, cols].bitcast(F32), ALU.subtract).then_inc(g_drained[k], 1)
                if KIND[ph] == L1:
                    dve.tensor_copy(cU[:, :, 0:DC], cRaw[:, :, 0:DC]).then_inc(cu_copied, 1)

            def maxima(ph, g, i, scores):
                dve.reduce_max(negmax[:, i % 4, :], scores, AX_X, negate=True).then_inc(max_ready, 1)

            def score_maxima(ph, g, i):
                dve.wait_ge(s_full, quads_before(ph, g) + i + 1)
                maxima(ph, g, i, psS[i % 3][:, :].rearrange("p (h n) -> p h n", h=4))

            def reciprocals(ph, g, i):
                dve.wait_ge(exp_done, quads_before(ph, g) + i + 1)
                dve.reciprocal(rsum[:, i % 4, :], esum[:, i % 4, :]).then_inc(rsum_ready, 1)

            def drain_turned(ph, g, i):
                dve.wait_ge(t_full, quads_before(ph, g) + i + 1)
                dve.tensor_copy(PT[:, i % 2, :], psT[:, :]).then_inc(pt_ready, 1)

            def low_o(ph, g, o):
                dve.wait_ge(o_rounded, o_before(ph, g) + o + 1)
                dve.tensor_tensor(o_parts(Ol, o), psO[o % 2][:, :].rearrange("p (b n) -> p b n", b=2),
                                  o_parts(Oh, o).bitcast(F32), ALU.subtract).then_inc(o_drained, 1)

            def residual(ph, g, b, use, k, banks=psG):
                dve.wait_ge(g_full, use + 1)
                dve.wait_ge(xb_ready, norms_before(ph, g) + 1)
                dve.tensor_tensor(X[:, bass.ds(2 * g + b, 1), :], banks[k][:, 0:D].unsqueeze(1), XB[:, b:b + 1, :],
                                  ALU.add).then_inc(g_drained[k], 1)

            def own_writes(ph, g):
                for k in (0, 1):
                    dve.wait_ge(g_drained[k], halves_before(ph, g))
                if ph == L1PH + 1:
                    dve.wait_ge(post_done, B)

            def drain_k(u, use):
                dve.wait_ge(g_full, use + 1)
                for e in range(2):
                    rows = slice(e * HD, (e + 1) * HD)
                    ins = dve.tensor_copy(K[rows, 2 * u:2 * u + 2, :, e, :],
                                          psG[1][rows, :].rearrange("p (f b n) -> p f b n", f=2, b=2))
                ins.then_inc(g_drained[1], 1)

            def drain_v(ph, half, use):
                dve.wait_ge(g_full, use + 1)
                dve.tensor_scalar(V[:, 0, half * 512:(half + 1) * 512], psG[0][:, :], V_SCALE[ph], None,
                                  ALU.mult).then_inc(g_drained[0], 1)

            def project(ph, first):
                drain_k(0, first + 1)
                drain_k(2, first + 5)
                drain_v(ph, 0, first + 8)
                drain_v(ph, 1, first + 10)

            def attention(ph, g, left):
                ub, proj, nxt = uses_before(ph, g), projected(ph, g, left), prepared(ph, g, left)
                p0 = 12 if proj else 0
                own_writes(ph, g)
                score_maxima(ph, g, 0)
                score_maxima(ph, g, 1)
                for i in range(8):
                    if i + 2 < 8:
                        score_maxima(ph, g, i + 2)
                    if i == 0:
                        reciprocals(ph, g, 0)
                    if i in (3, 5, 7):
                        low_o(ph, g, (i - 3) // 2)
                    if proj and i in (0, 4):
                        drain_k(i // 2, ub + i + 1)
                    drain_turned(ph, g, i)
                    if i + 1 < 8:
                        reciprocals(ph, g, i + 1)
                    if proj and i == 6:
                        drain_v(proj[0], 0, ub + 8)
                    if nxt:
                        norm_part(*nxt, 2 * i)
                        norm_part(*nxt, 2 * i + 1)
                low_o(ph, g, 3)
                if proj:
                    drain_v(proj[0], 1, ub + 10)
                if nxt:
                    turn_x(*nxt, (ub + p0, 0))
                    if KIND[nxt[0]] == CROSS:
                        turn_c(*nxt, (ub + p0 + 2, 0))
                for b in range(2):
                    residual(ph, g, b, ub + p0 + prep_uses(nxt) + b, b)

            def mlp(ph, g, left):
                nxt, ub = prepared(ph, g, left), uses_before(ph, g)
                bias = hid_cols[:, list(HIDDEN_BIAS).index(ph), :]
                own_writes(ph, g)
                for m in range(8):
                    dve.wait_ge(gelu_done, gh_due(ph, g, m + 1))
                    if m >= 4:
                        dve.wait_ge(gl_done, gh_due(ph, g, m - 3))
                    dve.scalar_tensor_tensor(Uf[:, m % 4, :], hidden_ps[m % 4][:, 0:GT], bias[:, m:m + 1], GE[:, m % 4, :],
                                             ALU.add, ALU.mult).then_inc(hidden_done, 1)
                    if nxt:
                        norm_part(*nxt, 2 * m)
                        norm_part(*nxt, 2 * m + 1)
                if nxt:
                    turn_x(*nxt, (ub, 0))
                for b in range(2):
                    residual(ph, g, b, ub + prep_uses(nxt) + b, b, psO)

            def reassociated(ph, g, left):
                nxt, ub, qb = prepared(ph, g, left), uses_before(ph, g), quads_before(ph, g)
                own_writes(ph, g)
                if nxt:
                    normalise_tokens(*nxt)
                dve.wait_ge(mask_loaded, 16 * g + 16)
                dve.tensor_scalar(maskb.rearrange("p b n -> p (b n)"), maski, 0, NEG, ALU.is_equal,
                                  ALU.mult).then_inc(mask_ready, 1)
                for u in (0, 2, 4):
                    dve.wait_ge(g_full, ub + u + 1)
                    dve.tensor_scalar(TT[:, 2 * u:2 * u + 2, :], psG[0][:, :].rearrange("p (m n) -> p m n", m=2),
                                      D1 ** -0.5, None, ALU.mult).then_inc(g_drained[0], 1)
                dve.wait_ge(mask_ready, g + 1)

                def masked(i):
                    dve.wait_ge(s_full, qb + i + 1)
                    if i >= 2:
                        dve.wait_ge(exp_done, qb + i - 1)
                    dve.tensor_tensor(Sm[:, i % 2, :, :], psS[i % 3][:, :].rearrange("p (h n) -> p h n", h=4),
                                      maskb[:, i // 2:i // 2 + 1, :].to_broadcast([P, 4, P]), ALU.add).then_inc(mask_added, 1)
                    dve.wait_ge(mask_added, 4 * g + i + 1)
                    maxima(ph, g, i, Sm[:, i % 2, :, :])

                def low_u(i):
                    dve.wait_ge(o_rounded, o_before(ph, g) + i + 1)
                    j = i % 2
                    for cols, of in ((slice(j * 512, (j + 1) * 512), psO[0][:, :]),
                                     (slice(CH + j * GT, CH + (j + 1) * GT), psO[1][:, 0:GT])):
                        ins = dve.tensor_tensor(Ol[:, cols], of, Oh[:, cols].bitcast(F32), ALU.subtract)
                    ins.then_inc(o_drained, 1)

                def post_norm(b, ub, offset, k):
                    done = POST_STEPS * (2 * g + b)
                    dve.wait_ge(g_full, ub + offset + 1)
                    dve.tensor_tensor(R1.unsqueeze(1), psG[k][:, 0:D].unsqueeze(1), X[:, bass.ds(2 * g + b, 1), :],
                                      ALU.add).then_inc(g_drained[k], 1)
                    dve.wait_ge(g_drained[k], halves_before(ph, g) + offset // 2 + 1)
                    dve.bn_stats(pstats[:, 0, :], R1).then_inc(post_step, 1)
                    for n in range(14):
                        moments_part(post_step, done + 1, pstats, pmeans[:, :], prstd, psa, psc, pve[:, :], n)
                    dve.wait_ge(post_step, done + 1 + MOMENT_STEPS)
                    dve.tensor_scalar(R2, R1, pmeans[:, :], prstd[:, 3, :], ALU.subtract, ALU.mult).then_inc(post_step, 1)
                    dve.wait_ge(post_step, done + 2 + MOMENT_STEPS)
                    dve.tensor_tensor(R3, R2, bo_rows[:, L1PH, :], ALU.mult).then_inc(post_step, 1)
                    dve.wait_ge(post_step, done + 3 + MOMENT_STEPS)
                    dve.tensor_tensor(X[:, bass.ds(2 * g + b, 1), :], R3.unsqueeze(1), bo_rows[:, 8:9, :],
                                      ALU.add).then_inc(post_done, 1)

                masked(0)
                masked(1)
                reciprocals(ph, g, 0)
                masked(2)
                reciprocals(ph, g, 1)
                drain_turned(ph, g, 0)
                masked(3)
                reciprocals(ph, g, 2)
                drain_turned(ph, g, 1)
                low_u(0)
                reciprocals(ph, g, 3)
                drain_turned(ph, g, 2)
                low_u(1)
                drain_turned(ph, g, 3)
                low_u(2)
                post_norm(0, ub, 6, 0)
                if nxt:
                    turn_x(*nxt, (ub + 7, 1))
                low_u(3)
                if nxt:
                    turn_c(*nxt, (ub + 9, 1))
                post_norm(1, ub, 7 + prep_uses(nxt), 1)

            def low_product(n):
                dve.wait_ge(pre_hi, n + 1)
                for (to, of), (hi, _) in zip(product_parts(WAl, n), product_parts(WAh, n)):
                    ins = dve.tensor_tensor(to, of, hi.bitcast(F32), ALU.subtract)
                ins.then_inc(pre_lo, 1)

            def low_chunk(ph, c):
                dve.wait_ge(wa_rounded, wa_due(ph, c + 1))
                to, off = (WAh, WAl) if stacked(ph, c) else (WAl, WAh)
                dve.tensor_tensor(to[:, chunk(c)], raw[:, chunk(c)], off[:, chunk(c)].bitcast(F32),
                                  ALU.subtract).then_inc(wa_split, 1)

            bodies = {SELF: attention, CROSS: attention, FF: mlp, L1: reassociated}

            def zero_k():
                dve.memset(K[0:HD, :, :, 1, :], 0.0).then_inc(k_zeroed, 1)
                dve.memset(K[HD:P, :, :, 0, :], 0.0).then_inc(k_zeroed, 1)

            zero_k()
            dve.wait_ge(x_loaded, 16)
            normalise_tokens(0, 0)
            for c in range(A_CHUNKS[0]):
                low_chunk(0, c)
                if c == 1:
                    turn_x(0, 0, (0, 0))
            dve.wait_ge(x_rest_loaded, 16)
            for ph in range(len(KIND)):
                if KIND[ph] == L1:
                    own_writes_before_l1 = G_BASE[ph] - opening_uses(ph)
                    for k in (0, 1):
                        dve.wait_ge(g_drained[k], own_writes_before_l1 // 2)
                    normalise_tokens(ph, 0)
                    for n in range(2 * H1):
                        s = n % 2
                        dve.wait_ge(pre_turned, n + 1)
                        if n >= 2:
                            dve.wait_ge(pre_full, n - 1)
                        dve.tensor_copy(Pr[:, 2 * s + 1, 0:2 * DC], psO[s][:, 0:2 * DC]).then_inc(pre_k, 1)
                        if n >= 1:
                            low_product(n - 1)
                    low_product(2 * H1 - 1)
                    dve.memset(cB[0:DB, :, 1, :], 0.0).then_inc(k_zeroed, 1)
                    dve.memset(cB[DB:P, :, 0, :], 0.0).then_inc(k_zeroed, 1)
                    turn_x(ph, 0, (G_BASE[ph] - 4, 0))
                    turn_c(ph, 0, (G_BASE[ph] - 2, 0))
                if ph == L1PH + 1:
                    for c in range(A_CHUNKS[ph]):
                        low_chunk(ph, c)
                    zero_k()
                if attends(ph) and opening_uses(ph):
                    prep = PREP_USES[KIND[ph]]
                    if ph:
                        dve.wait_ge(post_done, B)
                    project(ph, G_BASE[ph] - prep - 12)
                    normalise_tokens(ph, 1)
                    turn_x(ph, 1, (G_BASE[ph] - prep, 0))
                    if KIND[ph] == CROSS:
                        turn_c(ph, 1, (G_BASE[ph] - 2, 0))
                groups(dve, bodies[KIND[ph]], ph)

        @block.tensor
        def _(pe):
            def three(ps, lh, ll, rh, rl, start, stop):
                pe.matmul(ps, lh, rh, start=start, stop=False)
                pe.matmul(ps, lh, rl, start=False, stop=False)
                return pe.matmul(ps, ll, rh, start=False, stop=stop)

            def bank_free(ph, g, k):
                pe.wait_ge(g_drained[k % 2], halves_before(ph, g) + k // 2)

            def turn_x(ph, g, first, free):
                r = 2 * (GROUPS * ph + g)
                for b in range(2):
                    k = first + b
                    free(k)
                    pe.wait_ge(z_ready, r + b + 1)
                    for c in range(2):
                        ins = pe.transpose(psG[k % 2][:, c * P:(c + 1) * P], Z[:, b, c * P:(c + 1) * P], ident[:, :])
                    ins.then_inc(g_full, 1)

            def turn_c(ph, g, first, free):
                pe.wait_ge(context_loaded, 32 * (context_preps_before(ph, g) + 1))
                for b in range(2):
                    k = first + b
                    free(k)
                    for c in range(2):
                        ins = pe.transpose(psG[k % 2][:, c * P:(c + 1) * P], cRaw[:, b, c * P:(c + 1) * P], ident[:, :])
                    ins.then_inc(g_full, 1)

            def turn_probabilities(ph, g, i):
                qb = quads_before(ph, g)
                pe.wait_ge(p_ready, qb + i + 1)
                if i >= 1:
                    pe.wait_ge(pt_ready, qb + i)
                for h in range(4):
                    ins = pe.transpose(psT[:, h * P:(h + 1) * P], Pr[:, i % 4, h * P:(h + 1) * P], ident[:, :])
                ins.then_inc(t_full, 1)

            def project(ph, u, k, free):
                context = KIND[ph] == CROSS and k % 2 == 1
                c0 = 2 * (k % 2)
                pe.wait_ge(wa_split, wa_due(ph, c0 + 2))
                free(k)
                for f in (2 * u, 2 * u + 1):
                    ps = psG[k % 2][:, (f % 2) * GT:(f % 2 + 1) * GT]
                    for c in range(2):
                        cols = slice((c0 + c) * CH + f * P, (c0 + c) * CH + (f + 1) * P)
                        if context and c == 1:
                            pe.matmul(ps, WAh[:, cols], cTh[:, 1, :], start=False, stop=False)
                            ins = pe.matmul(ps, WAh[:, cols], cTl[:, 1, :], start=False, stop=True)
                        else:
                            h, l = (cTh, cTl) if context else (hTh, hTl)
                            ins = three(ps, WAh[:, cols], WAl[:, cols], h[:, c, :], l[:, c, :], c == 0, c == 1)
                ins.then_inc(g_full, 1)

            def values(ph, b, half, k, free):
                cross = KIND[ph] == CROSS
                ps, tok = psG[k % 2][:, :], slice(b * P, (b + 1) * P)
                pe.wait_ge(wa_split, wa_due(ph, 6))
                free(k)
                h, l = (cTh, cTl) if cross else (hTh, hTl)
                for c in range(2):
                    cols = slice((4 + c) * CH + half * 512, (4 + c) * CH + (half + 1) * 512)
                    if cross and c == 1:
                        pe.matmul(ps, h[:, 1, tok], WAh[:, cols], start=False, stop=False)
                        ins = pe.matmul(ps, l[:, 1, tok], WAh[:, cols], start=False, stop=True)
                    else:
                        ins = three(ps, h[:, c, tok], l[:, c, tok], WAh[:, cols], WAl[:, cols], c == 0, c == 1)
                ins.then_inc(g_full, 1)

            def attention(ph, g, left):
                proj, nxt = projected(ph, g, left), prepared(ph, g, left)
                hb, qb, ob = halves_before(ph, g), quads_before(ph, g), o_before(ph, g)
                p0 = 12 if proj else 0

                def free(k):
                    bank_free(ph, g, k)

                def scores(i):
                    b, j = i % 2, i // 2
                    if i >= 3:
                        pe.wait_ge(exp_done, qb + i - 2)
                    for p in range(2):
                        f = 2 * j + p
                        ins = pe.matmul(psS[i % 3][:, p * GT:(p + 1) * GT], Q[:, f, b * P:(b + 1) * P],
                                        K[:, f, b, :, :].rearrange("p e n -> p (e n)"), start=True, stop=True)
                    ins.then_inc(s_full, 1)

                def weigh(i):
                    b, j = i % 2, i // 2
                    pe.wait_ge(pt_ready, qb + i + 1)
                    if b == 0 and j >= 2:
                        pe.wait_ge(o_drained, ob + j - 1)
                    for h in range(4):
                        e, at = h % 2, b * GT + (h // 2) * P
                        ins = pe.matmul(psO[j % 2][e * HD:(e + 1) * HD, at:at + P],
                                        V[:, b, (4 * j + h) * HD:(4 * j + h + 1) * HD], PT[:, i % 2, h * P:(h + 1) * P],
                                        start=True, stop=True)
                    ins.then_inc(pv_done, 1)

                def merge(b, k):
                    free(k)
                    pe.wait_ge(wb_split, wb_due(ph, B_CHUNKS[ph]))
                    pe.wait_ge(o_drained, ob + 4)
                    for f in range(PAIRS):
                        o = slice(b * CH + f * P, b * CH + (f + 1) * P)
                        w = slice(f * D, (f + 1) * D)
                        ins = three(psG[k % 2][:, 0:D], Oh[:, o], Ol[:, o], WBh[:, w], WBl[:, w], f == 0, f == PAIRS - 1)
                    ins.then_inc(g_full, 1)

                scores(0)
                scores(1)
                if proj:
                    pe.wait_ge(g_drained[1], hb)
                    project(proj[0], 0, 0, free)
                for i in range(8):
                    if i + 2 < 8:
                        scores(i + 2)
                    if proj and i < 7:
                        project(proj[0], (i + 1) // 2, i + 1, free)
                    if proj and i == 6:
                        values(proj[0], 0, 0, 8, free)
                    turn_probabilities(ph, g, i)
                    if i >= 1:
                        weigh(i - 1)
                if proj:
                    values(proj[0], 1, 0, 9, free)
                weigh(7)
                if proj:
                    values(proj[0], 0, 1, 10, free)
                    values(proj[0], 1, 1, 11, free)
                if nxt:
                    turn_x(*nxt, p0, free)
                    if KIND[nxt[0]] == CROSS:
                        turn_c(*nxt, p0 + 2, free)
                for b in range(2):
                    merge(b, p0 + prep_uses(nxt) + b)

            def mlp(ph, g, left):
                nxt, hb = prepared(ph, g, left), halves_before(ph, g)

                def free(k):
                    bank_free(ph, g, k)

                pe.wait_ge(g_drained[1], hb)
                pe.wait_ge(wa_split, wa_due(ph, 4))
                for m in range(8):
                    if m >= 4:
                        pe.wait_ge(hidden_done, gh_due(ph, g, m - 3))
                    for part in range(2):
                        for c in range(2):
                            at = (2 * c + part) * CH + m * P
                            ins = three(hidden_ps[m % 4][:, part * GT:(part + 1) * GT], WAh[:, at:at + P], WAl[:, at:at + P],
                                        hTh[:, c, :], hTl[:, c, :], c == 0, c == 1)
                    ins.then_inc(hidden_full, 1)
                if nxt:
                    turn_x(*nxt, 0, free)
                pe.wait_ge(wb_split, wb_due(ph, B_CHUNKS[ph]))
                for b in range(2):
                    pe.wait_ge(g_drained[b], hb)
                    for m in range(8):
                        if b == 0:
                            pe.wait_ge(gl_done, gh_due(ph, g, m + 1))
                        o, w = slice(m * GT + b * P, m * GT + (b + 1) * P), slice(m * D, (m + 1) * D)
                        ins = three(psO[b][:, 0:D], Oh[:, o], Ol[:, o], WBh[:, w], WBl[:, w], m == 0, m == 7)
                    ins.then_inc(g_full, 1)

            def reassociated(ph, g, left):
                nxt, hb = prepared(ph, g, left), halves_before(ph, g)
                qb, ob = quads_before(ph, g), o_before(ph, g)

                def free(k):
                    bank_free(ph, g, k)

                def scores(i):
                    b, j = i // 2, i % 2
                    tok = slice(b * P, (b + 1) * P)
                    if i == 3:
                        pe.wait_ge(mask_added, 4 * g + 1)
                    for p in range(2):
                        ps = psS[i % 3]
                        pe.matmul(ps[:, p * GT:(p + 1) * GT], TT[:, H1 + 2 * j + p, tok],
                                  cB[:, b, :, :].rearrange("p e n -> p (e n)"), start=True, stop=False, skip_group_check=True)
                        for e in range(2):
                            h = 2 * p + e
                            ins = pe.matmul(ps[:, h * P:(h + 1) * P], TT[:, 4 * j + h, tok], cA[:, tok],
                                            start=False, stop=True, skip_group_check=True)
                    ins.then_inc(s_full, 1)

                def weigh(i):
                    b = i // 2
                    pe.wait_ge(pt_ready, qb + i + 1)
                    if i >= 1:
                        pe.wait_ge(o_drained, ob + i)
                    pe.matmul(psO[0][:, :], cU[:, b, 0:P], PT[:, i % 2, :], start=True, stop=True)
                    pairs = PT[:, i % 2, :].rearrange("p (f e n) -> p f e n", f=2, e=2)
                    for e in range(2):
                        ins = pe.matmul(psO[1][e * DB:(e + 1) * DB, 0:GT], cU[:, b, P:DC], pairs[:, :, e, :],
                                        start=True, stop=True)
                    ins.then_inc(pv_done, 1)

                def merge(b, k):
                    free(k)
                    pe.wait_ge(o_drained, ob + 2 * b + 2)
                    for n in range(H1 + H1 // 2):
                        o, w = slice(n * P, (n + 1) * P), slice(2 * NA + n * D, 2 * NA + (n + 1) * D)
                        ins = three(psG[k % 2][:, 0:D], Oh[:, o], Ol[:, o], WAh[:, w], WAl[:, w], n == 0, n == 11)
                    ins.then_inc(g_full, 1)

                pe.wait_ge(g_drained[1], hb - 1)
                for u in range(6):
                    free(u)
                    for m in (2 * u, 2 * u + 1):
                        for c in range(2):
                            at = c * NA + m * P
                            ins = three(psG[u % 2][:, (m % 2) * GT:(m % 2 + 1) * GT], WAh[:, at:at + P], WAl[:, at:at + P],
                                        hTh[:, c, :], hTl[:, c, :], c == 0, c == 1)
                    ins.then_inc(g_full, 1)
                for k in (0, 1):
                    pe.wait_ge(g_drained[k], hb + 3)
                scores(0)
                scores(1)
                scores(2)
                turn_probabilities(ph, g, 0)
                scores(3)
                turn_probabilities(ph, g, 1)
                weigh(0)
                turn_probabilities(ph, g, 2)
                weigh(1)
                turn_probabilities(ph, g, 3)
                merge(0, 6)
                weigh(2)
                if nxt:
                    turn_x(*nxt, 7, free)
                weigh(3)
                if nxt:
                    turn_c(*nxt, 9, free)
                merge(1, 7 + prep_uses(nxt))

            def products_of_weights():
                def turn(n):
                    h, s = n % H1, n % 2
                    if 2 <= n < H1:
                        pe.wait_ge(pre_q, n - 1)
                    if n >= 2:
                        pe.wait_ge(pre_k, n - 1)
                    if n == H1:
                        pe.wait_ge(big_loaded, 48)
                    for d in range(2):
                        at = h * D1 + d * P
                        if n < H1:
                            for c in range(2):
                                pe.transpose(psS[s][:, d * D + c * P:d * D + (c + 1) * P], raw_q1[:, c, at:at + P], ident[:, :])
                        w = raw_k1 if n < H1 else raw_v1
                        pe.transpose(psO[s][:, d * DC:d * DC + P], w[:, 0, at:at + P], ident[:, :])
                        ins = pe.transpose(psO[s][:, d * DC + P:(d + 1) * DC], w[0:DB, 1, at:at + P], ident[0:DB, 0:DB])
                    ins.then_inc(pre_turned, 1)

                def product(n):
                    h, s, e = n % H1, n % 2, n % 2
                    q, w = Pr[:, 2 * s, :], Pr[:, 2 * s + 1, :]
                    if n < H1:
                        pe.wait_ge(pre_q, n + 1)
                    pe.wait_ge(pre_k, n + 1)
                    if n >= 2:
                        pe.wait_ge(pre_lo, n - 1)
                    if n < H1:
                        for c in range(2):
                            for d in range(2):
                                ins = pe.matmul(psG[s][:, c * DC:(c + 1) * DC], q[:, d * D + c * P:d * D + (c + 1) * P],
                                                w[:, d * DC:(d + 1) * DC], start=d == 0, stop=d == 1)
                    else:
                        for d in range(2):
                            pe.matmul(psG[s][:, 0:D], w[:, d * DC:d * DC + P], raw_o1[:, 2 * h + d, :],
                                      start=d == 0, stop=d == 1)
                        for d in range(2):
                            ins = pe.matmul(psG[s][e * DB:(e + 1) * DB, D:2 * D], w[:, d * DC + P:(d + 1) * DC],
                                            raw_o1[:, 2 * h + d, :], start=d == 0, stop=d == 1)
                    ins.then_inc(pre_full, 1)

                pe.wait_ge(raw_loaded, raw_due(L1PH))
                turn(0)
                for n in range(2 * H1):
                    if n + 1 < 2 * H1:
                        turn(n + 1)
                    product(n)

            bodies = {SELF: attention, CROSS: attention, FF: mlp, L1: reassociated}
            pe.wait_ge(ident_ready, 2)
            turn_x(0, 0, 0, lambda k: None)
            for ph in range(len(KIND)):
                if KIND[ph] == L1:
                    first = (G_BASE[ph] - opening_uses(ph)) // 2
                    for k in (0, 1):
                        pe.wait_ge(g_drained[k], first)
                    products_of_weights()
                    pe.wait_ge(pre_lo, 2 * H1)
                    turn_x(ph, 0, 0, lambda k: None)
                    turn_c(ph, 0, 2, lambda k: pe.wait_ge(g_drained[k % 2], first + 1))
                    pe.wait_ge(g_drained[1], first + 2)
                    pe.wait_ge(k_zeroed, 4)
                if ph in (0, L1PH + 1):
                    pe.wait_ge(k_zeroed, 2 if ph == 0 else 6)
                if attends(ph) and opening_uses(ph):
                    first = (G_BASE[ph] - PREP_USES[KIND[ph]] - 12) // 2

                    def free(k):
                        pe.wait_ge(g_drained[k % 2], first + k // 2)

                    free(1)
                    for k in range(8):
                        project(ph, k // 2, k, free)
                    for k in range(8, 12):
                        values(ph, k % 2, (k - 8) // 2, k, free)
                    turn_x(ph, 1, 12, free)
                    if KIND[ph] == CROSS:
                        turn_c(ph, 1, 14, free)
                groups(pe, bodies[KIND[ph]], ph)


def kernel(**inputs):
    import numpy as np
    import concourse.bacc as bacc
    from concourse.bass_utils import run_bass_kernel_spmd

    laid_out = {name: inputs[name] for name in ["x", "ctx_768", "mask_BxS2_if1"] + [n for ws in WEIGHTS for n in ws]}
    pairs = [pair or ("L1_xattn_gamma", "L1_xattn_beta") for pair in NORMS]
    laid_out["norm_columns"] = np.stack([[inputs[n] for n in pair] for pair in pairs]).reshape(
        len(NORMS), 2, 2, P).transpose(3, 0, 1, 2)
    laid_out["hidden_bias_columns"] = np.stack([inputs[n] for n in HIDDEN_BIAS.values()]).reshape(
        2, 16, P).transpose(2, 0, 1)
    rows = BIASES[:L1PH] + ["L1_xattn_gamma"] + BIASES[L1PH + 1:] + ["L1_xattn_beta"]
    laid_out["bias_rows"] = np.stack([inputs[n] for n in rows])

    nc = bacc.Bacc("TRN2", target_bir_lowering=False, num_devices=1)
    arrays, tensors = {}, {}
    for name, a in laid_out.items():
        arrays[f"in_{name}"] = a = np.ascontiguousarray(a)
        tensors[name] = nc.dram_tensor(f"in_{name}", a.shape, mybir.dt.from_np(a.dtype), kind="ExternalInput").ap()
    out = nc.dram_tensor("out_x", (B, P, D), F32, kind="ExternalOutput").ap()
    build(nc, tensors, out)
    result = run_bass_kernel_spmd(nc, [arrays], core_ids=[0])
    return result.results[0]["out_x"]
```

```python
from contextlib import ExitStack

import concourse.bass as bass
from concourse import mybir

ALU = mybir.AluOpType
ACT = mybir.ActivationFunctionType
F32 = mybir.dt.float32
F32R = mybir.dt.float32r
I32 = mybir.dt.int32
AX_X = mybir.AxisListType.X

P = 128
B = 16
D = 256
DC = 192
DB = DC - P
INNER = 1024
HD = 64
PAIRS = INNER // P
HID = 1024
H1 = 8
D1 = 256
GROUPS = B // 2
GT = 2 * P
EPS = 1e-5
MAGIC = float(0x5F3759DF)
NEG = -1e30
CH = 1024

SELF, CROSS, FF, L1 = "self", "cross", "ff", "l1"
KIND = [SELF, CROSS, FF, L1, CROSS, SELF, CROSS, FF]
LAST = len(KIND) - 1
L1PH = KIND.index(L1)
WEIGHTS = [
    ("L0_xattn_a1_Wq", "L0_xattn_a1_Wk", "L0_xattn_a1_Wv", "L0_xattn_a1_Wo"),
    ("L0_xattn_a2_Wq", "L0_xattn_a2_Wk", "L0_xattn_a2_Wv", "L0_xattn_a2_Wo"),
    ("L0_xattn_ff_Wp", "L0_xattn_ff_Wo"),
    ("L1_xattn_Wq", "L1_xattn_Wk", "L1_xattn_Wv", "L1_xattn_Wo"),
    ("L2_xattn_Wq", "L2_xattn_Wk", "L2_xattn_Wv", "L2_xattn_Wo"),
    ("L3_xattn_Wq1", "L3_xattn_Wk1", "L3_xattn_Wv1", "L3_xattn_Wo1"),
    ("L3_xattn_Wq2", "L3_xattn_Wk2", "L3_xattn_Wv2", "L3_xattn_Wo2"),
    ("L3_xattn_Wp", "L3_xattn_W2"),
]
NORMS = [("L0_xattn_ln1_g", "L0_xattn_ln1_b"), ("L0_xattn_ln2_g", "L0_xattn_ln2_b"),
         ("L0_xattn_ln3_g", "L0_xattn_ln3_b"), None, ("L2_xattn_gamma", "L2_xattn_beta"),
         ("L3_xattn_g1", "L3_xattn_be1"), ("L3_xattn_g2", "L3_xattn_be2"),
         ("L3_xattn_g3", "L3_xattn_be3")]
BIASES = ["L0_xattn_a1_bo", "L0_xattn_a2_bo", "L0_xattn_ff_bo", None, "L2_xattn_bo",
          "L3_xattn_bo1", "L3_xattn_bo2", "L3_xattn_b2"]
HIDDEN_BIAS = {2: "L0_xattn_ff_bp", 7: "L3_xattn_bp"}
Q_SCALE = [HD ** -0.5, HD ** -0.5, None, None, 1.0, HD ** -0.5, HD ** -0.5, None]
V_SCALE = [1.0, 1.0, None, None, HD ** -0.5, 1.0, 1.0, None]

QUADS = [{SELF: 8, CROSS: 8, FF: 0, L1: 4}[k] for k in KIND]
O_USES = [{SELF: 4, CROSS: 4, FF: 0, L1: 4}[k] for k in KIND]
PREP_USES = {SELF: 2, CROSS: 4, FF: 2, L1: 2}
A_CHUNKS = [{SELF: 6, CROSS: 6, FF: 4, L1: 0}[k] for k in KIND]
B_CHUNKS = [{SELF: 2, CROSS: 2, FF: 2, L1: 0}[k] for k in KIND]


def before(counts, ph):
    return sum(counts[:ph])


def attends(ph):
    return ph <= LAST and KIND[ph] in (SELF, CROSS)


LOOP = 2


def later(ph, g, left, n):
    return (ph, g + n) if left >= n else (ph + 1, n - left - 1)


def projected(ph, g, left):
    after = later(ph, g, left, 1)
    return after if attends(ph) and attends(after[0]) else None


def prepared(ph, g, left):
    if attends(ph):
        after = later(ph, g, left, 2)
        return after if attends(after[0]) or left == 1 else None
    if KIND[ph] == L1:
        return (ph, g + 2) if left >= 2 else None if left else (ph + 1, 0)
    after = later(ph, g, left, 1)
    return None if after[0] in (L1PH, LAST + 1) and left == 0 else after


def prep_uses(group):
    return PREP_USES[KIND[group[0]]] if group else 0


def l1_order(left):
    if left == 0:
        return ["M0", "X0", "X1", "M1", "C0", "C1"]
    order = ["T0", "T1", "T2", "M0", "T3", "C0", "T4", "M1", "C1", "T5"]
    return order + ["X0", "X1"] if left >= 2 else order


def tail_order(nxt):
    if not nxt:
        return ["M0", "M1"]
    return ["X0", "M0", "X1", "C0", "M1", "C1"] if KIND[nxt[0]] == CROSS else ["X0", "M0", "X1", "M1"]


def body_uses(ph, left):
    if KIND[ph] == L1:
        return len(l1_order(left))
    main = 2
    return main + 12 * bool(projected(ph, 0, left)) + prep_uses(prepared(ph, 0, left))


def opening_uses(ph):
    if attends(ph) and not (ph and attends(ph - 1)):
        return 12 + PREP_USES[KIND[ph]] + (PREP_USES[KIND[ph]] if ph == 0 else 0)
    return 12 if KIND[ph] == L1 else 0


G_BASE = []
_n = 0
for _p in range(LAST + 1):
    G_BASE.append(_n + opening_uses(_p))
    _n = G_BASE[-1] + (GROUPS - 2) * body_uses(_p, LOOP) + body_uses(_p, 1) + body_uses(_p, 0)
G_BASE.append(_n)
assert all(n % 2 == 0 for n in G_BASE)


def uses_before(ph, g):
    if isinstance(g, int) and g == GROUPS - 1:
        return G_BASE[ph] + (GROUPS - 2) * body_uses(ph, LOOP) + body_uses(ph, 1)
    return G_BASE[ph] + g * body_uses(ph, LOOP)


def halves_before(ph, g):
    if isinstance(g, int):
        return uses_before(ph, g) // 2
    return G_BASE[ph] // 2 + g * (body_uses(ph, LOOP) // 2)


def halves_behind(ph, g):
    return G_BASE[ph + 1] // 2 if isinstance(g, int) and g == GROUPS - 1 else halves_before(ph, g + 1)


def quads_before(ph, g):
    return GROUPS * before(QUADS, ph) + g * QUADS[ph]


def o_before(ph, g):
    return GROUPS * before(O_USES, ph) + g * O_USES[ph]


def context_preps_before(ph, g):
    return GROUPS * sum(k in (CROSS, L1) for k in KIND[:ph]) + g


def norms_before(ph, g):
    return GROUPS * sum(k != L1 for k in KIND[:ph]) + g


def build(nc, t, out):
    with ExitStack() as ctx:
        def sb(name, shape, dt=F32):
            return ctx.enter_context(nc.sbuf_tensor(name, shape, dt))

        def sem(name):
            return ctx.enter_context(nc.semaphore(name))

        X = sb("X", [P, B, D])
        XB = sb("XB", [P, 2, D])
        WAh, WAl = sb("WAh", [P, 6 * CH], F32R), sb("WAl", [P, 6 * CH], F32R)
        WBh, WBl = sb("WBh", [P, 2 * CH], F32R), sb("WBl", [P, 2 * CH], F32R)
        raw = sb("raw", [P, 8 * CH])
        big = sb("big", [P, 8 * CH])
        Oh, Ol = sb("Oh", [P, 2 * CH], F32R), sb("Ol", [P, 2 * CH], F32R)
        hTh, hTl = sb("hTh", [P, 2, GT], F32R), sb("hTl", [P, 2, GT], F32R)
        hTf = sb("hTf", [P, 2, GT])
        cRaw = sb("cRaw", [P, 2, 2 * P])
        cTh, cTl = sb("cTh", [P, 2, GT], F32R), sb("cTl", [P, 2, GT], F32R)
        Z = sb("Z", [P, 2, D])
        Pr = sb("Pr", [P, 4, 4 * P])
        PT = sb("PT", [P, 2, 4 * P])
        ident = sb("ident", [P, P])
        bo_rows = sb("bo_rows", [P, 9, D])
        norm_cols = sb("norm_cols", [P, len(NORMS), 2, 2])
        hid_cols = sb("hid_cols", [P, 2, 16])
        negmax = sb("negmax", [P, 4, 4])
        esum = sb("esum", [P, 4, 4])
        rsum = sb("rsum", [P, 4, 4])
        stats, means, ve = sb("stats", [P, 2, 6]), sb("means", [P, 2]), sb("ve", [P, 2])
        sa, sc, rstd = sb("sa", [P, 3, 2]), sb("sc", [P, 2, 2]), sb("rstd", [P, 4, 2])
        pstats, pmeans, pve = sb("pstats", [P, 2, 6]), sb("pmeans", [P, 2]), sb("pve", [P, 2])
        psa, psc, prstd = sb("psa", [P, 3, 2]), sb("psc", [P, 2, 2]), sb("prstd", [P, 4, 2])

        Q = big[:, 0:2 * CH].rearrange("p (f n) -> p f n", f=PAIRS)
        K = big[:, 2 * CH:6 * CH].rearrange("p (f b e n) -> p f b e n", f=PAIRS, b=2, e=2)
        V = big[:, 6 * CH:8 * CH].rearrange("p (b n) -> p b n", b=2)
        GE, Uf = Pr[:, :, 0:GT], Pr[:, :, GT:2 * GT]
        TT = big[:, 8 * GT:20 * GT].rearrange("p (m n) -> p m n", m=12)
        cA = big[:, 20 * GT:21 * GT]
        cB = big[:, 21 * GT:23 * GT].rearrange("p (b e n) -> p b e n", b=2, e=2)
        cU = big[:, 0:2 * GT].rearrange("p (b n) -> p b n", b=2)
        R1, R2, R3 = sb("R1", [P, 2, D]), sb("R2", [P, 2, D]), sb("R3", [P, 2, D])
        mask_row = big[0:1, 24 * GT:24 * GT + B * P].bitcast(I32)
        mask_added = WBh[0:1, 12 * P:12 * P + GT]
        ones_row = sb("ones_row", [1, P], F32R)
        U_hi, U_lo = (Oh, WBh), (Ol, WBl)
        raw_q1 = raw[:, 0:4 * CH].rearrange("p (c n) -> p c n", c=2)
        raw_k1 = raw[:, 4 * CH:8 * CH].rearrange("p (c n) -> p c n", c=2)
        raw_v1 = big[:, 0:4 * CH].rearrange("p (c n) -> p c n", c=2)
        raw_o1 = big[:, 4 * CH:8 * CH].rearrange("p (c n) -> p c n", c=16)
        NA = 12 * P

        psS = [ctx.enter_context(nc.psum_tensor(f"psS{i}", [P, 512], F32)) for i in range(3)]
        psT = ctx.enter_context(nc.psum_tensor("psT", [P, 512], F32))
        psO = [ctx.enter_context(nc.psum_tensor(f"psO{i}", [P, 512], F32)) for i in range(2)]
        psG = [ctx.enter_context(nc.psum_tensor(f"psG{i}", [P, 512], F32)) for i in range(2)]

        hidden_ps = psS + [psT]

        x_loaded = sem("x_loaded")
        x_second_loaded, x_rest_loaded = sem("x_second_loaded"), sem("x_rest_loaded")
        norms_loaded = sem("norms_loaded")
        params_loaded = sem("params_loaded")
        first_loaded = [sem(f"first_loaded_{w}") for w in "qkvo"]
        raw_loaded = sem("raw_loaded")
        big_loaded = sem("big_loaded")
        context_loaded = sem("context_loaded")
        mask_loaded = sem("mask_loaded")
        stored = sem("stored")
        ident_ready = sem("ident_ready")
        k_zeroed = sem("k_zeroed")
        cb_zeroed = sem("cb_zeroed")
        wa_rounded, wa_split = sem("wa_rounded"), sem("wa_split")
        wb_rounded, wb_split = sem("wb_rounded"), sem("wb_split")
        g_full = sem("g_full")
        g_drained = [sem("g_drained0"), sem("g_drained1")]
        ln_step = sem("ln_step")
        z_ready = sem("z_ready")
        x_turned = sem("x_turned")
        c_turned = sem("c_turned")
        cu_copied = sem("cu_copied")
        turn_step = sem("turn_step")
        s_full = sem("s_full")
        max_ready = sem("max_ready")
        ones_ready = sem("ones_ready")
        mask_ready = sem("mask_ready")
        exp_done = sem("exp_done")
        rsum_ready = sem("rsum_ready")
        p_ready = sem("p_ready")
        t_full = sem("t_full")
        pt_ready = sem("pt_ready")
        pv_done = sem("pv_done")
        u_full, u_rounded = sem("u_full"), sem("u_rounded")
        o_rounded, o_drained = sem("o_rounded"), sem("o_drained")
        xb_ready = sem("xb_ready")
        hidden_full = sem("hidden_full")
        gelu_done = sem("gelu_done")
        hidden_done = sem("hidden_done")
        gh_done, gl_done = sem("gh_done"), sem("gl_done")
        post_step = sem("post_step")
        post_done = sem("post_done")
        pre_turned, pre_q, pre_k = sem("pre_turned"), sem("pre_q"), sem("pre_k")
        pre_full, pre_hi, pre_lo = sem("pre_full"), sem("pre_hi"), sem("pre_lo")

        MOMENT_STEPS = 9 + 9
        LN_STEPS = 2 + MOMENT_STEPS
        POST_STEPS = 2 + MOMENT_STEPS + 4

        def rows_of(ph):
            w = [t[n] for n in WEIGHTS[ph]]
            if KIND[ph] == FF:
                yield raw[:, 0:4 * CH].rearrange("p (c n) -> p c n", c=2), w[0].rearrange("(c p) n -> p c n", p=P)
                yield raw[:, 6 * CH:8 * CH].rearrange("p (c n) -> p c n", c=8), w[1].rearrange("(c p) n -> p c n", p=P)
                return
            if KIND[ph] == L1:
                yield raw_q1, w[0].rearrange("(c p) n -> p c n", p=P)
                yield raw_k1[:, 0, :], w[1][0:P, :]
                yield raw_k1[0:DB, 1, :], w[1][P:DC, :]
                return
            yield raw[:, 0:2 * CH].rearrange("p (c n) -> p c n", c=2), w[0].rearrange("(c p) n -> p c n", p=P)
            for n in (1, 2):
                to = raw[:, 2 * n * CH:(2 * n + 2) * CH].rearrange("p (c n) -> p c n", c=2)
                if KIND[ph] == SELF:
                    yield to, w[n].rearrange("(c p) n -> p c n", p=P)
                else:
                    yield to[:, 0, :], w[n][0:P, :]
                    yield to[0:DB, 1, :], w[n][P:DC, :]
                    yield to[DB:P, 1, :], w[n][P:DC, :]
            yield raw[:, 6 * CH:8 * CH].rearrange("p (c n) -> p c n", c=8), w[3].rearrange("(c p) n -> p c n", p=P)

        RAW_DMAS = [{SELF: 4, CROSS: 8, FF: 2, L1: 3}[k] for k in KIND]

        def raw_due(ph):
            return 16 * (before(RAW_DMAS, ph + 1) - RAW_DMAS[0])

        def wa_due(ph, chunks):
            return before(A_CHUNKS, ph) + chunks

        def wb_due(ph, chunks):
            return before(B_CHUNKS, ph) + chunks

        def stacked(ph, c):
            return KIND[ph] == CROSS and c in (3, 5)

        PARAMS = 2

        def gh_due(ph, g, tiles):
            return GROUPS * 8 * sum(k == FF for k in KIND[:ph]) + 8 * g + tiles

        def o_parts(O, o):
            return O[:, :].rearrange("p (b n) -> p b n", b=2)[:, :, o * GT:(o + 1) * GT]

        def product_parts(W, n):
            h, e = n % H1, n % 2
            ps = psG[n % 2]
            if n < H1:
                to = W[:, 0:2 * NA].rearrange("p (c n) -> p c n", c=2)
                of = ps[:, 0:2 * DC].rearrange("p (c n) -> p c n", c=2)
                return [(to[:, :, h * P:(h + 1) * P], of[:, :, 0:P]),
                        (to[:, :, CH + h * DB:CH + (h + 1) * DB], of[:, :, P:DC])]
            rows, at = slice(e * DB, (e + 1) * DB), 2 * NA + H1 * D + (h // 2) * D
            return [(W[:, 2 * NA + h * D:2 * NA + (h + 1) * D], ps[:, 0:D]),
                    (W[rows, at:at + D], ps[rows, D:2 * D])]

        block = ctx.enter_context(nc.Block())

        def chunk(c):
            return slice(c * CH, (c + 1) * CH)

        def opens(g):
            return isinstance(g, int) and g == 0

        def groups(eng, body, ph):
            body(ph, 0, LOOP)
            with eng.Fori(1, GROUPS - 2) as g:
                body(ph, g, LOOP)
            body(ph, GROUPS - 2, 1)
            body(ph, GROUPS - 1, 0)


        @block.sync
        def _(sp):
            def load_weights(ph):
                for to, src in rows_of(ph):
                    sp.dma_start(to, src).then_inc(raw_loaded, 16)

            def load_context(ph, g):
                n = context_preps_before(ph, g)
                src = t["ctx_768"][bass.ds(2 * g, 2), :, :].rearrange("b p n -> p b n")
                if ph == L1PH and not opens(g):
                    sp.wait_ge(cu_copied, g)
                elif ph > 1 or not opens(g):
                    sp.wait_ge(c_turned, 2 * n)
                if ph == L1PH + 1 and opens(g):
                    sp.wait_ge(cu_copied, GROUPS)
                sp.dma_start(cRaw[:, :, 0:DC], src).then_inc(context_loaded, 16)
                sp.dma_start(cRaw[:, :, DC:2 * P], src[:, :, P:DC]).then_inc(context_loaded, 16)

            def body(ph, g, left):
                nxt = prepared(ph, g, left)
                if KIND[ph] == L1 and left:
                    load_context(ph, g + 1)
                elif nxt and KIND[nxt[0]] == CROSS:
                    load_context(*nxt)
                if ph == LAST:
                    for k in (0, 1):
                        sp.wait_ge(g_drained[k], halves_behind(ph, g))
                    sp.dma_start(out[bass.ds(2 * g, 2), :, :].rearrange("b p n -> p b n"),
                                 X[:, bass.ds(2 * g, 2), :]).then_inc(stored, 16)

            xs = t["x"].rearrange("b p n -> p b n")
            sp.dma_start(X[:, 0:2, :], xs[:, 0:2, :]).then_inc(x_loaded, 16)
            for n, ((to, src), loaded) in enumerate(zip(rows_of(0), first_loaded)):
                sp.dma_start(to, src).then_inc(loaded, 16)
                if n == 1:
                    sp.dma_start(X[:, 2:4, :], xs[:, 2:4, :]).then_inc(x_second_loaded, 16)
            sp.dma_start(X[:, 4:B, :], xs[:, 4:B, :]).then_inc(x_rest_loaded, 16)
            for ph in range(len(KIND)):
                if attends(ph) and ph and not attends(ph - 1):
                    load_context(ph, 1)
                if ph < LAST and ph + 1 != L1PH + 1:
                    if KIND[ph] != L1:
                        sp.wait_ge(wa_split, wa_due(ph, A_CHUNKS[ph]))
                        sp.wait_ge(wb_split, wb_due(ph, B_CHUNKS[ph]))
                    load_weights(ph + 1)
                if ph + 1 == L1PH:
                    sp.wait_ge(g_full, uses_before(ph, 0))
                    sp.dma_start(raw_v1[:, 0, :], t["L1_xattn_Wv"][0:P, :]).then_inc(big_loaded, 16)
                    sp.dma_start(raw_v1[0:DB, 1, :], t["L1_xattn_Wv"][P:DC, :]).then_inc(big_loaded, 16)
                    sp.dma_start(raw_o1, t["L1_xattn_Wo"].rearrange("(c p) n -> p c n", p=P)).then_inc(big_loaded, 16)
                if ph == L1PH:
                    load_context(ph, 0)
                    sp.wait_ge(pre_turned, H1)
                    load_weights(ph + 1)
                    sp.wait_ge(pre_full, 2 * H1)
                    sp.dma_start(mask_row, t["mask_BxS2_if1"].rearrange("b n -> (b n)").unsqueeze(0)).then_inc(mask_loaded, 16)
                groups(sp, body, ph)
            sp.wait_ge(stored, 16 * GROUPS)

        @block.gpsimd
        def _(pool):
            pool.memset(ident[:, :], 0.0).then_inc(ident_ready, 1)
            pool.wait_ge(ident_ready, 1)
            pool.affine_select(out=ident[:, :], in_=ident[:, :], compare_op=ALU.not_equal, fill=1.0, base=0,
                               pattern=[[-1, P]], channel_multiplier=1).then_inc(ident_ready, 1)

            def zero_k():
                pool.memset(big[:, 2 * CH:6 * CH], 0.0).then_inc(k_zeroed, 1)

            zero_k()

            def low_part(ph, c):
                pool.wait_ge(wa_rounded, wa_due(ph, c + 1))
                to, off = (WAh, WAl) if stacked(ph, c) else (WAl, WAh)
                pool.tensor_tensor(to[:, chunk(c)], raw[:, chunk(c)], off[:, chunk(c)].bitcast(F32),
                                   ALU.subtract).then_inc(wa_split, 1)

            def low_b(ph, c):
                pool.wait_ge(wb_rounded, wb_due(ph, c + 1))
                pool.tensor_tensor(WBl[:, chunk(c)], raw[:, chunk(6 + c)], WBh[:, chunk(c)].bitcast(F32),
                                   ALU.subtract).then_inc(wb_split, 1)

            def normalise(ph, g, i):
                qb = quads_before(ph, g)
                pool.wait_ge(rsum_ready, qb + i + 1)
                p4 = Pr[:, i % 4, :].rearrange("p (h n) -> p h n", h=4)
                pool.tensor_tensor(p4, p4, rsum[:, i % 4, :].unsqueeze(2).to_broadcast([P, 4, P]),
                                   ALU.mult).then_inc(p_ready, 1)

            def body(ph, g, left):
                if attends(ph):
                    normalise(ph, g, 0)
                    normalise(ph, g, 1)
                if KIND[ph] != L1:
                    for k in (0, 1):
                        pool.wait_ge(g_drained[k], halves_before(ph, g))
                    if ph == L1PH + 1:
                        pool.wait_ge(post_done, B)
                    pool.tensor_tensor(XB[:, :, :], X[:, bass.ds(2 * g, 2), :],
                                       bo_rows[:, ph:ph + 1, :].to_broadcast([P, 2, D]), ALU.add).then_inc(xb_ready, 1)
                if KIND[ph] == FF:
                    if opens(g):
                        low_b(ph, 0)
                        low_b(ph, 1)
                    for m in range(8):
                        pool.wait_ge(gh_done, gh_due(ph, g, m + 1))
                        pool.tensor_tensor(Ol[:, m * GT:(m + 1) * GT], Uf[:, m % 4, :],
                                           Oh[:, m * GT:(m + 1) * GT].bitcast(F32), ALU.subtract).then_inc(gl_done, 1)
                for i in range(QUADS[ph]):
                    if i > 1 or not attends(ph):
                        normalise(ph, g, i)
                    if opens(g) and attends(ph) and i in (3, 5):
                        low_b(ph, (i - 3) // 2)
                    if left == 0 and attends(ph) and attends(ph + 1) and i in (3, 5):
                        low_part(ph + 1, 4 + i // 4)
                if left == 1 and attends(ph):
                    for c in range(2):
                        low_part(ph + 1, c)
                if left == 0 and KIND[ph] == L1:
                    for c in range(3):
                        low_part(ph + 1, c)
                    zero_k()

            pool.wait_ge(params_loaded, 16 * PARAMS)
            pool.wait_ge(x_loaded, 16)
            pool.wait_ge(x_second_loaded, 16)
            pool.wait_ge(x_rest_loaded, 16)
            for ph in range(len(KIND)):
                if ph == 0:
                    for c in (4, 5):
                        pool.wait_ge(wa_split, c)
                        low_part(ph, c)
                groups(pool, body, ph)

        @block.scalar
        def _(act):
            act.dma_start(norm_cols[:, :, :, :], t["norm_columns"]).then_inc(norms_loaded, 16)
            act.dma_start(hid_cols[:, :, :], t["hidden_bias_columns"]).then_inc(params_loaded, 16)
            act.dma_start(bo_rows[:, :, :], t["bias_rows"].partition_broadcast(P)).then_inc(params_loaded, 16)

            def round_chunk(ph, c):
                if stacked(ph, c):
                    act.activation(WAl[0:DB, chunk(c)], raw[0:DB, chunk(c)], ACT.Copy, scale=0.0)
                    act.activation(WAl[DB:P, chunk(c)], raw[DB:P, chunk(c)], ACT.Copy).then_inc(wa_rounded, 1)
                else:
                    act.activation(WAh[:, chunk(c)], raw[:, chunk(c)], ACT.Copy).then_inc(wa_rounded, 1)

            def turn_x_batch(ph, b, use, k):
                ps = psG[k]
                act.wait_ge(g_full, use + 1)
                if KIND[ph] == L1:
                    act.activation(hTh[:, :, b * P:(b + 1) * P], ps[:, 0:GT].rearrange("p (c n) -> p c n", c=2),
                                   ACT.Copy).then_inc(x_turned, 1)
                    return
                for c in range(2):
                    ins = act.activation(hTh[:, c, b * P:(b + 1) * P], ps[:, c * P:(c + 1) * P], ACT.Identity,
                                         scale=norm_cols[:, ph, 0, c:c + 1], bias=norm_cols[:, ph, 1, c:c + 1])
                ins.then_inc(x_turned, 1)

            def turn_c_batch(ph, b, use, k):
                ps = psG[k]
                act.wait_ge(g_full, use + 1)
                if KIND[ph] == L1:
                    act.activation(cA[:, b * P:(b + 1) * P], ps[:, 0:P], ACT.Copy).then_inc(c_turned, 1)
                else:
                    act.activation(cTh[:, :, b * P:(b + 1) * P], ps[:, 0:GT].rearrange("p (c n) -> p c n", c=2),
                                   ACT.Copy).then_inc(c_turned, 1)

            def turn_x(ph, g, first):
                for b in range(2):
                    turn_x_batch(ph, b, first[0] + b, (first[1] + b) % 2)

            def turn_c(ph, first):
                for b in range(2):
                    turn_c_batch(ph, b, first[0] + b, (first[1] + b) % 2)

            def exps(ph, g, i, scores):
                qb = quads_before(ph, g)
                act.wait_ge(max_ready, qb + i + 1)
                for h in range(4):
                    ins = act.activation(Pr[:, i % 4, h * P:(h + 1) * P], scores[:, h * P:(h + 1) * P], ACT.Exp,
                                         bias=negmax[:, i % 4, h:h + 1], accum_out=esum[:, i % 4, h:h + 1])
                ins.then_inc(exp_done, 1)

            def round_o(ph, g, o):
                act.wait_ge(pv_done, quads_before(ph, g) + 2 * o + 2)
                act.activation(o_parts(Oh, o), psO[o % 2][:, :].rearrange("p (b n) -> p b n", b=2),
                               ACT.Copy).then_inc(o_rounded, 1)

            def drain_q(ph, u, use, k=0):
                act.wait_ge(g_full, use + 1)
                act.activation(Q[:, 2 * u:2 * u + 2, :], psG[k][:, :].rearrange("p (f n) -> p f n", f=2),
                               ACT.Copy, scale=Q_SCALE[ph]).then_inc(g_drained[k], 1)

            def round_b(ph, c):
                act.wait_ge(first_loaded[3] if ph == 0 else raw_loaded, 16 if ph == 0 else raw_due(ph))
                act.activation(WBh[:, chunk(c)], raw[:, chunk(6 + c)], ACT.Copy).then_inc(wb_rounded, 1)

            def drain_k(u, use):
                act.wait_ge(g_full, use + 1)
                for e in range(2):
                    rows = slice(e * HD, (e + 1) * HD)
                    ins = act.activation(K[rows, 2 * u:2 * u + 2, :, e, :],
                                         psG[1][rows, :].rearrange("p (f b n) -> p f b n", f=2, b=2), ACT.Copy)
                ins.then_inc(g_drained[1], 1)

            def drain_v(ph, half, use):
                act.wait_ge(g_full, use + 1)
                act.activation(V[:, 1, half * 512:(half + 1) * 512], psG[1][:, :], ACT.Copy,
                               scale=V_SCALE[ph]).then_inc(g_drained[1], 1)

            def project(ph, use):
                for u in range(4):
                    if ph == 0 and u >= 2:
                        act.wait_ge(first_loaded[2], 16)
                        round_chunk(ph, 2 + u)
                    if ph and u != 1:
                        act.wait_ge(g_full, G_BASE[ph] - opening_uses(ph))
                        round_chunk(ph, 3 + (u + 1) // 2)
                    drain_q(ph, u, use + u, u % 2)
                act.wait_ge(k_zeroed, 1 if ph == 0 else 2)
                drain_k(1, use + 5)
                drain_k(3, use + 7)
                drain_v(ph, 0, use + 9)
                drain_v(ph, 1, use + 11)

            def attention(ph, g, left):
                ub, proj, nxt = uses_before(ph, g), projected(ph, g, left), prepared(ph, g, left)
                p0 = 12 if proj else 0
                exps(ph, g, 1, psS[1])
                if proj:
                    drain_q(proj[0], 0, ub)
                for i in range(8):
                    if i + 2 < 8:
                        exps(ph, g, i + 2, psS[(i + 2) % 3])
                    if opens(g) and i in (1, 3):
                        round_b(ph, i // 2)
                    if proj and i in (1, 3, 5):
                        drain_q(proj[0], (i + 1) // 2, ub + i + 1)
                    if proj and i in (2, 6):
                        drain_k(i // 2 if i == 6 else 1, ub + i + 1)
                    if i in (2, 4, 6):
                        round_o(ph, g, i // 2 - 1)
                    if proj and i == 7:
                        drain_v(proj[0], 0, ub + 9)
                    if left == 0 and attends(ph + 1) and i in (1, 3):
                        if i == 1:
                            act.wait_ge(g_full, uses_before(ph, g))
                        round_chunk(ph + 1, 4 + i // 2)
                    if left == 1 and i >= 6:
                        if i == 6:
                            act.wait_ge(raw_loaded, raw_due(ph + 1))
                            act.wait_ge(g_full, ub + 8)
                        round_chunk(ph + 1, i - 6)
                if left == 1:
                    round_chunk(ph + 1, 2)
                round_o(ph, g, 3)
                if proj:
                    drain_v(proj[0], 1, ub + 11)
                for n, use in enumerate(tail_order(nxt)):
                    if use[0] in "XC":
                        turn = turn_x_batch if use[0] == "X" else turn_c_batch
                        turn(nxt[0], int(use[1]), ub + p0 + n, n % 2)
                    if n == 1 and left == 1:
                        round_chunk(ph + 1, 3)
                    if n == 3 and proj:
                        exps(*proj, 0, psS[0])

            def mlp(ph, g, left):
                nxt, ub = prepared(ph, g, left), uses_before(ph, g)
                bias = hid_cols[:, list(HIDDEN_BIAS).index(ph), :]
                if opens(g):
                    act.wait_ge(params_loaded, 16 * PARAMS)

                def gate(m):
                    act.wait_ge(hidden_full, gh_due(ph, g, m + 1))
                    if m >= 4:
                        act.wait_ge(hidden_done, gh_due(ph, g, m - 3))
                    act.activation(GE[:, m % 4, :], hidden_ps[m % 4][:, GT:2 * GT], ACT.Gelu,
                                   bias=bias[:, 8 + m:9 + m]).then_inc(gelu_done, 1)

                def round_hidden(m):
                    act.wait_ge(hidden_done, gh_due(ph, g, m + 1))
                    act.activation(Oh[:, m * GT:(m + 1) * GT], Uf[:, m % 4, :], ACT.Copy).then_inc(gh_done, 1)

                gate(0)
                for m in range(1, 8):
                    gate(m)
                    if opens(g) and m in (1, 2):
                        round_b(ph, m - 1)
                    round_hidden(m - 1)
                round_hidden(7)
                if nxt:
                    turn_x(*nxt, (ub, 0))

            def reassociated(ph, g, left):
                nxt, ub, qb = prepared(ph, g, left), uses_before(ph, g), quads_before(ph, g)
                at = l1_order(left).index

                def round_u(i):
                    U, j = U_hi[i // 2], i % 2
                    act.wait_ge(u_full, 4 * g + i + 1)
                    act.activation(U[:, j * 512:(j + 1) * 512], psO[0][:, :], ACT.Copy).then_inc(u_rounded, 1)
                    act.wait_ge(pv_done, qb + i + 1)
                    act.activation(U[:, CH + j * GT:CH + (j + 1) * GT], psO[1][:, 0:GT], ACT.Copy).then_inc(o_rounded, 1)

                exps(ph, g, 1, psS[1])
                exps(ph, g, 2, psS[2])
                drain_turned(ph, g, 0)
                exps(ph, g, 3, psS[0])
                if left:
                    drain_t(0, ub + at("T0"), 0)
                if left == 0:
                    act.wait_ge(raw_loaded, raw_due(ph + 1))
                round_u(0)
                drain_turned(ph, g, 1)
                if left:
                    drain_t(1, ub + at("T1"), 1)
                round_u(1)
                drain_turned(ph, g, 2)
                if left:
                    drain_t(2, ub + at("T2"), 0)
                round_u(2)
                drain_turned(ph, g, 3)
                if left == 0:
                    for c in range(3):
                        round_chunk(ph + 1, c)
                if left:
                    drain_t(3, ub + at("T3"), 0)
                round_u(3)
                if left:
                    turn_c_batch(ph, 0, ub + at("C0"), 1)
                    drain_t(4, ub + at("T4"), 0)
                    turn_c_batch(ph, 1, ub + at("C1"), 0)
                    drain_t(5, ub + at("T5"), 1)
                if left >= 2:
                    turn_x(*nxt, (ub + at("X0"), 0))
                if left:
                    exps(ph, g + 1, 0, psS[0])
                if left == 0:
                    turn_x(*nxt, (ub + at("X0"), 1))
                    turn_c(nxt[0], (ub + at("C0"), 0))

            def drain_turned(ph, g, i):
                act.wait_ge(t_full, quads_before(ph, g) + i + 1)
                act.activation(PT[:, i % 2, :], psT[:, :], ACT.Copy).then_inc(pt_ready, 1)

            def drain_t(u, use, k):
                act.wait_ge(g_full, use + 1)
                act.activation(TT[:, 2 * u:2 * u + 2, :], psG[k][:, :].rearrange("p (m n) -> p m n", m=2),
                               ACT.Copy, scale=D1 ** -0.5).then_inc(g_drained[k], 1)

            def round_product(n):
                act.wait_ge(pre_full, n + 1)
                for to, of in product_parts(WAh, n):
                    ins = act.activation(to, of, ACT.Copy)
                ins.then_inc(pre_hi, 1)

            bodies = {SELF: attention, CROSS: attention, FF: mlp, L1: reassociated}
            for c in range(4):
                act.wait_ge(first_loaded[c // 2], 16)
                round_chunk(0, c)
                if c == 1:
                    act.wait_ge(norms_loaded, 16)
                    turn_x(0, 0, (0, 0))
            for ph in range(len(KIND)):
                if KIND[ph] == L1:
                    act.wait_ge(g_full, G_BASE[ph] - opening_uses(ph))
                    for n in range(2 * H1):
                        s = n % 2
                        if n < H1:
                            act.wait_ge(pre_turned, n + 1)
                            if n >= 2:
                                act.wait_ge(pre_full, n - 1)
                            act.activation(Pr[:, 2 * s, :], psS[s][:, :], ACT.Copy).then_inc(pre_q, 1)
                        if n >= 1:
                            round_product(n - 1)
                    round_product(2 * H1 - 1)
                    turn_x(ph, 0, (G_BASE[ph] - 12, 0))
                    turn_c(ph, (G_BASE[ph] - 10, 0))
                    for u in range(6):
                        drain_t(u, G_BASE[ph] - 8 + u, u % 2)
                    turn_x(ph, 1, (G_BASE[ph] - 2, 0))
                    exps(ph, 0, 0, psS[0])
                if attends(ph) and opening_uses(ph):
                    prep = PREP_USES[KIND[ph]]
                    project(ph, G_BASE[ph] - prep - 12)
                    turn_x(ph, 1, (G_BASE[ph] - prep, 0))
                    if KIND[ph] == CROSS:
                        turn_c(ph, (G_BASE[ph] - 2, 0))
                    exps(ph, 0, 0, psS[0])
                groups(act, bodies[KIND[ph]], ph)

        @block.vector
        def _(dve):
            def moments_part(step, done, st, m, y, a, c, e, n):
                if n == 0:
                    dve.wait_ge(step, done)
                    dve.tensor_tensor(a[:, 0, :], st[:, :, 1], st[:, :, 4], ALU.add).then_inc(step, 1)
                    dve.tensor_tensor(a[:, 1, :], st[:, :, 1], st[:, :, 4], ALU.subtract).then_inc(step, 1)
                    dve.tensor_tensor(a[:, 2, :], st[:, :, 2], st[:, :, 5], ALU.add).then_inc(step, 1)
                elif n == 1:
                    dve.wait_ge(step, done + 3)
                    dve.tensor_scalar(m, a[:, 0, :], 0.5, None, ALU.mult).then_inc(step, 1)
                    dve.scalar_tensor_tensor(c[:, 0, :], a[:, 1, :], 0.25, a[:, 1, :], ALU.mult, ALU.mult).then_inc(step, 1)
                    dve.tensor_scalar(c[:, 1, :], a[:, 2, :], 1.0 / D, EPS, ALU.mult, ALU.add).then_inc(step, 1)
                elif n == 2:
                    dve.wait_ge(step, done + 6)
                    dve.tensor_tensor(e, c[:, 0, :], c[:, 1, :], ALU.add).then_inc(step, 1)
                elif n == 3:
                    dve.wait_ge(step, done + 7)
                    dve.tensor_scalar(a[:, 0, :].bitcast(I32), e.bitcast(I32), 1, None, ALU.logical_shift_right).then_inc(step, 1)
                elif n == 4:
                    dve.wait_ge(step, done + 8)
                    dve.tensor_scalar(y[:, 0, :].bitcast(I32), a[:, 0, :].bitcast(I32), -1.0, MAGIC, ALU.mult, ALU.add).then_inc(step, 1)
                else:
                    k, at = divmod(n - 5, 3)
                    dve.wait_ge(step, done + 4 + n)
                    if at == 0:
                        dve.tensor_tensor(a[:, 0, :], y[:, k, :], y[:, k, :], ALU.mult).then_inc(step, 1)
                    elif at == 1:
                        dve.scalar_tensor_tensor(c[:, 0, :], a[:, 0, :], -0.5, e, ALU.mult, ALU.mult).then_inc(step, 1)
                    else:
                        dve.scalar_tensor_tensor(y[:, k + 1, :], c[:, 0, :], 1.5, y[:, k, :], ALU.add, ALU.mult).then_inc(step, 1)

            NORM_PARTS = 16

            def norm_part(ph, g, n):
                done = LN_STEPS * norms_before(ph, g)
                if KIND[ph] == L1:
                    if n == 0:
                        for b in range(2):
                            dve.tensor_copy(Z[:, b:b + 1, :], X[:, bass.ds(2 * g + b, 1), :]).then_inc(z_ready, 1)
                elif n == 0:
                    for b in range(2):
                        dve.bn_stats(stats[:, b, :], X[:, bass.ds(2 * g + b, 1), :].rearrange("p b n -> p (b n)")).then_inc(ln_step, 1)
                elif n < NORM_PARTS - 1:
                    moments_part(ln_step, done + 2, stats, means[:, :], rstd, sa, sc, ve[:, :], n - 1)
                else:
                    dve.wait_ge(ln_step, done + LN_STEPS)
                    for b in range(2):
                        dve.tensor_scalar(Z[:, b:b + 1, :], X[:, bass.ds(2 * g + b, 1), :], means[:, b:b + 1], rstd[:, 3, b:b + 1],
                                          ALU.subtract, ALU.mult).then_inc(z_ready, 1)

            def normalise_tokens(ph, g):
                for n in range(NORM_PARTS):
                    norm_part(ph, g, n)

            def turn_x_batch(ph, g, b, use, k):
                r, done = 2 * (GROUPS * ph + g), 4 * norms_before(ph, g)
                ps, cols = psG[k], slice(b * P, (b + 1) * P)
                dve.wait_ge(g_full, use + 1)
                dve.wait_ge(x_turned, r + b + 1)
                if KIND[ph] == L1:
                    dve.tensor_tensor(hTl[:, :, cols], ps[:, 0:GT].rearrange("p (c n) -> p c n", c=2),
                                      hTh[:, :, cols].bitcast(F32), ALU.subtract).then_inc(g_drained[k], 1)
                    return
                for c in range(2):
                    dve.tensor_scalar(hTf[:, c, cols], ps[:, c * P:(c + 1) * P], norm_cols[:, ph, 0, c:c + 1],
                                      norm_cols[:, ph, 1, c:c + 1], ALU.mult, ALU.add).then_inc(turn_step, 1)
                dve.wait_ge(turn_step, done + 2 * b + 2)
                dve.tensor_tensor(hTl[:, :, cols], hTf[:, :, cols], hTh[:, :, cols].bitcast(F32),
                                  ALU.subtract).then_inc(g_drained[k], 1)

            def turn_c_batch(ph, g, b, use, k):
                ps, cols = psG[k], slice(b * P, (b + 1) * P)
                dve.wait_ge(g_full, use + 1)
                dve.wait_ge(c_turned, 2 * context_preps_before(ph, g) + b + 1)
                if KIND[ph] == L1:
                    dve.tensor_copy(cB[0:DB, b, 0, :], ps[0:DB, P:2 * P])
                    dve.tensor_copy(cB[DB:P, b, 1, :], ps[DB:P, P:2 * P]).then_inc(g_drained[k], 1)
                else:
                    dve.tensor_tensor(cTl[:, :, cols], ps[:, 0:GT].rearrange("p (c n) -> p c n", c=2),
                                      cTh[:, :, cols].bitcast(F32), ALU.subtract).then_inc(g_drained[k], 1)

            def turn_x(ph, g, first):
                for b in range(2):
                    turn_x_batch(ph, g, b, first[0] + b, (first[1] + b) % 2)

            def turn_c(ph, g, first):
                for b in range(2):
                    turn_c_batch(ph, g, b, first[0] + b, (first[1] + b) % 2)

            def copy_context(g):
                if not opens(g):
                    dve.wait_ge(pv_done, quads_before(L1PH, g))
                dve.tensor_copy(cU[:, :, 0:DC], cRaw[:, :, 0:DC]).then_inc(cu_copied, 1)

            def maxima(ph, g, i, scores):
                dve.reduce_max(negmax[:, i % 4, :], scores, AX_X, negate=True).then_inc(max_ready, 1)

            def score_maxima(ph, g, i):
                dve.wait_ge(s_full, quads_before(ph, g) + i + 1)
                maxima(ph, g, i, psS[i % 3][:, :].rearrange("p (h n) -> p h n", h=4))

            def reciprocals(ph, g, i):
                dve.wait_ge(exp_done, quads_before(ph, g) + i + 1)
                dve.reciprocal(rsum[:, i % 4, :], esum[:, i % 4, :]).then_inc(rsum_ready, 1)

            def drain_turned(ph, g, i):
                dve.wait_ge(t_full, quads_before(ph, g) + i + 1)
                dve.tensor_copy(PT[:, i % 2, :], psT[:, :]).then_inc(pt_ready, 1)

            def low_o(ph, g, o):
                dve.wait_ge(o_rounded, o_before(ph, g) + o + 1)
                dve.tensor_tensor(o_parts(Ol, o), psO[o % 2][:, :].rearrange("p (b n) -> p b n", b=2),
                                  o_parts(Oh, o).bitcast(F32), ALU.subtract).then_inc(o_drained, 1)

            def residual(ph, g, b, use, k):
                dve.wait_ge(g_full, use + 1)
                dve.wait_ge(xb_ready, norms_before(ph, g) + 1)
                dve.tensor_tensor(X[:, bass.ds(2 * g + b, 1), :], psO[b][:, 0:D].unsqueeze(1), XB[:, b:b + 1, :],
                                  ALU.add).then_inc(g_drained[k], 1)

            def own_writes(ph, g):
                for k in (0, 1):
                    dve.wait_ge(g_drained[k], halves_before(ph, g))
                if ph == L1PH + 1:
                    dve.wait_ge(post_done, B)

            def drain_k(u, use, k=1):
                dve.wait_ge(g_full, use + 1)
                for e in range(2):
                    rows = slice(e * HD, (e + 1) * HD)
                    ins = dve.tensor_copy(K[rows, 2 * u:2 * u + 2, :, e, :],
                                          psG[k][rows, :].rearrange("p (f b n) -> p f b n", f=2, b=2))
                ins.then_inc(g_drained[k], 1)

            def drain_v(ph, half, use):
                dve.wait_ge(g_full, use + 1)
                dve.tensor_scalar(V[:, 0, half * 512:(half + 1) * 512], psG[0][:, :], V_SCALE[ph], None,
                                  ALU.mult).then_inc(g_drained[0], 1)

            def project(ph, use):
                dve.wait_ge(k_zeroed, 1 if ph == 0 else 2)
                if ph == 0:
                    dve.wait_ge(x_second_loaded, 16)
                for n in range(0, 5):
                    norm_part(ph, 1, n)
                drain_k(0, use + 4, 0)
                if ph:
                    low_chunk(ph, 5)
                for n in range(5, 8):
                    norm_part(ph, 1, n)
                drain_k(2, use + 6, 0)
                for n in range(8, 11):
                    norm_part(ph, 1, n)
                drain_v(ph, 0, use + 8)
                for n in range(11, NORM_PARTS):
                    norm_part(ph, 1, n)
                drain_v(ph, 1, use + 10)

            def attention(ph, g, left):
                ub, proj, nxt = uses_before(ph, g), projected(ph, g, left), prepared(ph, g, left)
                p0 = 12 if proj else 0
                own_writes(ph, g)
                reciprocals(ph, g, 0)
                score_maxima(ph, g, 1)
                for i in range(8):
                    if i + 2 < 8:
                        score_maxima(ph, g, i + 2)
                    if i + 1 < 8:
                        reciprocals(ph, g, i + 1)
                    if i in (3, 5, 7):
                        low_o(ph, g, (i - 3) // 2)
                    if proj and i in (0, 4):
                        drain_k(i // 2, ub + i + 1)
                    drain_turned(ph, g, i)
                    if proj and i == 6:
                        drain_v(proj[0], 0, ub + 8)
                    if nxt:
                        norm_part(*nxt, 2 * i)
                        norm_part(*nxt, 2 * i + 1)
                if proj:
                    drain_v(proj[0], 1, ub + 10)
                low_o(ph, g, 3)
                if left == 1:
                    dve.wait_ge(wa_split, wa_due(ph + 1, 2))
                    low_chunk(ph + 1, 2)
                for n, use in enumerate(tail_order(nxt)):
                    b = int(use[1])
                    if use[0] == "M":
                        residual(ph, g, b, ub + p0 + n, n % 2)
                    else:
                        turn = turn_x_batch if use[0] == "X" else turn_c_batch
                        turn(*nxt, b, ub + p0 + n, n % 2)
                    if n == 2 and proj:
                        score_maxima(*proj, 0)
                    if n == 3 and left == 1:
                        low_chunk(ph + 1, 3)

            def mlp(ph, g, left):
                nxt, ub = prepared(ph, g, left), uses_before(ph, g)
                bias = hid_cols[:, list(HIDDEN_BIAS).index(ph), :]
                if opens(g):
                    dve.wait_ge(params_loaded, 16 * PARAMS)
                own_writes(ph, g)
                for m in range(8):
                    dve.wait_ge(gelu_done, gh_due(ph, g, m + 1))
                    if m >= 4:
                        dve.wait_ge(gl_done, gh_due(ph, g, m - 3))
                    dve.scalar_tensor_tensor(Uf[:, m % 4, :], hidden_ps[m % 4][:, 0:GT], bias[:, m:m + 1], GE[:, m % 4, :],
                                             ALU.add, ALU.mult).then_inc(hidden_done, 1)
                    if nxt:
                        for n in range(3 * m, min(3 * m + 3, NORM_PARTS)):
                            norm_part(*nxt, n)
                if nxt:
                    turn_x(*nxt, (ub, 0))
                for b in range(2):
                    residual(ph, g, b, ub + prep_uses(nxt) + b, b)

            def reassociated(ph, g, left):
                nxt, ub, qb = prepared(ph, g, left), uses_before(ph, g), quads_before(ph, g)
                at = l1_order(left).index
                own_writes(ph, g)

                def low_u(i):
                    j, hi, lo = i % 2, U_hi[i // 2], U_lo[i // 2]
                    cols = slice(j * 512, (j + 1) * 512)
                    dve.wait_ge(u_rounded, 4 * g + i + 1)
                    dve.tensor_tensor(lo[:, cols], psO[0][:, :], hi[:, cols].bitcast(F32), ALU.subtract)
                    cols = slice(CH + j * GT, CH + (j + 1) * GT)
                    dve.wait_ge(o_rounded, o_before(ph, g) + i + 1)
                    dve.tensor_tensor(lo[:, cols], psO[1][:, 0:GT], hi[:, cols].bitcast(F32),
                                      ALU.subtract).then_inc(o_drained, 1)

                def add_stream(b):
                    use = at(f"M{b}")
                    k = use % 2
                    if not opens(g):
                        dve.wait_ge(post_done, 2 * g)
                    dve.wait_ge(g_full, ub + use + 1)
                    dve.tensor_tensor(R1[:, b:b + 1, :], psG[k][:, 0:D].unsqueeze(1), X[:, bass.ds(2 * g + b, 1), :],
                                      ALU.add).then_inc(g_drained[k], 1)
                    dve.wait_ge(g_drained[k], halves_before(ph, g) + use // 2 + 1)
                    dve.bn_stats(pstats[:, b, :], R1[:, b, :]).then_inc(post_step, 1)

                def norms(start, end):
                    if nxt:
                        for n in range(start, end):
                            norm_part(*nxt, n)

                def last_norm(start, end):
                    if not opens(g):
                        for n in range(start, end):
                            post_part(g - 1, n)

                reciprocals(ph, g, 0)
                score_maxima(ph, g, 1)
                last_norm(0, 3)
                score_maxima(ph, g, 2)
                last_norm(3, 5)
                reciprocals(ph, g, 1)
                score_maxima(ph, g, 3)
                reciprocals(ph, g, 2)
                last_norm(5, 7)
                low_u(0)
                last_norm(7, 9)
                reciprocals(ph, g, 3)
                if left:
                    write_mask(g + 1)
                low_u(1)
                last_norm(9, POST_PARTS)
                if left == 0:
                    dve.wait_ge(post_done, B - 2)
                norms(0, 6)
                low_u(2)
                norms(6, 16)
                add_stream(0)
                low_u(3)
                if left:
                    turn_c_batch(ph, g + 1, 0, ub + at("C0"), 1)
                else:
                    turn_x(*nxt, (ub + at("X0"), 1))
                add_stream(1)
                if left:
                    turn_c_batch(ph, g + 1, 1, ub + at("C1"), 0)
                    copy_context(g + 1)
                    score_maxima(ph, g + 1, 0)
                else:
                    turn_c(*nxt, (ub + at("C0"), 0))
                if left >= 2:
                    turn_x(*nxt, (ub + at("X0"), 0))

            POST_PARTS = 17

            def post_part(g, n):
                done = POST_STEPS * g + 2
                if n < 14:
                    moments_part(post_step, done, pstats, pmeans[:, :], prstd, psa, psc, pve[:, :], n)
                    return
                done = done + MOMENT_STEPS
                if n == 14:
                    dve.wait_ge(post_step, done)
                for b in range(2):
                    if n == 14:
                        dve.tensor_scalar(R2[:, b, :], R1[:, b, :], pmeans[:, b:b + 1], prstd[:, 3, b:b + 1],
                                          ALU.subtract, ALU.mult).then_inc(post_step, 1)
                    elif n == 15:
                        dve.wait_ge(post_step, done + 1 + b)
                        dve.tensor_tensor(R3[:, b, :], R2[:, b, :], bo_rows[:, L1PH, :], ALU.mult).then_inc(post_step, 1)
                    else:
                        dve.wait_ge(post_step, done + 3 + b)
                        dve.tensor_tensor(X[:, bass.ds(2 * g + b, 1), :], R3[:, b:b + 1, :], bo_rows[:, 8:9, :],
                                          ALU.add).then_inc(post_done, 1)

            def write_mask(g):
                dve.tensor_scalar(mask_added, mask_row[:, bass.ds(g * GT, GT)], 0, NEG, ALU.is_equal,
                                  ALU.mult).then_inc(mask_ready, 1)

            def low_product(n):
                dve.wait_ge(pre_hi, n + 1)
                for (to, of), (hi, _) in zip(product_parts(WAl, n), product_parts(WAh, n)):
                    ins = dve.tensor_tensor(to, of, hi.bitcast(F32), ALU.subtract)
                ins.then_inc(pre_lo, 1)

            def low_chunk(ph, c):
                dve.wait_ge(wa_rounded, wa_due(ph, c + 1))
                to, off = (WAh, WAl) if stacked(ph, c) else (WAl, WAh)
                dve.tensor_tensor(to[:, chunk(c)], raw[:, chunk(c)], off[:, chunk(c)].bitcast(F32),
                                  ALU.subtract).then_inc(wa_split, 1)

            bodies = {SELF: attention, CROSS: attention, FF: mlp, L1: reassociated}

            dve.wait_ge(x_loaded, 16)
            normalise_tokens(0, 0)
            for c in range(4):
                low_chunk(0, c)
                if c == 1:
                    turn_x(0, 0, (0, 0))
            for ph in range(len(KIND)):
                if KIND[ph] == L1:
                    for k in (0, 1):
                        dve.wait_ge(g_drained[k], (G_BASE[ph] - opening_uses(ph)) // 2)
                    normalise_tokens(ph, 0)
                    for n in range(2 * H1):
                        s = n % 2
                        dve.wait_ge(pre_turned, n + 1)
                        if n >= 2:
                            dve.wait_ge(pre_full, n - 1)
                        dve.tensor_copy(Pr[:, 2 * s + 1, 0:2 * DC], psO[s][:, 0:2 * DC]).then_inc(pre_k, 1)
                        if n >= 2:
                            low_product(n - 2)
                    low_product(2 * H1 - 2)
                    low_product(2 * H1 - 1)
                    dve.memset(cB[0:DB, :, 1, :], 0.0).then_inc(cb_zeroed, 1)
                    dve.memset(cB[DB:P, :, 0, :], 0.0).then_inc(cb_zeroed, 1)
                    dve.wait_ge(ident_ready, 2)
                    dve.tensor_scalar(ones_row[:, :], ident[0:1, :], 0.0, 1.0, ALU.mult, ALU.add).then_inc(ones_ready, 1)
                    turn_x(ph, 0, (G_BASE[ph] - 12, 0))
                    turn_c(ph, 0, (G_BASE[ph] - 10, 0))
                    copy_context(0)
                    dve.wait_ge(mask_loaded, 16)
                    write_mask(0)
                    normalise_tokens(ph, 1)
                    turn_x(ph, 1, (G_BASE[ph] - 2, 0))
                    score_maxima(ph, 0, 0)
                if ph == L1PH + 1:
                    dve.wait_ge(wa_split, wa_due(ph, 3))
                    for c in (3, 4):
                        low_chunk(ph, c)
                if attends(ph) and opening_uses(ph):
                    prep = PREP_USES[KIND[ph]]
                    project(ph, G_BASE[ph] - prep - 12)
                    turn_x(ph, 1, (G_BASE[ph] - prep, 0))
                    if KIND[ph] == CROSS:
                        turn_c(ph, 1, (G_BASE[ph] - 2, 0))
                    score_maxima(ph, 0, 0)
                    if ph == 0:
                        dve.wait_ge(x_rest_loaded, 16)
                    if ph == L1PH + 1:
                        for n in range(POST_PARTS):
                            post_part(GROUPS - 1, n)
                groups(dve, bodies[KIND[ph]], ph)

        @block.tensor
        def _(pe):
            def three(ps, lh, ll, rh, rl, start, stop):
                pe.matmul(ps, lh, rh, start=start, stop=False)
                pe.matmul(ps, lh, rl, start=False, stop=False)
                return pe.matmul(ps, ll, rh, start=False, stop=stop)

            def bank_free(ph, g, k):
                pe.wait_ge(g_drained[k % 2], halves_before(ph, g) + k // 2)

            def turn_x_batch(ph, g, b, k, free):
                free(k)
                pe.wait_ge(z_ready, 2 * (GROUPS * ph + g) + b + 1)
                for c in range(2):
                    ins = pe.transpose(psG[k % 2][:, c * P:(c + 1) * P], Z[:, b, c * P:(c + 1) * P], ident[:, :])
                ins.then_inc(g_full, 1)

            def turn_c_batch(ph, g, b, k, free):
                if b == 0:
                    pe.wait_ge(context_loaded, 32 * (context_preps_before(ph, g) + 1))
                free(k)
                for c in range(2):
                    ins = pe.transpose(psG[k % 2][:, c * P:(c + 1) * P], cRaw[:, b, c * P:(c + 1) * P], ident[:, :])
                ins.then_inc(g_full, 1)

            def turn_x(ph, g, first, free):
                for b in range(2):
                    turn_x_batch(ph, g, b, first + b, free)

            def turn_c(ph, g, first, free):
                for b in range(2):
                    turn_c_batch(ph, g, b, first + b, free)

            def turn_probabilities(ph, g, i):
                qb = quads_before(ph, g)
                pe.wait_ge(p_ready, qb + i + 1)
                if i >= 1:
                    pe.wait_ge(pt_ready, qb + i)
                for h in range(4):
                    ins = pe.transpose(psT[:, h * P:(h + 1) * P], Pr[:, i % 4, h * P:(h + 1) * P], ident[:, :])
                ins.then_inc(t_full, 1)

            def project(ph, u, k, free, keys):
                context = KIND[ph] == CROSS and keys
                c0 = 2 * keys
                pe.wait_ge(wa_split, wa_due(ph, c0 + 2))
                free(k)
                for f in (2 * u, 2 * u + 1):
                    ps = psG[k % 2][:, (f % 2) * GT:(f % 2 + 1) * GT]
                    for c in range(2):
                        cols = slice((c0 + c) * CH + f * P, (c0 + c) * CH + (f + 1) * P)
                        if context and c == 1:
                            pe.matmul(ps, WAh[:, cols], cTh[:, 1, :], start=False, stop=False)
                            ins = pe.matmul(ps, WAh[:, cols], cTl[:, 1, :], start=False, stop=True)
                        else:
                            h, l = (cTh, cTl) if context else (hTh, hTl)
                            ins = three(ps, WAh[:, cols], WAl[:, cols], h[:, c, :], l[:, c, :], c == 0, c == 1)
                ins.then_inc(g_full, 1)

            def values(ph, b, half, k, free):
                cross = KIND[ph] == CROSS
                ps, tok = psG[k % 2][:, :], slice(b * P, (b + 1) * P)
                pe.wait_ge(wa_split, wa_due(ph, 6))
                free(k)
                h, l = (cTh, cTl) if cross else (hTh, hTl)
                for c in range(2):
                    cols = slice((4 + c) * CH + half * 512, (4 + c) * CH + (half + 1) * 512)
                    if cross and c == 1:
                        pe.matmul(ps, h[:, 1, tok], WAh[:, cols], start=False, stop=False)
                        ins = pe.matmul(ps, l[:, 1, tok], WAh[:, cols], start=False, stop=True)
                    else:
                        ins = three(ps, h[:, c, tok], l[:, c, tok], WAh[:, cols], WAl[:, cols], c == 0, c == 1)
                ins.then_inc(g_full, 1)

            def scores(ph, g, i):
                b, j = i % 2, i // 2
                if i >= 3:
                    pe.wait_ge(exp_done, quads_before(ph, g) + i - 2)
                for p in range(2):
                    f = 2 * j + p
                    ins = pe.matmul(psS[i % 3][:, p * GT:(p + 1) * GT], Q[:, f, b * P:(b + 1) * P],
                                    K[:, f, b, :, :].rearrange("p e n -> p (e n)"), start=True, stop=True)
                ins.then_inc(s_full, 1)

            def attention(ph, g, left):
                proj, nxt = projected(ph, g, left), prepared(ph, g, left)
                hb, qb, ob = halves_before(ph, g), quads_before(ph, g), o_before(ph, g)
                p0 = 12 if proj else 0

                def free(k):
                    bank_free(ph, g, k)

                def weigh(i):
                    b, j = i % 2, i // 2
                    pe.wait_ge(pt_ready, qb + i + 1)
                    if b == 0 and j < 2:
                        pe.wait_ge(g_drained[j], hb)
                        pe.wait_ge(g_drained[1 - j], hb)
                    if b == 0 and j >= 2:
                        pe.wait_ge(o_drained, ob + j - 1)
                    for h in range(4):
                        e, at = h % 2, b * GT + (h // 2) * P
                        ins = pe.matmul(psO[j % 2][e * HD:(e + 1) * HD, at:at + P],
                                        V[:, b, (4 * j + h) * HD:(4 * j + h + 1) * HD], PT[:, i % 2, h * P:(h + 1) * P],
                                        start=True, stop=True)
                    ins.then_inc(pv_done, 1)

                def merge(b):
                    pe.wait_ge(wb_split, wb_due(ph, B_CHUNKS[ph]))
                    pe.wait_ge(o_drained, ob + 4)
                    for f in range(PAIRS):
                        o = slice(b * CH + f * P, b * CH + (f + 1) * P)
                        w = slice(f * D, (f + 1) * D)
                        ins = three(psO[b][:, 0:D], Oh[:, o], Ol[:, o], WBh[:, w], WBl[:, w], f == 0, f == PAIRS - 1)
                    ins.then_inc(g_full, 1)

                scores(ph, g, 1)
                if proj:
                    if opens(g) and opening_uses(ph):
                        pe.wait_ge(g_drained[1], hb)
                    project(proj[0], 0, 0, free, False)
                for i in range(8):
                    if i + 2 < 8:
                        scores(ph, g, i + 2)
                    if proj and i < 7:
                        project(proj[0], (i + 1) // 2, i + 1, free, i % 2 == 0)
                    if proj and i == 6:
                        values(proj[0], 0, 0, 8, free)
                    if proj and i == 7:
                        values(proj[0], 1, 0, 9, free)
                    turn_probabilities(ph, g, i)
                    if i >= 1:
                        weigh(i - 1)
                if proj:
                    values(proj[0], 0, 1, 10, free)
                weigh(7)
                if proj:
                    values(proj[0], 1, 1, 11, free)
                for n, use in enumerate(tail_order(nxt)):
                    if use[0] == "M":
                        merge(int(use[1]))
                    else:
                        turn = turn_x_batch if use[0] == "X" else turn_c_batch
                        turn(*nxt, int(use[1]), p0 + n, free)
                    if n == 2 and proj:
                        scores(*proj, 0)

            def mlp(ph, g, left):
                nxt, hb = prepared(ph, g, left), halves_before(ph, g)

                def free(k):
                    bank_free(ph, g, k)

                for k in (0, 1):
                    pe.wait_ge(g_drained[k], hb - 1)
                pe.wait_ge(wa_split, wa_due(ph, 4))
                for m in range(8):
                    if m >= 4:
                        pe.wait_ge(hidden_done, gh_due(ph, g, m - 3))
                    for part in range(2):
                        for c in range(2):
                            at = (2 * c + part) * CH + m * P
                            ins = three(hidden_ps[m % 4][:, part * GT:(part + 1) * GT], WAh[:, at:at + P], WAl[:, at:at + P],
                                        hTh[:, c, :], hTl[:, c, :], c == 0, c == 1)
                    ins.then_inc(hidden_full, 1)
                if nxt:
                    turn_x(*nxt, 0, free)
                pe.wait_ge(wb_split, wb_due(ph, B_CHUNKS[ph]))
                for b in range(2):
                    pe.wait_ge(g_drained[b], hb)
                    for m in range(8):
                        if b == 0:
                            pe.wait_ge(gl_done, gh_due(ph, g, m + 1))
                        o, w = slice(m * GT + b * P, m * GT + (b + 1) * P), slice(m * D, (m + 1) * D)
                        ins = three(psO[b][:, 0:D], Oh[:, o], Ol[:, o], WBh[:, w], WBl[:, w], m == 0, m == 7)
                    ins.then_inc(g_full, 1)

            def context_scores(g, i):
                b, j = i // 2, i % 2
                tok = slice(b * P, (b + 1) * P)
                ps = psS[i % 3]
                if i == 0:
                    pe.wait_ge(mask_ready, g + 1)
                if i == 3:
                    pe.wait_ge(exp_done, quads_before(L1PH, g) + 1)
                pe.matmul(ps[:, :].rearrange("p (h n) -> p h n", h=4), ones_row[:, :],
                          mask_added[:, tok].unsqueeze(1).to_broadcast([1, 4, P]),
                          start=True, stop=False, skip_group_check=True)
                for p in range(2):
                    pe.matmul(ps[:, p * GT:(p + 1) * GT], TT[:, H1 + 2 * j + p, tok],
                              cB[:, b, :, :].rearrange("p e n -> p (e n)"), start=False, stop=False, skip_group_check=True)
                    for e in range(2):
                        h = 2 * p + e
                        ins = pe.matmul(ps[:, h * P:(h + 1) * P], TT[:, 4 * j + h, tok], cA[:, tok],
                                        start=False, stop=True, skip_group_check=True)
                ins.then_inc(s_full, 1)

            def reassociated(ph, g, left):
                nxt, hb = prepared(ph, g, left), halves_before(ph, g)
                qb, ob = quads_before(ph, g), o_before(ph, g)
                at = l1_order(left).index

                def free(k):
                    bank_free(ph, g, k)

                def weigh(i):
                    b = i // 2
                    pe.wait_ge(pt_ready, qb + i + 1)
                    if i == 0:
                        pe.wait_ge(cu_copied, g + 1)
                    else:
                        pe.wait_ge(o_drained, ob + i)
                    pe.matmul(psO[0][:, :], cU[:, b, 0:P], PT[:, i % 2, :], start=True, stop=True).then_inc(u_full, 1)
                    pairs = PT[:, i % 2, :].rearrange("p (f e n) -> p f e n", f=2, e=2)
                    for e in range(2):
                        ins = pe.matmul(psO[1][e * DB:(e + 1) * DB, 0:GT], cU[:, b, P:DC], pairs[:, :, e, :],
                                        start=True, stop=True)
                    ins.then_inc(pv_done, 1)

                def merge(b):
                    k = at(f"M{b}")
                    free(k)
                    pe.wait_ge(o_drained, ob + 2 * b + 2)
                    for n in range(H1 + H1 // 2):
                        o, w = slice(n * P, (n + 1) * P), slice(2 * NA + n * D, 2 * NA + (n + 1) * D)
                        ins = three(psG[k % 2][:, 0:D], U_hi[b][:, o], U_lo[b][:, o], WAh[:, w], WAl[:, w], n == 0, n == 11)
                    ins.then_inc(g_full, 1)

                def next_tiles(u):
                    if left:
                        stream_by_a(u, at(f"T{u}"), free)

                if left:
                    pe.wait_ge(g_drained[1], hb - 1)
                else:
                    for k in (0, 1):
                        pe.wait_ge(g_drained[k], hb)
                for i in range(1, 4):
                    context_scores(g, i)
                turn_probabilities(ph, g, 0)
                if left:
                    pe.wait_ge(g_drained[1], hb)
                next_tiles(0)
                weigh(0)
                turn_probabilities(ph, g, 1)
                next_tiles(1)
                weigh(1)
                turn_probabilities(ph, g, 2)
                next_tiles(2)
                weigh(2)
                turn_probabilities(ph, g, 3)
                merge(0)
                next_tiles(3)
                weigh(3)
                if left:
                    turn_c_batch(ph, g + 1, 0, at("C0"), free)
                else:
                    turn_x(*nxt, at("X0"), free)
                next_tiles(4)
                merge(1)
                if left:
                    turn_c_batch(ph, g + 1, 1, at("C1"), free)
                else:
                    turn_c(*nxt, at("C0"), free)
                next_tiles(5)
                if left:
                    context_scores(g + 1, 0)
                if left >= 2:
                    turn_x(*nxt, at("X0"), free)

            def stream_by_a(u, k, free):
                free(k)
                for m in (2 * u, 2 * u + 1):
                    for c in range(2):
                        at = c * NA + m * P
                        ins = three(psG[k % 2][:, (m % 2) * GT:(m % 2 + 1) * GT], WAh[:, at:at + P], WAl[:, at:at + P],
                                    hTh[:, c, :], hTl[:, c, :], c == 0, c == 1)
                ins.then_inc(g_full, 1)

            def products_of_weights():
                def turn(n):
                    h, s = n % H1, n % 2
                    if 2 <= n < H1:
                        pe.wait_ge(pre_q, n - 1)
                    if n >= 2:
                        pe.wait_ge(pre_k, n - 1)
                    if n == H1:
                        pe.wait_ge(big_loaded, 48)
                    for d in range(2):
                        at = h * D1 + d * P
                        if n < H1:
                            for c in range(2):
                                pe.transpose(psS[s][:, d * D + c * P:d * D + (c + 1) * P], raw_q1[:, c, at:at + P], ident[:, :])
                        w = raw_k1 if n < H1 else raw_v1
                        pe.transpose(psO[s][:, d * DC:d * DC + P], w[:, 0, at:at + P], ident[:, :])
                        ins = pe.transpose(psO[s][:, d * DC + P:(d + 1) * DC], w[0:DB, 1, at:at + P], ident[0:DB, 0:DB])
                    ins.then_inc(pre_turned, 1)

                def product(n):
                    h, s, e = n % H1, n % 2, n % 2
                    q, w = Pr[:, 2 * s, :], Pr[:, 2 * s + 1, :]
                    if n < H1:
                        pe.wait_ge(pre_q, n + 1)
                    pe.wait_ge(pre_k, n + 1)
                    if n >= 2:
                        pe.wait_ge(pre_lo, n - 1)
                    if n < H1:
                        for c in range(2):
                            for d in range(2):
                                ins = pe.matmul(psG[s][:, c * DC:(c + 1) * DC], q[:, d * D + c * P:d * D + (c + 1) * P],
                                                w[:, d * DC:(d + 1) * DC], start=d == 0, stop=d == 1)
                    else:
                        for d in range(2):
                            pe.matmul(psG[s][:, 0:D], w[:, d * DC:d * DC + P], raw_o1[:, 2 * h + d, :],
                                      start=d == 0, stop=d == 1)
                        for d in range(2):
                            ins = pe.matmul(psG[s][e * DB:(e + 1) * DB, D:2 * D], w[:, d * DC + P:(d + 1) * DC],
                                            raw_o1[:, 2 * h + d, :], start=d == 0, stop=d == 1)
                    ins.then_inc(pre_full, 1)

                pe.wait_ge(raw_loaded, raw_due(L1PH))
                turn(0)
                for n in range(2 * H1):
                    if n + 1 < 2 * H1:
                        turn(n + 1)
                    product(n)

            bodies = {SELF: attention, CROSS: attention, FF: mlp, L1: reassociated}
            pe.wait_ge(ident_ready, 2)
            turn_x(0, 0, 0, lambda k: None)
            for ph in range(len(KIND)):
                if KIND[ph] == L1:
                    first = (G_BASE[ph] - opening_uses(ph)) // 2
                    for k in (0, 1):
                        pe.wait_ge(g_drained[k], first)
                    products_of_weights()
                    pe.wait_ge(pre_lo, 2 * H1)
                    turn_x(ph, 0, 0, lambda k: None)

                    def free(k):
                        pe.wait_ge(g_drained[k % 2], first + k // 2)

                    turn_c(ph, 0, 2, free)
                    free(3)
                    for u in range(6):
                        stream_by_a(u, 4 + u, free)
                    turn_x(ph, 1, 10, free)
                    pe.wait_ge(cb_zeroed, 2)
                    pe.wait_ge(ones_ready, 1)
                    context_scores(0, 0)
                if ph in (0, L1PH + 1):
                    pe.wait_ge(k_zeroed, 1 if ph == 0 else 2)
                if attends(ph) and opening_uses(ph):
                    first = (G_BASE[ph] - PREP_USES[KIND[ph]] - 12) // 2

                    def free(k):
                        pe.wait_ge(g_drained[k % 2], first + k // 2)

                    if ph == 0:
                        free(1)
                    for k in range(8):
                        project(ph, k % 4, k, free, k >= 4)
                    for k in range(8, 12):
                        values(ph, k % 2, (k - 8) // 2, k, free)
                    turn_x(ph, 1, 12, free)
                    if KIND[ph] == CROSS:
                        turn_c(ph, 1, 14, free)
                    scores(ph, 0, 0)
                groups(pe, bodies[KIND[ph]], ph)


def kernel(**inputs):
    import numpy as np
    import concourse.bacc as bacc
    from concourse.bass_utils import run_bass_kernel_spmd

    laid_out = {name: inputs[name] for name in ["x", "ctx_768", "mask_BxS2_if1"] + [n for ws in WEIGHTS for n in ws]}
    pairs = [pair or ("L1_xattn_gamma", "L1_xattn_beta") for pair in NORMS]
    laid_out["norm_columns"] = np.stack([[inputs[n] for n in pair] for pair in pairs]).reshape(
        len(NORMS), 2, 2, P).transpose(3, 0, 1, 2)
    laid_out["hidden_bias_columns"] = np.stack([inputs[n] for n in HIDDEN_BIAS.values()]).reshape(
        2, 16, P).transpose(2, 0, 1)
    rows = BIASES[:L1PH] + ["L1_xattn_gamma"] + BIASES[L1PH + 1:] + ["L1_xattn_beta"]
    laid_out["bias_rows"] = np.stack([inputs[n] for n in rows])

    nc = bacc.Bacc("TRN2", target_bir_lowering=False, num_devices=1)
    arrays, tensors = {}, {}
    for name, a in laid_out.items():
        arrays[f"in_{name}"] = a = np.ascontiguousarray(a)
        tensors[name] = nc.dram_tensor(f"in_{name}", a.shape, mybir.dt.from_np(a.dtype), kind="ExternalInput").ap()
    out = nc.dram_tensor("out_x", (B, P, D), F32, kind="ExternalOutput").ap()
    build(nc, tensors, out)
    result = run_bass_kernel_spmd(nc, [arrays], core_ids=[0])
    return result.results[0]["out_x"]
```
